# Optimizing a Trainium2 kernel written in Bass

```python
import numpy as np
import jax
import jax.numpy as jnp

def _softmax(x, axis=-1):
    return jax.nn.softmax(x, axis=axis)

def _gelu(x):
    return jax.nn.gelu(x, approximate=True)

def _silu(x):
    return jax.nn.silu(x)

def _sigmoid(x):
    return jax.nn.sigmoid(x)

def _layernorm(x, axis=-1, eps=1e-05):
    m = jnp.mean(x, axis=axis, keepdims=True)
    v = jnp.var(x, axis=axis, keepdims=True)
    return (x - m) / jnp.sqrt(v + eps)

def _scatter_add(tgt, idx, src, axis=0):
    return tgt.at[idx].add(src)

def _segment_sum(src, seg, n):
    return jax.ops.segment_sum(src, seg, n)
kernel_name = 'mk_vit_tower_d1_tok_img256_r4_1967c8'

def setup_inputs(seed: int=0):
    np.random.seed(seed)
    _w = jnp.asarray

    def _rec_inputs():
        import jax
        import jax.numpy as jnp
        _rk = jax.random.key(seed)
        x = -0.000596345 + 1.00056 * jax.random.normal(jax.random.fold_in(_rk, 1), (32, 64, 64, 3), jnp.float32)
        return x
    x = _rec_inputs()

    def _L0_tok_setup():
        import jax, jax.numpy as jnp
        import numpy as np
        M1, M2, WIDTH, LAYERS = (16, 16, 64, 4)
        B, H, W = (16, 64, 64)
        EPS = 1e-05

        def _spectral_conv(h, w1, w2):
            xf = jnp.fft.rfft2(h)
            top = jnp.einsum('bixy,ioxy->boxy', xf[:, :, :M1, :M2], w1)
            bot = jnp.einsum('bixy,ioxy->boxy', xf[:, :, -M1:, :M2], w2)
            of = jnp.zeros(xf.shape, dtype=xf.dtype)
            of = of.at[:, :, :M1, :M2].set(top)
            of = of.at[:, :, -M1:, :M2].set(bot)
            return jnp.fft.irfft2(of, s=(h.shape[-2], h.shape[-1]))
        key = jax.random.key(seed)
        ks = jax.random.split(key, 16)
        scale = 1.0 / (WIDTH * WIDTH)
        inp = {'x': jax.random.normal(ks[0], (B, H, W, 3), dtype=jnp.float32), 'fc0_w': jax.random.normal(ks[1], (3, WIDTH), dtype=jnp.float32) * 0.3, 'fc0_b': jnp.zeros((WIDTH,), jnp.float32), 'w1r': jax.random.normal(ks[2], (LAYERS, WIDTH, WIDTH, M1, M2), dtype=jnp.float32) * scale, 'w1i': jax.random.normal(ks[3], (LAYERS, WIDTH, WIDTH, M1, M2), dtype=jnp.float32) * scale, 'w2r': jax.random.normal(ks[4], (LAYERS, WIDTH, WIDTH, M1, M2), dtype=jnp.float32) * scale, 'w2i': jax.random.normal(ks[5], (LAYERS, WIDTH, WIDTH, M1, M2), dtype=jnp.float32) * scale, 'pw_w': jax.random.normal(ks[6], (LAYERS, WIDTH, WIDTH), dtype=jnp.float32) * (1.0 / np.sqrt(WIDTH)), 'pw_b': jnp.zeros((LAYERS, WIDTH), jnp.float32), 'gamma': jnp.ones((LAYERS, WIDTH), jnp.float32), 'beta': jnp.zeros((LAYERS, WIDTH), jnp.float32), 'fc1_w': jax.random.normal(ks[7], (WIDTH, 128), dtype=jnp.float32) * (1.0 / np.sqrt(WIDTH)), 'fc1_b': jnp.zeros((128,), jnp.float32), 'fc2_w': jax.random.normal(ks[8], (128, 1), dtype=jnp.float32) * (1.0 / np.sqrt(128.0)), 'fc2_b': jnp.zeros((1,), jnp.float32)}
        return inp
    _L0_tok_all = _L0_tok_setup()
    _L0_tok_in = {k: v for k, v in _L0_tok_all.items() if k in ('fc0_w', 'fc0_b', 'w1r', 'w1i', 'w2r', 'w2i', 'pw_w', 'pw_b', 'gamma', 'beta', 'fc1_w', 'fc1_b', 'fc2_w', 'fc2_b')}
    del _L0_tok_all

    def _L0_attn_setup():
        import jax, jax.numpy as jnp
        import numpy as np
        MIDC = 64
        HEADS = 16
        HEADC = MIDC // HEADS
        EPS = 1e-05

        def _layernorm(x, w, b):
            mean = jnp.mean(x, axis=-1, keepdims=True)
            std = jnp.std(x, axis=-1, keepdims=True, ddof=1)
            return w * (x - mean) / (std + EPS) + b
        key = jax.random.key(seed)
        ks = jax.random.split(key, 3)
        B, HW = (8, 4096)
        x = jax.random.normal(ks[0], (B, HW, MIDC), dtype=jnp.float32)
        W_qkv = jax.random.normal(ks[1], (3 * MIDC, MIDC), dtype=jnp.float32) * 0.02
        b_qkv = jnp.zeros((3 * MIDC,), dtype=jnp.float32)
        kln_w = jnp.ones((HEADS, 1, HEADC), dtype=jnp.float32)
        kln_b = jnp.zeros((HEADS, 1, HEADC), dtype=jnp.float32)
        vln_w = jnp.ones((HEADS, 1, HEADC), dtype=jnp.float32)
        vln_b = jnp.zeros((HEADS, 1, HEADC), dtype=jnp.float32)
        W_proj = jax.random.normal(ks[2], (MIDC, MIDC), dtype=jnp.float32) * 0.02
        b_proj = jnp.zeros((MIDC,), dtype=jnp.float32)
        return {'x': x, 'W_qkv': W_qkv, 'b_qkv': b_qkv, 'kln_w': kln_w, 'kln_b': kln_b, 'vln_w': vln_w, 'vln_b': vln_b, 'W_proj': W_proj, 'b_proj': b_proj}
    _L0_attn_all = _L0_attn_setup()
    _L0_attn_in = {k: v for k, v in _L0_attn_all.items() if k in ('W_qkv', 'b_qkv', 'kln_w', 'kln_b', 'vln_w', 'vln_b', 'W_proj', 'b_proj')}
    del _L0_attn_all

    def _L0_ffn_setup():
        import jax, jax.numpy as jnp
        import numpy as np
        B, S, H, NH, NE = (4, 256, 64, 4, 4)
        D = H // NH
        EPS = 1e-08

        def layernorm(x, g, b):
            m = jnp.mean(x, axis=-1, keepdims=True)
            v = jnp.mean((x - m) ** 2, axis=-1, keepdims=True)
            return (x - m) / jnp.sqrt(v + EPS) * g + b
        key = jax.random.key(seed)
        ks = jax.random.split(key, 18)
        sc = 0.05
        return {'x': jax.random.normal(ks[0], (B, S, H), jnp.float32), 'hl_w': jax.random.normal(ks[1], (NH, D, H), jnp.float32) * sc, 'hl_b': jax.random.normal(ks[2], (NH, D), jnp.float32) * sc, 'wq': jax.random.normal(ks[3], (NH, NE, D, D), jnp.float32) * sc, 'wk': jax.random.normal(ks[4], (NH, D, D), jnp.float32) * sc, 'wv': jax.random.normal(ks[5], (NH, D, D), jnp.float32) * sc, 'gate_w': jax.random.normal(ks[6], (NH, NE, NE * D), jnp.float32) * sc, 'gate_b': jax.random.normal(ks[7], (NH, NE), jnp.float32) * sc, 'ln_g': jnp.ones((D,), jnp.float32), 'ln_b': jnp.zeros((D,), jnp.float32), 'fc1_w': jax.random.normal(ks[8], (D, D), jnp.float32) * sc, 'fc1_b': jax.random.normal(ks[9], (D,), jnp.float32) * sc, 'fc2_w': jax.random.normal(ks[10], (D, D), jnp.float32) * sc, 'fc2_b': jax.random.normal(ks[11], (D,), jnp.float32) * sc, 'fnorm_g': jnp.ones((D,), jnp.float32), 'fnorm_b': jnp.zeros((D,), jnp.float32), 'fgate_w': jax.random.normal(ks[12], (NH, H), jnp.float32) * sc}
    _L0_ffn_all = _L0_ffn_setup()
    _L0_ffn_in = {k: v for k, v in _L0_ffn_all.items() if k in ('hl_w', 'hl_b', 'wq', 'wk', 'wv', 'gate_w', 'gate_b', 'ln_g', 'ln_b', 'fc1_w', 'fc1_b', 'fc2_w', 'fc2_b', 'fnorm_g', 'fnorm_b', 'fgate_w')}
    del _L0_ffn_all
    return {'x': x, 'L0_tok_fc0_w': _L0_tok_in['fc0_w'], 'L0_tok_fc0_b': _L0_tok_in['fc0_b'], 'L0_tok_w1r': _L0_tok_in['w1r'], 'L0_tok_w1i': _L0_tok_in['w1i'], 'L0_tok_w2r': _L0_tok_in['w2r'], 'L0_tok_w2i': _L0_tok_in['w2i'], 'L0_tok_pw_w': _L0_tok_in['pw_w'], 'L0_tok_pw_b': _L0_tok_in['pw_b'], 'L0_tok_gamma': _L0_tok_in['gamma'], 'L0_tok_beta': _L0_tok_in['beta'], 'L0_tok_fc1_w': _L0_tok_in['fc1_w'], 'L0_tok_fc1_b': _L0_tok_in['fc1_b'], 'L0_tok_fc2_w': _L0_tok_in['fc2_w'], 'L0_tok_fc2_b': _L0_tok_in['fc2_b'], 'L0_attn_W_qkv': _L0_attn_in['W_qkv'], 'L0_attn_b_qkv': _L0_attn_in['b_qkv'], 'L0_attn_kln_w': _L0_attn_in['kln_w'], 'L0_attn_kln_b': _L0_attn_in['kln_b'], 'L0_attn_vln_w': _L0_attn_in['vln_w'], 'L0_attn_vln_b': _L0_attn_in['vln_b'], 'L0_attn_W_proj': _L0_attn_in['W_proj'], 'L0_attn_b_proj': _L0_attn_in['b_proj'], 'L0_ffn_hl_w': _L0_ffn_in['hl_w'], 'L0_ffn_hl_b': _L0_ffn_in['hl_b'], 'L0_ffn_wq': _L0_ffn_in['wq'], 'L0_ffn_wk': _L0_ffn_in['wk'], 'L0_ffn_wv': _L0_ffn_in['wv'], 'L0_ffn_gate_w': _L0_ffn_in['gate_w'], 'L0_ffn_gate_b': _L0_ffn_in['gate_b'], 'L0_ffn_ln_g': _L0_ffn_in['ln_g'], 'L0_ffn_ln_b': _L0_ffn_in['ln_b'], 'L0_ffn_fc1_w': _L0_ffn_in['fc1_w'], 'L0_ffn_fc1_b': _L0_ffn_in['fc1_b'], 'L0_ffn_fc2_w': _L0_ffn_in['fc2_w'], 'L0_ffn_fc2_b': _L0_ffn_in['fc2_b'], 'L0_ffn_fnorm_g': _L0_ffn_in['fnorm_g'], 'L0_ffn_fnorm_b': _L0_ffn_in['fnorm_b'], 'L0_ffn_fgate_w': _L0_ffn_in['fgate_w']}

def reference(x, L0_tok_fc0_w, L0_tok_fc0_b, L0_tok_w1r, L0_tok_w1i, L0_tok_w2r, L0_tok_w2i, L0_tok_pw_w, L0_tok_pw_b, L0_tok_gamma, L0_tok_beta, L0_tok_fc1_w, L0_tok_fc1_b, L0_tok_fc2_w, L0_tok_fc2_b, L0_attn_W_qkv, L0_attn_b_qkv, L0_attn_kln_w, L0_attn_kln_b, L0_attn_vln_w, L0_attn_vln_b, L0_attn_W_proj, L0_attn_b_proj, L0_ffn_hl_w, L0_ffn_hl_b, L0_ffn_wq, L0_ffn_wk, L0_ffn_wv, L0_ffn_gate_w, L0_ffn_gate_b, L0_ffn_ln_g, L0_ffn_ln_b, L0_ffn_fc1_w, L0_ffn_fc1_b, L0_ffn_fc2_w, L0_ffn_fc2_b, L0_ffn_fnorm_g, L0_ffn_fnorm_b, L0_ffn_fgate_w):
    import jax
    import jax.numpy as jnp

    def _L0_tok_ref(x, fc0_w, fc0_b, w1r, w1i, w2r, w2i, pw_w, pw_b, gamma, beta, fc1_w, fc1_b, fc2_w, fc2_b):
        import jax, jax.numpy as jnp
        import numpy as np
        M1, M2, WIDTH, LAYERS = (16, 16, 64, 4)
        B, H, W = (16, 64, 64)
        EPS = 1e-05

        def _spectral_conv(h, w1, w2):
            xf = jnp.fft.rfft2(h)
            top = jnp.einsum('bixy,ioxy->boxy', xf[:, :, :M1, :M2], w1)
            bot = jnp.einsum('bixy,ioxy->boxy', xf[:, :, -M1:, :M2], w2)
            of = jnp.zeros(xf.shape, dtype=xf.dtype)
            of = of.at[:, :, :M1, :M2].set(top)
            of = of.at[:, :, -M1:, :M2].set(bot)
            return jnp.fft.irfft2(of, s=(h.shape[-2], h.shape[-1]))
        h = jnp.einsum('bhwi,ic->bhwc', x, fc0_w) + fc0_b
        h = h.transpose(0, 3, 1, 2)
        for l in range(LAYERS):
            sc = _spectral_conv(h, w1r[l] + 1j * w1i[l], w2r[l] + 1j * w2i[l])
            pw = jnp.einsum('bihw,oi->bohw', h, pw_w[l]) + pw_b[l][None, :, None, None]
            y = sc + pw
            mean = y.mean(axis=(0, 2, 3), keepdims=True)
            var = y.var(axis=(0, 2, 3), keepdims=True)
            y = (y - mean) * jax.lax.rsqrt(var + EPS)
            y = y * gamma[l][None, :, None, None] + beta[l][None, :, None, None]
            h = jax.nn.gelu(y, approximate=False)
        h = h.transpose(0, 2, 3, 1)
        h = jax.nn.gelu(h @ fc1_w + fc1_b, approximate=False)
        out = (h @ fc2_w + fc2_b).squeeze(-1)
        return out

    def _L0_attn_ref(x, W_qkv, b_qkv, kln_w, kln_b, vln_w, vln_b, W_proj, b_proj):
        import jax, jax.numpy as jnp
        import numpy as np
        MIDC = 64
        HEADS = 16
        HEADC = MIDC // HEADS
        EPS = 1e-05

        def _layernorm(x, w, b):
            mean = jnp.mean(x, axis=-1, keepdims=True)
            std = jnp.std(x, axis=-1, keepdims=True, ddof=1)
            return w * (x - mean) / (std + EPS) + b
        B, HW, C = x.shape
        bias = x
        qkv = jnp.einsum('bnc,oc->bno', x, W_qkv) + b_qkv
        qkv = qkv.reshape(B, HW, HEADS, 3 * HEADC).transpose(0, 2, 1, 3)
        q, k, v = jnp.split(qkv, 3, axis=-1)
        k = _layernorm(k, kln_w, kln_b)
        v = _layernorm(v, vln_w, vln_b)
        kv = jnp.einsum('bhnd,bhne->bhde', k, v) / HW
        out = jnp.einsum('bhnd,bhde->bhne', q, kv)
        out = out.transpose(0, 2, 1, 3).reshape(B, HW, C)
        ret = out + bias
        proj = jnp.einsum('bnc,oc->bno', ret, W_proj) + b_proj
        return jax.nn.gelu(proj, approximate=False) + bias

    def _L0_ffn_ref(x, hl_w, hl_b, wq, wk, wv, gate_w, gate_b, ln_g, ln_b, fc1_w, fc1_b, fc2_w, fc2_b, fnorm_g, fnorm_b, fgate_w):
        import jax, jax.numpy as jnp
        import numpy as np
        B, S, H, NH, NE = (4, 256, 64, 4, 4)
        D = H // NH
        EPS = 1e-08

        def layernorm(x, g, b):
            m = jnp.mean(x, axis=-1, keepdims=True)
            v = jnp.mean((x - m) ** 2, axis=-1, keepdims=True)
            return (x - m) / jnp.sqrt(v + EPS) * g + b
        b, s, h = x.shape
        nh, d, _ = wk.shape
        ne = wq.shape[1]
        sx = jnp.einsum('bsh,ndh->bnsd', x, hl_w) + hl_b[None, :, None, :]
        pad = sx == 0
        q = jnp.einsum('bnsd,neod->bneso', sx, wq)
        k = jnp.einsum('bnsd,nod->bnso', sx, wk)
        v = jnp.einsum('bnsd,nod->bnso', sx, wv)
        causal = jnp.where(jnp.tril(jnp.ones((s, s), bool)), 0.0, -jnp.inf).astype(x.dtype)
        scores = jnp.einsum('bnesd,bntd->bnest', q, k) * d ** 0.5 + causal
        att = jax.nn.softmax(scores, axis=-1)
        qkv = jnp.einsum('bnest,bntd->bnesd', att, v)
        qkv = jnp.where(pad[:, :, None], 0.0, qkv)
        out = jnp.transpose(qkv, (0, 1, 3, 2, 4)).reshape(b, nh, s, ne * d)
        gs = jax.nn.softmax(jnp.einsum('bnsf,nef->bnse', out, gate_w) + gate_b[None, :, None, :], axis=-1)
        mixed = jnp.einsum('bnsed,bnse->bnsd', out.reshape(b, nh, s, ne, d), gs)
        resid = sx[jnp.arange(nh), jnp.arange(nh)]
        hn = layernorm(mixed + resid, ln_g, ln_b)
        f_n = jnp.transpose(hn, (0, 2, 1, 3)).reshape(b, s, h)
        fx = f_n.reshape(b, s, nh, d)
        pm = fx == 0
        hx = jnp.where(pm, 0.0, fx @ fc1_w.T + fc1_b)
        hx = jax.nn.relu(hx)
        hx = jnp.where(pm, 0.0, hx @ fc2_w.T + fc2_b)
        hx = layernorm(hx + fx, fnorm_g, fnorm_b)
        fout = hx.reshape(b, s, h)
        fg = jax.nn.softmax(fout @ fgate_w.T, axis=-1)
        return (fout.reshape(b, s, nh, d) * fg[..., None]).reshape(b, s, h)
    h = _L0_tok_ref(x, L0_tok_fc0_w, L0_tok_fc0_b, L0_tok_w1r, L0_tok_w1i, L0_tok_w2r, L0_tok_w2i, L0_tok_pw_w, L0_tok_pw_b, L0_tok_gamma, L0_tok_beta, L0_tok_fc1_w, L0_tok_fc1_b, L0_tok_fc2_w, L0_tok_fc2_b)
    h = h + _L0_attn_ref(_layernorm(h, axis=-1), L0_attn_W_qkv, L0_attn_b_qkv, L0_attn_kln_w, L0_attn_kln_b, L0_attn_vln_w, L0_attn_vln_b, L0_attn_W_proj, L0_attn_b_proj)
    h = h + _L0_ffn_ref(_layernorm(h, axis=-1), L0_ffn_hl_w, L0_ffn_hl_b, L0_ffn_wq, L0_ffn_wk, L0_ffn_wv, L0_ffn_gate_w, L0_ffn_gate_b, L0_ffn_ln_g, L0_ffn_ln_b, L0_ffn_fc1_w, L0_ffn_fc1_b, L0_ffn_fc2_w, L0_ffn_fc2_b, L0_ffn_fnorm_g, L0_ffn_fnorm_b, L0_ffn_fgate_w)
    return h

_drawn_inputs = setup_inputs


def setup_inputs(seed=0):
    import zlib

    import numpy as np

    out = dict(_drawn_inputs(seed))
    spreads = {'L0_tok_fc0_b': (0.0, 2.0),
     'L0_tok_pw_b': (0.0, 2.0),
     'L0_tok_gamma': (1.0, 0.2),
     'L0_tok_beta': (0.0, 0.1),
     'L0_tok_fc1_b': (0.0, 0.1),
     'L0_attn_b_qkv': (0.0, 0.8),
     'L0_attn_kln_w': (1.0, 0.6),
     'L0_attn_kln_b': (0.0, 0.8),
     'L0_attn_vln_w': (1.0, 0.6),
     'L0_attn_vln_b': (0.0, 0.8),
     'L0_attn_b_proj': (0.0, 0.1),
     'L0_ffn_ln_g': (1.0, 0.592),
     'L0_ffn_ln_b': (0.0, 0.474),
     'L0_ffn_fnorm_g': (1.0, 0.2),
     'L0_ffn_fnorm_b': (0.0, 0.462)}
    factors = {'L0_tok_w1r': 23.299,
     'L0_tok_w1i': 23.443,
     'L0_tok_w2r': 23.482,
     'L0_tok_w2i': 23.278,
     'L0_attn_W_qkv': 8.0,
     'L0_ffn_wq': 8.0,
     'L0_ffn_wk': 8.0,
     'L0_ffn_wv': 4.364,
     'L0_ffn_gate_w': 8.0,
     'L0_ffn_gate_b': 25.593,
     'L0_ffn_fc1_w': 8.0,
     'L0_ffn_fc1_b': 8.0,
     'L0_ffn_fc2_w': 8.0,
     'L0_ffn_fc2_b': 4.4}
    for name, (base, spread) in spreads.items():
        noise = np.random.default_rng([zlib.crc32(name.encode()), seed]).standard_normal(out[name].shape)
        drawn = base * np.exp(spread * noise) if base else spread * noise
        out[name] = jnp.asarray(drawn.astype(out[name].dtype))
    for name, factor in factors.items():
        out[name] = (out[name] * factor).astype(out[name].dtype)
    return out
```

```python
from contextlib import ExitStack

import concourse.bass as bass
from concourse import mybir

F32 = mybir.dt.float32
ALU = mybir.AluOpType
ACT = mybir.ActivationFunctionType
AX = mybir.AxisListType

P = 128
BATCH, SIDE, CH = 32, 64, 64
PAIRS = BATCH // 2
PIX = SIDE * SIDE
LAYERS = 4
NKX, NKY = 32, 16
CHUNKS = 4
CM = NKX * NKY // CHUNKS
BANK = 512
BN_EPS = 1e-5
HID = 128


TAIL_W = {"wkv": [65, P], "wq2": [65, P], "wproj": [65, CH], "hlp": [65, P], "wqp": [P, 4, P], "wkp": [P, 4, P], "wvp": [P, 2, 32],
          "gwb": [P, 2, 16], "gateb": [P, 16], "kvw": [P, P], "kvb": [P, P], "bd": [P, CH], "lng": [P, CH], "lnb": [P, CH],
          "fng": [P, CH], "fnb": [P, CH], "fc1d": [65, CH], "fc2d": [65, CH], "fgt": [CH, 4], "mask": [P, BANK]}


def tower_kernel(nc, io):
    ctx = ExitStack()
    with ctx:
        def sb(name, shape, dt=F32):
            return ctx.enter_context(nc.sbuf_tensor(name, shape, dt))

        def sem(name):
            return ctx.enter_context(nc.semaphore(name))

        def sems(name):
            return [sem(f"{name}{u}") for u in range(2)]

        field = nc.dram_tensor("field", [PAIRS, P, PIX], F32, kind="Internal").ap()
        xmodes = nc.dram_tensor("xmodes", [CHUNKS, 2, BATCH, CH, CM], F32, kind="Internal").ap()
        zmodes = nc.dram_tensor("zmodes", [2, NKX, NKY, BATCH, CH], F32, kind="Internal").ap()

        big = sb("big", [P, 4, PIX])
        ytile = big[:, 0:2, :]
        htile = big[:, 2:4, :]
        xin = big[:, :, :].rearrange("p (u v) (b m) -> p u v b m", u=2, b=BATCH)
        wt = sb("wt", [P, 2, CM, CH])
        work = sb("work", [P, 2 * PIX])
        ht = work[:, 0:PIX].rearrange("p (t c) -> p t c", c=P)
        atile = work[:, PIX:2 * PIX].rearrange("p (u ky rx) -> p u ky rx", u=2, ky=NKY)
        zout = work[:, :].rearrange("p (u m o) -> p u m o", u=2, o=CH)
        gtile = work[:, 0:2048].rearrange("p (x r k) -> p x r k", r=2, k=NKY)
        gt = work[:, PIX:2 * PIX].rearrange("p (u q c) -> p u q c", u=2, c=P)
        att_t = sb("att_t", [P, NKY, P])
        zin_all = sb("zin", [P, 2 * NKY * P])
        zin = zin_all[0:64, :].rearrange("p (u k c) -> p u k c", u=2, k=NKY)
        xout = sb("xout", [P, 2, CHUNKS, 2, CM])
        ident = sb("ident", [P, P])
        fy = sb("fy", [P, 64])
        fx = sb("fx", [P, 64])
        ix = sb("ix", [64, P])
        iy = sb("iy", [P, 256])
        avg = sb("avg", [P, P])
        pw = sb("pw", [P, P])
        vecs = sb("vecs", [P, 3])
        fc0 = sb("fc0", [8, P])
        fc0b = sb("fc0b", [P, 1])
        fc1 = sb("fc1", [P, HID])
        fc1b = sb("fc1b", [P, 1])
        fc2 = sb("fc2", [P, 1])
        fc2b = sb("fc2b", [P, 1])
        stats = sb("stats", [P, PAIRS * 8, 6])
        mv = sb("mv", [P, 2])
        sm = sb("sm", [P, 8])
        bn_scale = sb("bn_scale", [P, 1])
        bn_bias = sb("bn_bias", [P, 1])
        epst = sb("epst", [P, 1])
        tok = sb("tok", [P, 1024])

        free = {"big": 0, "wt": 0}
        pools = {"big": big[:, :, :].rearrange("p a b -> p (a b)"), "wt": wt[:, :, :, :].rearrange("p a b c -> p (a b c)")}

        def view(n, where="big", parts=P):
            at = free[where]
            free[where] += n
            assert free[where] <= 4 * PIX
            return pools[where][0:parts, at:at + n]

        J = PAIRS
        TD = J * CH
        h1t = nc.dram_tensor("h1_rows", [BATCH * SIDE * SIDE], F32, kind="Internal").ap()
        rows = view(TD); h1 = view(TD); xn = view(TD); xc = view(2 * TD); sq = view(2 * TD)
        kv = view(2 * TD); kn = view(TD); vn = view(TD); kvm = view(TD); ret = view(TD); ga = view(TD)
        h2 = view(TD); sx = view(TD)
        xt = view(2048, "wt", 65); qt = view(2048, "wt"); att_out = view(4 * TD, "wt"); att_T = view(4096, "wt")
        s1 = view(512, "wt"); s2 = view(512, "wt"); sd = view(512, "wt")
        prod = sq; mixed = kn; fxt = view(TD, "wt"); hx = ga; fo = view(TD, "wt")
        x2 = xn
        lg = s1[:, 0:256]; gmax = s2[:, 0:64]; gexp = sd[:, 0:256]; gsum = s2[:, 64:128]
        res = sb("res", [P, CH]); keep = tok[:, :]
        keepT = qt[0:64, :]
        sxT = work[:, 0:256].rearrange("p (u t) -> p u t", u=2)
        qb = work[:, 256:1280].rearrange("p (u t) -> p u t", u=2)
        kb = work[:, 1280:2304].rearrange("p (u t) -> p u t", u=2)
        vb = work[:, 2304:2304 + 2 * 136].rearrange("p (u i q h o) -> p u i q h o", u=2, i=2, q=2, h=2)
        ex = work[:, 2576:2576 + 2048].rearrange("p (u i t) -> p u i t", u=2, i=2)
        exT = work[:, 4624:4624 + 1024].rearrange("p (i t) -> p i t", i=2)
        mx = work[:, 5648:5680].rearrange("p (u i g) -> p u i g", u=2, i=2)
        rden = work[:, 5680:5712].rearrange("p (u g) -> p u g", u=2)
        tw = {}
        at = 0
        for name, shape in TAIL_W.items():
            n = shape[1] * (shape[2] if len(shape) == 3 else 1)
            tw[name] = zin_all[0:shape[0], at:at + n]
            if len(shape) == 3:
                tw[name] = tw[name].rearrange("p (a b) -> p a b", a=shape[1])
            at += n
        maskb = sb("maskb", [P, BANK], mybir.dt.bfloat16)
        identb = sb("identb", [P, P], mybir.dt.bfloat16)
        eps5 = sb("eps5", [P, 1])
        eps8 = sb("eps8", [P, 1])
        zero1 = sb("zero1", [P, 1])

        fills = {}
        nth = [0] * 8
        for name, banks in (("rows", (0, 1)), ("xT", (0, 1, 2, 3)), ("q", (4, 5, 6, 7)), ("kv", (0, 1, 2, 3)), ("kvm", (4, 5)),
                            ("out", (6, 7)), ("retT", (0, 1, 2, 3)), ("proj", (4, 5)), ("x2T", (0, 1, 2, 3)),
                            ("attT", (0, 1, 2, 3, 4, 5, 6, 7)), ("gate", (0,)), ("fT", (4, 5, 6, 7)), ("fc1", (0, 1, 2, 3)),
                            ("fc2", (4, 5)), ("foT", (0, 1, 2, 3)), ("fg", (4,))):
            for i, b in enumerate(banks):
                fills[name, i] = (b, nth[b])
                nth[b] += 1

        bank = [ctx.enter_context(nc.psum_tensor(f"bank{i}", [P, BANK], F32)) for i in range(8)]

        phase = sem("phase")
        carrier = sem("carrier")
        cst = sem("cst")
        par = sem("par")
        zero_done = sem("zero_done")
        xld = sems("xld"); pF = sem("pF"); pFe = sem("pFe"); pSt = sems("pSt")
        aYld = sems("aYld"); aG = sem("aG"); aT = sem("aT"); aTe = sem("aTe")
        aY = sem("aY"); aYe = sem("aYe"); aR = sem("aR"); aRe = sem("aRe")
        aX = sem("aX"); aXe = sem("aXe"); aXst = sems("aXst")
        wld = sems("wld"); mXld = sems("mXld"); mNeg = sem("mNeg"); mM = sem("mM")
        mE = sems("mE"); mZst = sems("mZst")
        bYld = sems("bYld"); bZld = sems("bZld"); bG = sem("bG"); bK = sem("bK"); bKe = sem("bKe")
        bT = sem("bT"); bTe = sem("bTe"); bF = sem("bF"); bFe = sem("bFe"); bS = sem("bS")
        bYst = sems("bYst")
        stv = sem("stv"); stp = sem("stp"); sta = sem("sta")
        fYld = sems("fYld"); fG = sem("fG"); fC = sem("fC"); fCe = sem("fCe"); fO = sem("fO"); fOe = sem("fOe")

        full = [sem(f"full{b}") for b in range(8)]
        empty = [sem(f"empty{b}") for b in range(8)]
        twl = sem("twl"); chain = sem("chain"); h1_st = sem("h1_st"); h1_ld = sem("h1_ld"); out_st = sem("out_st")
        clear = sem("clear"); masks = sem("masks")
        ev = {n: sem("ev_" + n) for n in (
            "rows", "xn", "var", "rstd", "xT", "qT", "kn", "kvm", "ret", "retT", "ga", "x2", "x2T", "att", "attT", "lg", "gexp",
            "fx", "fxT", "hx", "fo", "foT", "fl", "fexp", "done")}
        lSX = sem("lSX"); lSXe = sem("lSXe"); lQ = sem("lQ"); lQe = sem("lQe"); lK = sem("lK"); lKe = sem("lKe")
        lV = sem("lV"); lVe = sem("lVe"); lS = sem("lS"); lSe = sem("lSe"); lE = sem("lE"); lT = sem("lT"); lTe = sem("lTe")
        lO = sem("lO"); lOe = sem("lOe"); lMx = sem("lMx"); lRd = sem("lRd")

        def filled(eng, name, i):
            b, n = fills[name, i]
            eng.wait_ge(full[b], n + 1)
            return bank[b]

        def to_fill(name, i):
            b, n = fills[name, i]
            if n:
                nc.tensor.wait_ge(empty[b], n)
            return bank[b]

        def skewed3(eng, step):
            step(0, 0, True, False, False)
            step(1, 1, True, True, False)
            with eng.Fori(0, J // 2 - 1) as i:
                step(i * 2 + 2, 0, True, True, True)
                step(i * 2 + 3, 1, True, True, True)
            step(J, 0, False, True, True)
            step(J + 1, 1, False, False, True)

        NCONST = 12
        NPH = 3

        def apart(eng):
            eng.sem_inc(carrier, 1)

        def barrier(eng, k):
            apart(eng)
            eng.drain().then_inc(phase, 1)
            eng.wait_ge(phase, k * 5)
            apart(eng)

        def skewed(eng, step):
            step(0, 0, True, False, True)
            with eng.Fori(0, PAIRS // 2 - 1) as i:
                step(i * 2 + 1, 1, True, True, True)
                step(i * 2 + 2, 0, True, True, True)
            step(PAIRS - 1, 1, True, True, False)
            step(PAIRS, 0, False, True, False)

        def pairs(eng, body, n=PAIRS):
            with eng.Fori(0, n // 2) as i:
                for u in range(2):
                    body(i * 2 + u, u, i)

        block = ctx.enter_context(nc.Block())

        @block.sync
        def _(sp):
            for dst, src in ((ident, "c_ident"), (fy, "c_fy"), (fx, "c_fx"), (ix, "c_ix"), (iy, "c_iy"), (avg, "c_avg"),
                             (fc1, "fc1"), (fc1b, "fc1b"), (fc2, "fc2"), (fc2b, "fc2b"), (fc0b, "fc0b")):
                sp.dma_start(dst[:, :], io[src]).then_inc(cst, 16)
            sp.wait_ge(zero_done, 1)
            for s in range(2):
                sp.dma_start(fc0[3 * s:3 * s + 3, CH * s:CH * s + CH], io["fc0_w"]).then_inc(cst, 16)

            def load_image(n, u, i):
                sp.wait_ge(pF, n * 8 + 8)
                apart(sp)
                sp.dma_start(htile[0:6, u, :], io["x"][bass.ds(n, 1)].rearrange("a p m -> p (a m)")).then_inc(xld[u], 16)
            pairs(sp, load_image)
            barrier(sp, 1)

            def layer(l):
                def load_y(n, u, i):
                    N = l * PAIRS + n
                    sp.wait_ge(aG, N + 1)
                    apart(sp)
                    sp.dma_start(ytile[:, u, :], field[bass.ds(n, 1)].rearrange("a p m -> p (a m)")).then_inc(aYld[u], 16)
                pairs(sp, load_y)
                barrier(sp, l * NPH + 2)
                def load_modes(g, u, i):
                    G = l * CHUNKS + g
                    sp.wait_ge(mM, G * 8 + 8)
                    apart(sp)
                    for half, v in ((0, 0), (1, 1)):
                        xs = xmodes[bass.ds(g, 1), v].rearrange("a b c m -> c (a b) m")
                        sp.dma_start(xin[CH * half:CH * half + CH, u, 0], xs).then_inc(mXld[u], 16)
                    for half, v in ((0, 1), (1, 0)):
                        xs = xmodes[bass.ds(g, 1), v].rearrange("a b c m -> c (a b) m")
                        sp.dma_start(xin[CH * half:CH * half + CH, u, 1], xs).then_inc(mXld[u], 16)
                pairs(sp, load_modes, CHUNKS)
                for s in range(2):
                    sp.dma_start(pw[CH * s:CH * s + CH, CH * s:CH * s + CH], io["pw"][bass.ds(l, 1)].rearrange("a i o -> (a i) o")).then_inc(par, 16)
                sp.dma_start(vecs[:, :], io["vecs"][bass.ds(l, 1)].rearrange("a p k -> (a p) k")).then_inc(par, 16)
                barrier(sp, l * NPH + 3)
                def load_back(n, u, i):
                    N = l * PAIRS + n
                    M = l * (PAIRS // 2) + i
                    sp.wait_ge(bYst[u], M * 16 + 16)
                    apart(sp)
                    sp.wait_ge(bS, N + 1)
                    apart(sp)
                    sp.dma_start(ytile[:, u, :], field[bass.ds(n, 1)].rearrange("a p m -> p (a m)")).then_inc(bYld[u], 16)
                    sp.wait_ge(bK, N * 4 + 4)
                    apart(sp)
                    for v in range(2):
                        zs = zmodes[v, :, :, bass.ds(n * 2, 2), :].rearrange("k y b o -> k y (b o)")
                        sp.dma_start(zin[NKX * v:NKX * v + NKX, u], zs).then_inc(bZld[u], 16)
                pairs(sp, load_back)
                barrier(sp, l * NPH + 4)

            layer(0)
            with sp.Fori(1, LAYERS) as l:
                layer(l)

            def load_last(n, u, i):
                sp.wait_ge(fG, n + 1)
                apart(sp)
                apart(sp)
                sp.dma_start(ytile[:, u, :], field[bass.ds(n, 1)].rearrange("a p m -> p (a m)")).then_inc(fYld[u], 16)
            pairs(sp, load_last)
            barrier(sp, LAYERS * NPH + 2)
            for name in TAIL_W:
                sp.dma_start(tw[name], io["t_" + name]).then_inc(twl, 16)
            sp.wait_ge(ev["rows"], 2)
            sp.dma_start(h1t.rearrange("(g p m) -> p g m", g=8, p=P), rows.rearrange("p (g m) -> p g m", g=8)).then_inc(h1_st, 16)
            sp.wait_ge(h1_st, 16)
            sp.dma_start(h1.rearrange("p (j c) -> p j c", j=J), h1t.rearrange("(j p c) -> p j c", j=J, p=P)).then_inc(h1_ld, 16)
            sp.wait_ge(ev["done"], 1)
            sp.dma_start(io["out"].rearrange("(j p c) -> p j c", j=J, p=P), h2.rearrange("p (j c) -> p j c", j=J)).then_inc(out_st, 16)
            sp.wait_ge(out_st, 16)

        @block.gpsimd
        def _(pool):
            nc.gpsimd.memset(fc0[:, :], 0.0).then_inc(zero_done, 1)
            nc.gpsimd.memset(pw[:, :], 0.0)
            nc.gpsimd.memset(epst[:, :], BN_EPS)
            barrier(pool, 1)

            def layer(l):
                def load_w(g, u, i):
                    G = l * CHUNKS + g
                    pool.wait_ge(mM, G * 8 + 8)
                    pool.dma_start(wt[:, u], io["w"][bass.ds(G, 1)].rearrange("a p m o -> (a p) m o")).then_inc(wld[u], 16)
                for u in range(2):
                    load_w(u, u, 0)
                barrier(pool, l * NPH + 2)
                for u in range(2):
                    load_w(2 + u, u, 1)
                barrier(pool, l * NPH + 3)
                barrier(pool, l * NPH + 4)
            layer(0)
            with pool.Fori(1, LAYERS) as l:
                layer(l)
            barrier(pool, LAYERS * NPH + 2)
            n_clear = 0
            for dst, value in [(vb.rearrange("p u i q h o -> p (u i q h o)"), 0.0), (xt[64:65, :], 1.0), (eps5[:, :], 1e-5), (eps8[:, :], 1e-8)] + [
                    (vb[64 * h:64 * h + 64, u, :, :, h, 16:17].rearrange("p i q o -> p (i q) o"), 1.0) for h in range(2) for u in range(2)]:
                nc.gpsimd.memset(dst, value).then_inc(clear, 1)
                n_clear += 1
                pool.wait_ge(clear, n_clear)

        @block.tensor
        def _(pe):
            pe.sem_inc(pF, 16)
            pe.sem_inc(aT, 16)
            pe.sem_inc(mM, 16)
            pe.sem_inc(bK, 8)
            pe.sem_inc(bF, 16)
            pe.wait_ge(cst, 16 * (NCONST + 1))

            def lift(n, u, i):
                pe.wait_ge(xld[u], i * 16 + 16)
                for k in range(8):
                    pe.wait_ge(pFe, n * 8 + k + 1)
                    pe.matmul(bank[k % 4][:, :], fc0[0:6, :], htile[0:6, u, k * BANK:(k + 1) * BANK], start=True, stop=True).then_inc(pF, 1)
            pairs(pe, lift)
            barrier(pe, 1)

            def layer(l):
                def fwd(k, u, front, back, ahead):
                    N = l * PAIRS + k
                    B = N + (-1)
                    ub = 1 - u

                    def T(j):
                        pe.wait_ge(aTe, N * 8 + j + 1)
                        for t in range(4):
                            s = 4 * j + t
                            mm = pe.transpose(bank[j % 2][:, t * P:(t + 1) * P], htile[:, u, s * P:(s + 1) * P], ident[:, :])
                        mm.then_inc(aT, 1)

                    def Y(g):
                        pe.wait_ge(aTe, N * 8 + 2 * g + 4)
                        pe.wait_ge(aYe, N * 4 + g + 1)
                        for t in range(8):
                            mm = pe.matmul(bank[2 + g % 2][:, t * 64:(t + 1) * 64], ht[:, 8 * g + t, :], fy[:, :], start=True, stop=True)
                        mm.then_inc(aY, 1)

                    def R(j):
                        if j == 0:
                            pe.wait_ge(aYe, B * 4 + 6)
                        pe.wait_ge(aRe, B * 4 + j + 1)
                        for t in range(4):
                            mm = pe.transpose(bank[4 + j % 2][:, t * P:(t + 1) * P], atile[:, ub, 4 * j + t, :], ident[:, :])
                        mm.then_inc(aR, 1)

                    def X(g):
                        pe.wait_ge(aRe, B * 4 + 2 * g + 4)
                        pe.wait_ge(aXe, B * 2 + g + 1)
                        for t in range(8):
                            mm = pe.matmul(bank[6 + g][:, t * 64:(t + 1) * 64], att_t[:, 8 * g + t, :], fx[:, :], start=True, stop=True)
                        mm.then_inc(aX, 1)

                    if front:
                        pe.wait_ge(aG, N + 3)
                        T(0); T(1); T(2); T(3)
                    if back:
                        R(0); R(1)
                    if front:
                        Y(0); T(4); T(5)
                    if back:
                        R(2); R(3)
                    if front:
                        Y(1); T(6); T(7)
                    if back:
                        X(0)
                    if front:
                        Y(2)
                    if back:
                        X(1)
                    if front:
                        Y(3)
                skewed(pe, fwd)
                barrier(pe, l * NPH + 2)

                def mix(g, u, i):
                    G = l * CHUNKS + g
                    M = l * (CHUNKS // 2) + i
                    pe.wait_ge(wld[u], M * 16 + 16)
                    pe.wait_ge(mNeg, G + 1)
                    for k in range(8):
                        pe.wait_ge(mE[k % 2], G * 4 + k // 2 + 1)
                        for t in range(8):
                            for par_ in range(2):
                                y0 = 2 * (8 * k + t) % 16 + par_
                                x0 = (8 * k + t) // 8
                                mm = pe.matmul(bank[k][64 * par_:64 * par_ + 64, t * 64:(t + 1) * 64],
                                               xin[:, u, :, :, y0 * 8 + x0], wt[:, u, x0 * 16 + y0, :], start=True, stop=True)
                        mm.then_inc(mM, 1)
                pairs(pe, mix, CHUNKS)
                barrier(pe, l * NPH + 3)
                pe.wait_ge(par, l * 48 + 48)
                apart(pe)

                def inv(k, u, front, back, ahead):
                    N = l * PAIRS + k
                    B = N + (-1)
                    M = l * (PAIRS // 2)
                    ub = 1 - u

                    def K(j):
                        if j == 0:
                            pe.wait_ge(bZld[u], zcount(l, k, u))
                        pe.wait_ge(bKe, N * 4 + j + 1)
                        for t in range(4):
                            mm = pe.matmul(bank[j % 2][:, t * P:(t + 1) * P], zin[:, u, 4 * j + t, :], ix[:, :], start=True, stop=True)
                        mm.then_inc(bK, 1)

                    def T(j):
                        if j == 0:
                            pe.wait_ge(bKe, N * 4 + 6)
                        pe.wait_ge(bTe, N * 4 + j + 1)
                        for t in range(4):
                            q = 4 * j + t
                            mm = pe.transpose(bank[2 + j % 2][:, t * P:(t + 1) * P],
                                              gtile[:, 4 * q:4 * q + 4].rearrange("p x r k -> p (x r k)"), ident[:, :])
                        mm.then_inc(bT, 1)

                    def F(f):
                        if f == 0:
                            pe.wait_ge(bG, B + 1)
                            pe.wait_ge(bTe, B * 4 + 6)
                        pe.wait_ge(bFe, B * 8 + f + 1)
                        o = bank[4 + f % 4]
                        pe.matmul(o[:, :], pw[:, :], htile[:, ub, f * BANK:(f + 1) * BANK], start=True, stop=True)
                        for t in range(2):
                            mm = pe.matmul(o[:, t * 256:(t + 1) * 256], gt[:, ub, 2 * f + t, :], iy[:, :], start=False, stop=True,
                                           skip_group_check=True)
                        mm.then_inc(bF, 1)

                    if back:
                        F(0)
                    if front:
                        K(0); K(1)
                    if back:
                        F(1)
                    if front:
                        K(2); K(3)
                    if back:
                        F(2)
                    if front:
                        T(0); T(1)
                    if back:
                        F(3); F(4)
                    if front:
                        T(2); T(3)
                    if back:
                        F(5); F(6); F(7)
                skewed(pe, inv)
                pe.wait_ge(stv, l * 8 + 2)
                pe.matmul(bank[0][:, 0:1], avg[:, :], mv[:, 0:1], start=True, stop=True).then_inc(stp, 1)
                pe.wait_ge(stv, l * 8 + 5)
                pe.matmul(bank[0][:, 1:2], avg[:, :], sm[:, 3:4], start=True, stop=True).then_inc(stp, 1)
                barrier(pe, l * NPH + 4)

            def zcount(l, k, u):
                return (l * PAIRS + k - u) * 16 + 32
            layer(0)
            with pe.Fori(1, LAYERS) as l:
                layer(l)

            def last(n, u, i):
                pe.wait_ge(fG, n + 3)
                pe.wait_ge(fOe, n + 1)

                def C(s, j):
                    c = 8 * s + j
                    pe.wait_ge(fCe, n * 16 + c + 1)
                    pe.matmul(bank[c % 4][:, :], fc1[64 * s:64 * s + 64, :], htile[64 * s:64 * s + 64, u, j * BANK:(j + 1) * BANK],
                              start=True, stop=True).then_inc(fC, 1)

                def O(s, j):
                    c = 8 * s + j
                    pe.wait_ge(fCe, n * 16 + c + 1 + 4)
                    for t in range(4):
                        mm = pe.matmul(bank[4 + u][:, s * 32 + j * 4 + t:s * 32 + j * 4 + t + 1],
                                       work[:, (c % 4) * BANK + t * P:(c % 4) * BANK + (t + 1) * P], fc2[:, :], start=True, stop=True)
                    mm.then_inc(fO, 1)
                for c in range(18):
                    if c < 16:
                        C(c // 8, c % 8)
                    if c >= 2:
                        O((c - 2) // 8, (c - 2) % 8)
            pairs(pe, last)
            barrier(pe, LAYERS * NPH + 2)

            def stage_T(name, src, cols=CH):
                for j in range(src.shape[1] // cols):
                    b = j // 4
                    o = to_fill(name, b) if j % 4 == 0 else bank[fills[name, b][0]]
                    mm = pe.transpose(o[0:cols, (j % 4) * P:(j % 4 + 1) * P], src[:, j * cols:(j + 1) * cols], ident[:, :])
                    if j % 4 == 3:
                        mm.then_inc(full[fills[name, b][0]], 1)

            def stage_W(name, w, src, n, k):
                per = min(BANK // n, J)
                for j in range(J):
                    b = j // per
                    o = to_fill(name, b) if j % per == 0 else bank[fills[name, b][0]]
                    mm = pe.matmul(o[:, (j % per) * n:(j % per + 1) * n], src[0:k, j * P:(j + 1) * P], w, start=True, stop=True)
                    if j % per == per - 1:
                        mm.then_inc(full[fills[name, b][0]], 1)

            def stage_F(name, w, src, m):
                for b in range(4):
                    o = to_fill(name, b)
                    pe.matmul(o[0:m, :], w, src[:, b * BANK:(b + 1) * BANK], start=True, stop=True).then_inc(full[fills[name, b][0]], 1)

            pe.wait_ge(twl, 16 * len(TAIL_W))
            stage_T("rows", tok[:, :], P)
            pe.wait_ge(ev["xn"], 1)
            stage_T("xT", xn)
            pe.wait_ge(clear, 8)
            pe.wait_ge(ev["xT"], 4)
            stage_F("q", tw["wq2"][:, :], xt[:, :], P)
            stage_W("kv", tw["wkv"][:, :], xt, P, 65)
            pe.wait_ge(ev["kn"], 1)
            for j in range(J):
                o = to_fill("kvm", j // 8) if j % 8 == 0 else bank[fills["kvm", j // 8][0]]
                for i in range(2):
                    half = slice(64 * i, 64 * i + 64)
                    mm = pe.matmul(o[half, (j % 8) * CH:(j % 8 + 1) * CH], kn[half, j * CH:(j + 1) * CH], vn[half, j * CH:(j + 1) * CH],
                                   start=True, stop=True)
                if j % 8 == 7:
                    mm.then_inc(full[fills["kvm", j // 8][0]], 1)
            pe.wait_ge(ev["qT"], 4)
            pe.wait_ge(ev["kvm"], 2)
            for j in range(J):
                o = to_fill("out", j // 8) if j % 8 == 0 else bank[fills["out", j // 8][0]]
                for i in range(2):
                    half = slice(64 * i, 64 * i + 64)
                    mm = pe.matmul(o[half, (j % 8) * CH:(j % 8 + 1) * CH], qt[half, j * P + 64 * i:j * P + 64 * i + 64],
                                   kvm[half, j * CH:(j + 1) * CH], start=True, stop=True)
                if j % 8 == 7:
                    mm.then_inc(full[fills["out", j // 8][0]], 1)
            pe.wait_ge(ev["ret"], 1)
            stage_T("retT", ret)
            pe.wait_ge(ev["retT"], 4)
            stage_W("proj", tw["wproj"][:, :], xt, CH, 65)
            pe.wait_ge(ev["x2"], 1)
            stage_T("x2T", x2)
            pe.wait_ge(ev["x2T"], 4)
            pe.wait_ge(ev["ga"], 2)
            pe.wait_ge(masks, 2)

            def pair_step(k, u, proj, score, comb):
                u1 = 1 - u

                def project():
                    pe.wait_ge(lSXe, k + 1)
                    pe.matmul(bank[0][:, 0:P], tw["hlp"][:, :], xt[:, bass.ds(k * P, P)], start=True, stop=True).then_inc(lSX, 1)

                def project2():
                    pe.wait_ge(lSXe, k + 2)
                    pe.wait_ge(lQe, k + 1)
                    for e in range(4):
                        mm = pe.matmul(bank[1][:, e * P:(e + 1) * P], tw["wqp"][:, e, :], sxT[:, u, :], start=True, stop=True)
                    mm.then_inc(lQ, 1)
                    pe.wait_ge(lKe, k + 1)
                    for n in range(4):
                        mm = pe.matmul(bank[2][:, n * P:(n + 1) * P], tw["wkp"][:, n, :], sxT[:, u, :], start=True, stop=True)
                    mm.then_inc(lK, 1)
                    pe.wait_ge(lVe, k + 1)
                    for i in range(2):
                        for h in range(2):
                            pe.matmul(bank[3][64 * h:64 * h + 64, i * 32:(i + 1) * 32], sxT[:, u, 64 * i:64 * i + 64], tw["wvp"][:, h, :],
                                      start=True, stop=True)
                    pe.transpose(bank[3][:, P:2 * P], sxT[:, u, :], ident[:, :]).then_inc(lV, 1)

                def scores(i):
                    B = k + (-1)
                    if i == 0:
                        pe.wait_ge(lQe, B + 2)
                        pe.wait_ge(lKe, B + 2)
                    pe.wait_ge(lSe, B * 2 + i + 1)
                    o = bank[4 + i]
                    pe.matmul(o[:, :], identb[:, :], maskb[:, :], start=True, stop=True)
                    for q in range(2):
                        mm = pe.matmul(o[:, q * 256:(q + 1) * 256], qb[:, u1, i * 256 + q * P:i * 256 + (q + 1) * P],
                                       kb[:, u1, i * 256:(i + 1) * 256], start=False, stop=True, skip_group_check=True)
                    mm.then_inc(lS, 1)

                def turn(i):
                    C = k + (-2)
                    pe.wait_ge(lE, C * 2 + i + 1)
                    pe.wait_ge(lTe, C * 2 + i + 1)
                    for q in range(4):
                        mm = pe.transpose(bank[6][:, q * P:(q + 1) * P], ex[:, u, i, q * P:(q + 1) * P], ident[:, :])
                    mm.then_inc(lT, 1)

                def combine(i):
                    C = k + (-2)
                    pe.wait_ge(lTe, C * 2 + i + 2)
                    if i == 0:
                        pe.wait_ge(lVe, C + 2)
                        pe.wait_ge(lOe, C + 1)
                    for e2 in range(2):
                        for q in range(2):
                            for h in range(2):
                                at = ((e2 * 2 + q) * 2 + h) * 34
                                mm = pe.matmul(bank[7][64 * i:64 * i + 64, at:at + 34],
                                               exT[:, i, (q * 2 + h) * P + 64 * e2:(q * 2 + h) * P + 64 * e2 + 64],
                                               vb[:, u, i, h].rearrange("p h o -> p (h o)"), start=True, stop=True)
                    if i == 1:
                        mm.then_inc(lO, 1)
                if proj: project()
                if comb: turn(0)
                if score: scores(0)
                if proj: project2()
                if comb: combine(0); turn(1)
                if score: scores(1)
                if comb: combine(1)
            skewed3(pe, pair_step)

            pe.wait_ge(ev["att"], 1)
            stage_T("attT", att_out, P)
            pe.wait_ge(ev["attT"], 8)
            o = to_fill("gate", 0)
            for j in range(J):
                for h in range(2):
                    mm = pe.matmul(o[:, j * 16:(j + 1) * 16], att_T[:, (2 * j + h) * P:(2 * j + h + 1) * P], tw["gwb"][:, h, :],
                                   start=(h == 0), stop=(h == 1))
            mm.then_inc(full[fills["gate", 0][0]], 1)
            pe.wait_ge(ev["fx"], 1)
            stage_T("fT", fxt)
            pe.wait_ge(ev["fxT"], 4)
            stage_F("fc1", tw["fc1d"][:, :], xt[:, :], CH)
            pe.wait_ge(ev["hx"], 4)
            stage_W("fc2", tw["fc2d"][:, :], xt, CH, 65)
            pe.wait_ge(ev["fo"], 1)
            stage_T("foT", fo)
            pe.wait_ge(ev["foT"], 4)
            o = to_fill("fg", 0)
            for j in range(J):
                mm = pe.matmul(o[:, j * 4:(j + 1) * 4], xt[0:64, j * P:(j + 1) * P], tw["fgt"][:, :], start=True, stop=True)
            mm.then_inc(full[fills["fg", 0][0]], 1)

        @block.vector
        def _(dve):
            dve.sem_inc(aTe, 2)
            dve.sem_inc(aRe, 2)
            dve.sem_inc(mE[1], 4)
            dve.sem_inc(bKe, 2)
            dve.sem_inc(bTe, 2)
            dve.sem_inc(bS, 2)
            dve.sem_inc(fOe, 2)
            barrier(dve, 1)

            def layer(l):
                def fwd(k, u, front, back, ahead):
                    N = l * PAIRS + k
                    B = N + (-1)

                    def T(j):
                        dve.wait_ge(aT, N * 8 + j + 1 + 16)
                        dve.tensor_copy(ht[:, 4 * j:4 * j + 4, :].rearrange("p t c -> p (t c)"), bank[j % 2][:, :]).then_inc(aTe, 1)

                    def R(j):
                        dve.wait_ge(aR, B * 4 + j + 1)
                        dve.tensor_copy(att_t[:, 4 * j:4 * j + 4, :].rearrange("p t c -> p (t c)"), bank[4 + j % 2][:, :]).then_inc(aRe, 1)
                    if front:
                        T(0); T(1); T(2); T(3)
                    if back:
                        R(0); R(1)
                    if front:
                        T(4); T(5)
                    if back:
                        R(2); R(3)
                    if front:
                        T(6); T(7)
                skewed(dve, fwd)
                barrier(dve, l * NPH + 2)

                def mix(g, u, i):
                    G = l * CHUNKS + g
                    M = l * (CHUNKS // 2) + i
                    dve.wait_ge(mZst[u], M * 64 + 64)
                    for k in range(1, 8, 2):
                        dve.wait_ge(mM, G * 8 + k + 1 + 16)
                        dve.tensor_copy(zout[:, u, 8 * k:8 * k + 8, :].rearrange("p m o -> p (m o)"), bank[k][:, :]).then_inc(mE[1], 1)
                pairs(dve, mix, CHUNKS)
                barrier(dve, l * NPH + 3)

                def inv(k, u, front, back, ahead):
                    N = l * PAIRS + k
                    B = N + (-1)
                    ub = 1 - u

                    def K(j):
                        dve.wait_ge(bK, N * 4 + j + 1 + 8)
                        dst = gtile[:, :, :, 4 * j:4 * j + 4].rearrange("p x r k -> p k r x")
                        dve.tensor_copy(dst, bank[j % 2][:, :].rearrange("p (k r x) -> p k r x", k=4, r=2)).then_inc(bKe, 1)

                    def T(j):
                        dve.wait_ge(bT, N * 4 + j + 1)
                        dve.tensor_copy(gt[:, u, 4 * j:4 * j + 4, :].rearrange("p t c -> p (t c)"), bank[2 + j % 2][:, :]).then_inc(bTe, 1)

                    def S(f):
                        dve.wait_ge(bFe, B * 8 + f + 1 + 4)
                        at = (k + (-1)) * 8 + f
                        st = dve.bn_stats(stats[:, bass.ds(at, 1), :].rearrange("p a s -> p (a s)"), ytile[:, ub, f * BANK:(f + 1) * BANK])
                        if f == 7:
                            st.then_inc(bS, 1)
                    if front:
                        K(0); K(1)
                    if back:
                        S(0)
                    if front:
                        K(2); K(3)
                    if back:
                        S(1)
                    if front:
                        T(0); T(1)
                    if back:
                        S(2); S(3)
                    if front:
                        T(2); T(3)
                    if back:
                        S(4); S(5); S(6); S(7)
                skewed(dve, inv)
                dve.wait_ge(bS, l * PAIRS + PAIRS + 2)
                dve.bn_aggr(mv[:, :], stats[:, :, :].rearrange("p a s -> p (a s)")).then_inc(stv, 2)
                dve.wait_ge(stp, l * 2 + 1)
                dve.tensor_copy(sm[:, 0:1], bank[0][:, 0:1]).then_inc(stv, 1)
                dve.wait_ge(stv, l * 8 + 3)
                dve.tensor_tensor(sm[:, 1:2], mv[:, 0:1], sm[:, 0:1], ALU.subtract).then_inc(stv, 1)
                dve.wait_ge(stv, l * 8 + 4)
                dve.scalar_tensor_tensor(out=sm[:, 3:4], in0=sm[:, 1:2], scalar=sm[:, 1:2], in1=mv[:, 1:2], op0=ALU.mult, op1=ALU.add).then_inc(stv, 1)
                dve.wait_ge(sta, l + 1)
                dve.reciprocal(sm[:, 5:6], sm[:, 4:5]).then_inc(stv, 1)
                dve.wait_ge(stv, l * 8 + 6)
                dve.tensor_tensor(bn_scale[:, :], sm[:, 5:6], vecs[:, 1:2], ALU.mult).then_inc(stv, 1)
                dve.wait_ge(stv, l * 8 + 7)
                dve.tensor_tensor(sm[:, 6:7], sm[:, 0:1], bn_scale[:, :], ALU.mult).then_inc(stv, 1)
                dve.wait_ge(stv, l * 8 + 8)
                dve.tensor_tensor(bn_bias[:, :], vecs[:, 2:3], sm[:, 6:7], ALU.subtract)
                barrier(dve, l * NPH + 4)
            layer(0)
            with dve.Fori(1, LAYERS) as l:
                layer(l)

            def last(n, u, i):
                dve.wait_ge(fO, n * 16 + 16)
                dve.tensor_scalar(tok[:, bass.ds(n * 64, 64)], bank[4 + u][:, 0:64], fc2b[:, 0:1], None, ALU.add).then_inc(fOe, 1)
            pairs(dve, last)
            dve.sem_inc(lKe, 1)
            dve.sem_inc(lSe, 2)
            dve.sem_inc(lTe, 1)
            dve.sem_inc(lOe, 1)
            dve.sem_inc(lVe, 1)
            barrier(dve, LAYERS * NPH + 2)
            n_chain = [0]

            def link(ins):
                n_chain[0] += 1
                ins.then_inc(chain, 1)
                dve.wait_ge(chain, n_chain[0])

            n_var = [0]

            def g3(x, g):
                return x.rearrange("p (g d) -> p g d", g=g)

            def wide(x, d):
                return x.rearrange("p (g o) -> p g o", o=1).to_broadcast([P, x.shape[1], d])

            def center_norm(x, out, g, d, eps_after=None):
                link(dve.tensor_reduce(s1[:, 0:g], g3(x, g), AX.X, ALU.add))
                link(dve.scalar_tensor_tensor(out=g3(xc[:, 0:g * d], g), in0=wide(s1[:, 0:g], d), scalar=-1.0 / d, in1=g3(x, g),
                                              op0=ALU.mult, op1=ALU.add))
                link(dve.tensor_tensor(sq[:, 0:g * d], xc[:, 0:g * d], xc[:, 0:g * d], ALU.mult))
                dve.tensor_reduce(s2[:, 0:g], g3(sq[:, 0:g * d], g), AX.X, ALU.add).then_inc(ev["var"], 1)
                n_var[0] += 1
                dve.wait_ge(ev["rstd"], n_var[0])
                if eps_after is not None:
                    link(dve.tensor_scalar(sd[:, 0:g], sd[:, 0:g], eps_after, None, ALU.add))
                link(dve.reciprocal(s2[:, 0:g], sd[:, 0:g]))
                return dve.tensor_tensor(g3(out, g), g3(xc[:, 0:g * d], g), wide(s2[:, 0:g], d), ALU.mult)

            def per_tile(w, n):
                return w.rearrange("p (o n) -> p o n", o=1).to_broadcast([P, J, n])

            dve.wait_ge(h1_ld, 16)
            center_norm(h1, xn, J, CH).then_inc(ev["xn"], 1)
            for b in range(4):
                o = filled(dve, "kv", b)
                ins = dve.tensor_copy(kv[:, b * BANK:(b + 1) * BANK], o[:, :])
                ins.then_inc(empty[fills["kv", b][0]], 1)
            for b in range(4):
                dve.wait_ge(empty[fills["kv", b][0]], fills["kv", b][1] + 1)
            link(center_norm(kv, kv, 512, 4, 1e-5))
            link(dve.tensor_tensor(g3(kv, J), g3(kv, J), per_tile(tw["kvw"], P), ALU.mult))
            for t, dst in ((0, kn), (1, vn)):
                src = kv.rearrange("p (j h t d) -> p t (j h) d", j=J, t=2, d=4)[:, t]
                link(dve.tensor_copy(dst.rearrange("p (g d) -> p g d", d=4), src))
            link(dve.tensor_tensor(g3(kn, J), g3(kn, J), per_tile(tw["kvb"][:, 0:CH], CH), ALU.add))
            dve.tensor_tensor(g3(vn, J), g3(vn, J), per_tile(tw["kvb"][:, CH:2 * CH], CH), ALU.add).then_inc(ev["kn"], 1)
            for b in range(2):
                o = filled(dve, "kvm", b)
                bd = tw["bd"].rearrange("p (o n) -> p o n", o=1).to_broadcast([P, 8, CH])
                dve.tensor_tensor(g3(kvm[:, b * BANK:(b + 1) * BANK], 8), g3(o[:, :], 8), bd, ALU.mult).then_inc(ev["kvm"], 1)
            dve.wait_ge(ev["kvm"], 2)
            for b in range(2):
                dve.sem_inc(empty[fills["kvm", b][0]], 1)
            for b in range(2):
                o = filled(dve, "out", b)
                link(dve.tensor_tensor(ret[:, b * BANK:(b + 1) * BANK], o[:, :], xn[:, b * BANK:(b + 1) * BANK], ALU.add))
                dve.sem_inc(empty[fills["out", b][0]], 1)
            dve.sem_inc(ev["ret"], 1)
            link(dve.tensor_tensor(h2, h1, xn, ALU.add))
            dve.wait_ge(ev["ga"], 2)
            link(dve.tensor_tensor(h2, h2, ga, ALU.add))
            center_norm(h2, x2, J, CH).then_inc(ev["x2"], 1)

            def pair_step(k, u, proj, score, comb):
                u1 = 1 - u

                def keys():
                    dve.wait_ge(lK, k + 1)
                    dst = kb[:, u].rearrange("p (i n t) -> p n i t", i=2, n=4)
                    dve.tensor_copy(dst, bank[2][:, :].rearrange("p (n i t) -> p n i t", n=4, i=2)).then_inc(lKe, 1)

                def values():
                    dve.wait_ge(lV, k + 1)
                    for h in range(2):
                        src = bank[3][64 * h:64 * h + 64, 0:64].rearrange("p (iq o) -> p iq o", o=16)
                        dve.tensor_copy(vb[64 * h:64 * h + 64, u, :, :, h, 0:16].rearrange("p i q o -> p (i q) o"), src)
                    dve.tensor_copy(sx[:, bass.ds(k * CH, CH)].rearrange("p (n d) -> p n d", d=16),
                                    bank[3][:, P:2 * P].rearrange("p (n d) -> p n d", d=32)[:, :, 0:16]).then_inc(lVe, 1)

                def soft(i):
                    B = k + (-1)
                    dve.wait_ge(lS, B * 2 + i + 1)
                    v = bank[4 + i][:, :].rearrange("p (g t) -> p g t", t=64)
                    dve.tensor_reduce(mx[:, u1, i, :], v, AX.X, ALU.max).then_inc(lMx, 1)
                    dve.wait_ge(lMx, B * 2 + i + 1)
                    m = mx[:, u1, i, :].rearrange("p (g o) -> p g o", o=1).to_broadcast([P, 8, 64])
                    dve.tensor_tensor(ex[:, u1, i, :].rearrange("p (g t) -> p g t", t=64), v, m, ALU.subtract).then_inc(lSe, 1)

                def turned(i):
                    C = k + (-2)
                    dve.wait_ge(lT, C * 2 + i + 1)
                    dve.tensor_copy(exT[:, i, :], bank[6][:, :]).then_inc(lTe, 1)

                def divide():
                    C = k + (-2)
                    dve.wait_ge(lO, C + 1)
                    v = bank[7][:, 0:272].rearrange("p (g o) -> p g o", o=17)
                    dve.reciprocal(rden[:, u, :].rearrange("p (g o) -> p g o", o=1), v[:, :, 16:17]).then_inc(lRd, 1)
                    dve.wait_ge(lRd, C + 1)
                    for e2 in range(2):
                        r = rden[:, u, 8 * e2:8 * e2 + 8].rearrange("p (g o) -> p g o", o=1).to_broadcast([P, 8, 16])
                        for ep in range(2):
                            d = att_out[:, bass.ds(C * 256 + ep * 128 + e2 * 64, 64)].rearrange("p (n d) -> p n d", d=16)
                            g = e2 * 8 + ep * 4
                            rr = rden[:, u, g:g + 4].rearrange("p (g o) -> p g o", o=1).to_broadcast([P, 4, 16])
                            ins = dve.tensor_tensor(d, v[:, g:g + 4, 0:16], rr, ALU.mult)
                    ins.then_inc(lOe, 1)
                if comb: turned(0)
                if score: soft(0)
                if proj: keys()
                if comb: turned(1)
                if score: soft(1)
                if comb: divide()
                if proj: values()
            dve.wait_ge(clear, 8)
            skewed3(dve, pair_step)
            dve.wait_ge(lOe, J + 1)
            apart(dve)
            link(dve.tensor_scalar(keep, sx, 0.0, None, ALU.not_equal))
            a4 = att_out.rearrange("p (j e c) -> p e j c", j=J, e=4)
            for e in range(4):
                ins = dve.tensor_tensor(a4[:, e], a4[:, e], g3(keep, J), ALU.mult)
            link(ins)
            dve.sem_inc(ev["att"], 1)
            for n in range(4):
                src = sx[64 * (n % 2):64 * (n % 2) + 64, (n // 2) * CH + 16 * n:(n // 2) * CH + 16 * n + 16]
                for i in range(2):
                    ins = dve.tensor_copy(res[64 * i:64 * i + 64, 16 * n:16 * n + 16], src)
            link(ins)
            for b in range(0, 8, 2):
                o = filled(dve, "attT", b)
                link(dve.tensor_copy(att_T[:, b * BANK:(b + 1) * BANK], o[:, :]))
                dve.sem_inc(empty[fills["attT", b][0]], 1)
                dve.sem_inc(ev["attT"], 1)
            o = filled(dve, "gate", 0)
            link(dve.tensor_tensor(g3(lg, J), g3(o[:, 0:256], J), per_tile(tw["gateb"], 16), ALU.add))
            dve.sem_inc(empty[fills["gate", 0][0]], 1)
            link(dve.tensor_reduce(gmax, g3(lg, 64), AX.X, ALU.max))
            link(dve.tensor_tensor(g3(lg, 64), g3(lg, 64), wide(gmax, 4), ALU.subtract))
            dve.sem_inc(ev["lg"], 1)
            dve.wait_ge(ev["gexp"], 1)
            link(dve.tensor_reduce(gsum, g3(gexp, 64), AX.X, ALU.add))
            link(dve.reciprocal(gmax, gsum))
            link(dve.tensor_tensor(g3(gexp, 64), g3(gexp, 64), wide(gmax, 4), ALU.mult))
            ge = gexp.rearrange("p (jn e) -> p e jn", e=4)
            for e in range(4):
                gw = ge[:, e].rearrange("p (g o) -> p g o", o=1).to_broadcast([P, 64, 16])
                dst = mixed if e == 0 else prod[:, 0:TD]
                gwj = gw.rearrange("p (j n) d -> p j n d", j=J)
                link(dve.tensor_tensor(dst.rearrange("p (j n d) -> p j n d", j=J, d=16),
                                       a4[:, e].rearrange("p j (n d) -> p j n d", d=16), gwj, ALU.mult))
                if e:
                    link(dve.tensor_tensor(mixed, mixed, prod[:, 0:TD], ALU.add))
            link(dve.tensor_tensor(g3(mixed, J), g3(mixed, J), per_tile(res[:, :], CH), ALU.add))
            link(center_norm(mixed, fxt, 64, 16))
            link(dve.tensor_tensor(g3(fxt, J), g3(fxt, J), per_tile(tw["lng"], CH), ALU.mult))
            link(dve.tensor_tensor(g3(fxt, J), g3(fxt, J), per_tile(tw["lnb"], CH), ALU.add))
            dve.sem_inc(ev["fx"], 1)
            link(dve.tensor_scalar(keep, fxt, 0.0, None, ALU.not_equal))
            dve.wait_ge(ev["fxT"], 4)
            link(dve.tensor_scalar(keepT, xt[0:64, :], 0.0, None, ALU.not_equal))
            for b in range(4):
                o = filled(dve, "fc1", b)
                if b == 0:
                    filled(dve, "fc1", 3)
                link(dve.scalar_tensor_tensor(out=xt[0:64, b * BANK:(b + 1) * BANK], in0=o[0:64, :], scalar=0.0,
                                              in1=keepT[:, b * BANK:(b + 1) * BANK], op0=ALU.max, op1=ALU.mult))
                dve.sem_inc(empty[fills["fc1", b][0]], 1)
                dve.sem_inc(ev["hx"], 1)
            for b in range(2):
                o = filled(dve, "fc2", b)
                link(dve.tensor_tensor(hx[:, b * BANK:(b + 1) * BANK], o[:, :], keep[:, b * BANK:(b + 1) * BANK], ALU.mult))
                dve.sem_inc(empty[fills["fc2", b][0]], 1)
            link(dve.tensor_tensor(hx, hx, fxt, ALU.add))
            link(center_norm(hx, fo, 64, 16))
            link(dve.tensor_tensor(g3(fo, J), g3(fo, J), per_tile(tw["fng"], CH), ALU.mult))
            link(dve.tensor_tensor(g3(fo, J), g3(fo, J), per_tile(tw["fnb"], CH), ALU.add))
            dve.sem_inc(ev["fo"], 1)
            o = filled(dve, "fg", 0)
            v = g3(o[:, 0:64], J)
            link(dve.tensor_reduce(gmax[:, 0:J], v, AX.X, ALU.max))
            link(dve.tensor_tensor(g3(lg[:, 0:64], J), v, wide(gmax[:, 0:J], 4), ALU.subtract))
            dve.sem_inc(ev["fl"], 1)
            dve.wait_ge(ev["fexp"], 1)
            link(dve.tensor_reduce(gsum[:, 0:J], g3(gexp[:, 0:64], J), AX.X, ALU.add))
            link(dve.reciprocal(gmax[:, 0:J], gsum[:, 0:J]))
            link(dve.tensor_tensor(g3(gexp[:, 0:64], J), g3(gexp[:, 0:64], J), wide(gmax[:, 0:J], 4), ALU.mult))
            link(dve.tensor_tensor(g3(fo, 64), g3(fo, 64), wide(gexp[:, 0:64], 16), ALU.mult))
            dve.tensor_tensor(h2, h2, fo, ALU.add).then_inc(ev["done"], 1)

        @block.scalar
        def _(act):
            act.sem_inc(pFe, 4)
            act.sem_inc(pSt[0], 16)
            act.sem_inc(pSt[1], 16)
            act.sem_inc(aG, 2)
            act.sem_inc(aYe, 2)
            act.sem_inc(aXe, 2)
            act.sem_inc(aXst[0], 16)
            act.sem_inc(aXst[1], 16)
            act.sem_inc(mE[0], 4)
            act.sem_inc(mZst[0], 64)
            act.sem_inc(mZst[1], 64)
            act.sem_inc(bFe, 4)
            act.sem_inc(bYst[0], 16)
            act.sem_inc(bYst[1], 16)
            act.sem_inc(fG, 2)
            act.sem_inc(fCe, 4)
            act.wait_ge(cst, 16 * (NCONST + 1))

            def lift(n, u, i):
                act.wait_ge(pSt[u], i * 16 + 16)
                for k in range(8):
                    act.wait_ge(pF, n * 8 + k + 1 + 16)
                    act.activation(ytile[:, u, k * BANK:(k + 1) * BANK], bank[k % 4][:, :], ACT.Identity, bias=fc0b[:, 0:1]).then_inc(pFe, 1)
                act.wait_ge(pFe, n * 8 + 8 + 4)
                act.dma_start(field[bass.ds(n, 1)].rearrange("a p m -> p (a m)"), ytile[:, u, :]).then_inc(pSt[u], 16)
            pairs(act, lift)
            for u in range(2):
                act.wait_ge(pSt[u], 16 * (PAIRS // 2 + 1))
            barrier(act, 1)

            def layer(l, first):
                def gelu(q, u):
                    src = ytile[:, u, q * 1024:(q + 1) * 1024]
                    dst = htile[:, u, q * 1024:(q + 1) * 1024]
                    if first:
                        return act.activation(dst, src, ACT.Identity)
                    return act.activation(dst, src, ACT.Gelu, bias=bn_bias[:, 0:1], scale=bn_scale[:, 0:1])

                def fwd(k, u, front, back, ahead):
                    N = l * PAIRS + k
                    B = N + (-1)
                    ub = 1 - u

                    def A(q):
                        if q == 0:
                            act.wait_ge(aYld[ub], (l * PAIRS + k + 1 - ub) * 8 + 16)
                            act.wait_ge(aT, (N + 1) * 8 + 8)
                        h = gelu(q, ub)
                        if q == 3:
                            h.then_inc(aG, 1)

                    def Y(g):
                        act.wait_ge(aY, N * 4 + g + 1)
                        dst = atile[:, u].rearrange("p k (r x) -> p x r k", r=2)[:, 16 * g:16 * g + 16]
                        act.copy(dst, bank[2 + g % 2][:, :].rearrange("p (x r k) -> p x r k", x=16, r=2)).then_inc(aYe, 1)

                    def X(g):
                        if g == 0:
                            act.wait_ge(aXst[ub], (B - ub) * 8 + 16)
                        act.wait_ge(aX, B * 2 + g + 1)
                        src = bank[6 + g][:, :].rearrange("p (k r c x) -> p r c k x", k=8, r=2, c=CHUNKS)
                        for r in range(2):
                            dst = xout[:, ub, :, r, 64 * g:64 * g + 64].rearrange("p c (k x) -> p c k x", x=8)
                            cp = act.copy(dst, src[:, r])
                        cp.then_inc(aXe, 1)

                    if ahead: A(0)
                    if front: Y(0)
                    if ahead: A(1)
                    if front: Y(1)
                    if back: X(0)
                    if ahead: A(2)
                    if front: Y(2)
                    if ahead: A(3)
                    if back: X(1)
                    if front: Y(3)
                    if back:
                        act.wait_ge(aXe, B * 2 + 4)
                        dst = xmodes.rearrange("g r b c m -> (b c) (g r) m")[bass.ds((k + (-1)) * P, P)]
                        act.dma_start(dst, xout[:, ub].rearrange("p g r m -> p (g r) m")).then_inc(aXst[ub], 16)
                act.wait_ge(aYld[0], l * PAIRS * 8 + 16)
                for q in range(4):
                    h = gelu(q, 0)
                h.then_inc(aG, 1)
                skewed(act, fwd)
                for u in range(2):
                    act.wait_ge(aXst[u], (l + 1) * 8 * PAIRS + 16)
                barrier(act, l * NPH + 2)

                def mix(g, u, i):
                    G = l * CHUNKS + g
                    M = l * (CHUNKS // 2) + i
                    act.wait_ge(mXld[u], M * 64 + 64)
                    act.mul(xin[CH:P, u, 0], xin[CH:P, u, 0], -1.0).then_inc(mNeg, 1)
                    act.wait_ge(mZst[u], M * 64 + 64)
                    for k in range(0, 8, 2):
                        act.wait_ge(mM, G * 8 + k + 1 + 16)
                        act.copy(zout[:, u, 8 * k:8 * k + 8, :].rearrange("p m o -> p (m o)"), bank[k][:, :]).then_inc(mE[0], 1)
                    act.wait_ge(mE[0], G * 4 + 4 + 4)
                    act.wait_ge(mE[1], G * 4 + 4 + 4)
                    for parity in range(2):
                        for v in range(2):
                            p0 = 64 * parity + 32 * v
                            dst = zmodes[v].rearrange("k (y q) b o -> q b (k y) o", q=2)[parity][:, bass.ds(g * 64, 64), :]
                            act.dma_start(dst, zout[p0:p0 + 32, u]).then_inc(mZst[u], 16)
                pairs(act, mix, CHUNKS)
                for u in range(2):
                    act.wait_ge(mZst[u], (l + 1) * 128 + 64)
                barrier(act, l * NPH + 3)
                act.wait_ge(par, l * 48 + 48)

                def inv(k, u, front, back, ahead):
                    N = l * PAIRS + k
                    B = N + (-1)
                    ub = 1 - u

                    def A(q):
                        if q == 0:
                            act.wait_ge(bYld[u], (N - u) * 8 + 16)
                            act.wait_ge(bF, N * 8 + 8)
                        h = gelu(q, u)
                        if q == 3:
                            h.then_inc(bG, 1)

                    def F(f):
                        act.wait_ge(bF, B * 8 + f + 1 + 16)
                        act.activation(ytile[:, ub, f * BANK:(f + 1) * BANK], bank[4 + f % 4][:, :], ACT.Identity, bias=vecs[:, 0:1]).then_inc(bFe, 1)
                    if front: A(0)
                    if back: F(0)
                    if front: A(1)
                    if back: F(1)
                    if back: F(2)
                    if front: A(2)
                    if back: F(3)
                    if back: F(4)
                    if front: A(3)
                    if back:
                        F(5); F(6); F(7)
                        act.wait_ge(bFe, B * 8 + 8 + 4)
                        act.dma_start(field[bass.ds(k + (-1), 1)].rearrange("a p m -> p (a m)"), ytile[:, ub, :]).then_inc(bYst[ub], 16)
                skewed(act, inv)
                for u in range(2):
                    act.wait_ge(bYst[u], (l + 1) * 8 * PAIRS + 16)
                act.wait_ge(stp, l * 2 + 2)
                act.activation(sm[:, 4:5], bank[0][:, 1:2], ACT.Sqrt, bias=epst[:, 0:1]).then_inc(sta, 1)
                barrier(act, l * NPH + 4)
            layer(0, True)
            with act.Fori(1, LAYERS) as l:
                layer(l, False)

            def lastg(u, q):
                return act.activation(htile[:, u, q * 1024:(q + 1) * 1024], ytile[:, u, q * 1024:(q + 1) * 1024], ACT.Gelu,
                                      bias=bn_bias[:, 0:1], scale=bn_scale[:, 0:1])

            def last(n, u, i):
                act.wait_ge(fYld[u], i * 16 + 16)
                for q in range(4):
                    h = lastg(u, q)
                h.then_inc(fG, 1)
                for c in range(16):
                    act.wait_ge(fC, n * 16 + c + 1)
                    act.activation(work[:, (c % 4) * BANK:(c % 4 + 1) * BANK], bank[c % 4][:, :], ACT.Gelu, bias=fc1b[:, 0:1]).then_inc(fCe, 1)
            pairs(act, last)
            act.sem_inc(lSXe, 1)
            act.sem_inc(lQe, 1)
            barrier(act, LAYERS * NPH + 2)

            def move(name, b, dst, event, parts=P):
                o = filled(act, name, b)
                act.copy(dst, o[0:parts, :]).then_inc(ev[event], 1)

            def emptied(name, n, event):
                act.wait_ge(ev[event], n)
                for b in range(n):
                    act.sem_inc(empty[fills[name, b][0]], 1)

            def root(n, g, scale, eps):
                act.wait_ge(ev["var"], n)
                bias = {} if eps is None else {"bias": eps[:, 0:1]}
                act.activation(sd[:, 0:g], s2[:, 0:g], ACT.Sqrt, scale=scale, **bias).then_inc(ev["rstd"], 1)

            for b in range(2):
                move("rows", b, rows[:, b * BANK:(b + 1) * BANK], "rows")
            emptied("rows", 2, "rows")
            act.wait_ge(clear, 8)
            root(1, J, 1.0 / CH, eps5)
            for b in range(4):
                move("xT", b, xt[0:64, b * BANK:(b + 1) * BANK], "xT", 64)
            emptied("xT", 4, "xT")
            for b in range(4):
                move("q", b, qt[:, b * BANK:(b + 1) * BANK], "qT")
            emptied("q", 4, "qT")
            act.copy(maskb[:, :], tw["mask"][:, :]).then_inc(masks, 1)
            act.copy(identb[:, :], ident[:, :]).then_inc(masks, 1)
            root(2, 512, 1.0 / 3.0, None)
            filled(act, "kv", 3)
            for b in range(4):
                move("retT", b, xt[0:64, b * BANK:(b + 1) * BANK], "retT", 64)
            emptied("retT", 4, "retT")
            for b in range(2):
                o = filled(act, "proj", b)
                act.activation(ga[:, b * BANK:(b + 1) * BANK], o[:, :], ACT.Gelu).then_inc(ev["ga"], 1)
            emptied("proj", 2, "ga")
            root(3, J, 1.0 / CH, eps5)
            for b in range(4):
                move("x2T", b, xt[0:64, b * BANK:(b + 1) * BANK], "x2T", 64)
            emptied("x2T", 4, "x2T")

            def pair_step(k, u, proj, score, comb):
                u1 = 1 - u

                def inputs():
                    act.wait_ge(lSX, k + 1)
                    act.copy(sxT[:, u, :], bank[0][:, 0:P]).then_inc(lSXe, 1)

                def queries():
                    act.wait_ge(lQ, k + 1)
                    dst = qb[:, u].rearrange("p (i e s) -> p e i s", i=2, e=4)
                    act.copy(dst, bank[1][:, :].rearrange("p (e i s) -> p e i s", e=4, i=2)).then_inc(lQe, 1)

                def exps(i):
                    B = k + (-1)
                    act.wait_ge(lSe, B * 2 + i + 1 + 2)
                    act.activation(ex[:, u1, i, :], ex[:, u1, i, :], ACT.Exp, scale=4.0).then_inc(lE, 1)
                if proj: inputs()
                if score: exps(0)
                if proj: queries()
                if score: exps(1)
            skewed3(act, pair_step)
            for b in range(1, 8, 2):
                o = filled(act, "attT", b)
                act.copy(att_T[:, b * BANK:(b + 1) * BANK], o[:, :]).then_inc(ev["attT"], 1)
            act.wait_ge(ev["attT"], 8)
            for b in range(1, 8, 2):
                act.sem_inc(empty[fills["attT", b][0]], 1)
            act.wait_ge(ev["lg"], 1)
            act.activation(gexp, lg, ACT.Exp).then_inc(ev["gexp"], 1)
            root(4, 64, 1.0 / 16, eps8)
            for b in range(4):
                move("fT", b, xt[0:64, b * BANK:(b + 1) * BANK], "fxT", 64)
            emptied("fT", 4, "fxT")
            root(5, 64, 1.0 / 16, eps8)
            for b in range(4):
                move("foT", b, xt[0:64, b * BANK:(b + 1) * BANK], "foT", 64)
            emptied("foT", 4, "foT")
            act.wait_ge(ev["fl"], 1)
            act.activation(gexp[:, 0:64], lg[:, 0:64], ACT.Exp).then_inc(ev["fexp"], 1)


def constants():
    import numpy as np
    f = np.float64
    y = np.arange(SIDE)
    ky = np.arange(NKY)
    kx = np.concatenate([np.arange(16), np.arange(SIDE - 16, SIDE)])
    ay = 2 * np.pi * np.outer(y, ky) / SIDE
    ax = 2 * np.pi * np.outer(y, kx) / SIDE
    one = np.stack([np.cos(ay), -np.sin(ay)], 1).reshape(SIDE, 2 * NKY)
    fy = np.kron(np.eye(2), one)
    c, s = np.cos(ax), np.sin(ax)
    fx = np.block([[c, -s], [s, c]])
    ix = np.block([[c.T, s.T], [-s.T, c.T]]) / SIDE
    wk = np.where(ky == 0, 1.0, 2.0)[:, None]
    inv = np.concatenate([wk * np.cos(ay.T), -wk * np.sin(ay.T)], 0) / SIDE
    iy = np.kron(np.eye(4), inv)
    avg = np.kron(np.full((2, 2), 0.5), np.eye(CH))
    return {"c_ident": np.eye(P), "c_fy": fy, "c_fx": fx, "c_ix": ix, "c_iy": iy, "c_avg": avg}


def layout(d):
    import numpy as np
    g = lambda k: np.asarray(d[k])
    out = {k: v.astype(np.float32) for k, v in constants().items()}
    out["x"] = np.ascontiguousarray(g("x").reshape(PAIRS, 2, PIX, 3).transpose(0, 1, 3, 2)).reshape(PAIRS, 6, PIX)
    out["fc0_w"] = g("L0_tok_fc0_w")
    two = lambda a: np.concatenate([a, a], 0)
    out["fc0b"] = two(g("L0_tok_fc0_b")[:, None])
    w = np.stack([np.stack([g("L0_tok_w1r"), g("L0_tok_w1i")], 1), np.stack([g("L0_tok_w2r"), g("L0_tok_w2i")], 1)], 1)
    w = w.reshape(LAYERS, 2, 2, CH, CH, 2, CM).transpose(0, 1, 5, 2, 3, 6, 4)
    out["w"] = np.ascontiguousarray(w).reshape(LAYERS * CHUNKS, P, CM, CH)
    out["pw"] = np.ascontiguousarray(g("L0_tok_pw_w").transpose(0, 2, 1))
    v = np.stack([g("L0_tok_pw_b"), g("L0_tok_gamma"), g("L0_tok_beta")], -1)
    out["vecs"] = np.concatenate([v, v], 1)
    out["fc1"] = two(g("L0_tok_fc1_w"))
    out["fc1b"] = g("L0_tok_fc1_b")[:, None]
    out["fc2"] = g("L0_tok_fc2_w")
    out["fc2b"] = np.broadcast_to(g("L0_tok_fc2_b")[:, None], (P, 1))
    a = lambda k: g("L0_attn_" + k)
    wq = a("W_qkv").reshape(16, 3, 4, CH)
    bq = a("b_qkv").reshape(16, 3, 4)
    t = {}
    t["wkv"] = np.concatenate([wq[:, 1:].reshape(P, CH).T, bq[:, 1:].reshape(1, P)], 0)
    q = np.concatenate([wq[:, 0].reshape(CH, CH).T, bq[:, 0].reshape(1, CH)], 0)
    t["wq2"] = np.concatenate([q, q], 1)
    t["wproj"] = np.concatenate([a("W_proj").T, a("b_proj")[None]], 0)
    rep = lambda v: np.broadcast_to(v.reshape(1, -1), (P, v.size))
    t["kvw"] = rep(np.stack([a("kln_w")[:, 0], a("vln_w")[:, 0]], 1))
    t["kvb"] = rep(np.stack([a("kln_b")[:, 0], a("vln_b")[:, 0]], 0))
    hd = np.arange(CH) // 4
    t["bd"] = np.tile((hd[:, None] == hd[None, :]) / CH, (2, 1)).astype(np.float32)
    f = lambda k: g("L0_ffn_" + k)
    z = lambda *s: np.zeros(s, np.float32)
    hl = z(65, 4, 32)
    hl[0:64, :, 0:16] = f("hl_w").transpose(2, 0, 1)
    hl[64, :, 0:16] = f("hl_b")
    t["hlp"] = hl.reshape(65, P)
    w = z(4, 32, 4, 4, 32)
    k_ = z(4, 32, 4, 4, 32)
    v_ = z(4, 32, 2, 2, 16)
    gw = z(2, 2, 4, 16, 4, 4)
    d1, d2 = z(65, 4, 16), z(65, 4, 16)
    for n in range(4):
        w[n, 0:16, :, n, 0:16] = f("wq")[n].transpose(2, 0, 1)
        k_[n, 0:16, n, n, 0:16] = f("wk")[n].T
        v_[n, 0:16, n % 2, n // 2] = f("wv")[n].T
        gw[:, :, n, :, n, :] = f("gate_w")[n].reshape(4, 2, 2, 16).transpose(1, 2, 3, 0)
        d1[16 * n:16 * n + 16, n] = f("fc1_w").T
        d2[16 * n:16 * n + 16, n] = f("fc2_w").T
        d1[64, n], d2[64, n] = f("fc1_b"), f("fc2_b")
    t["wqp"] = w.reshape(P, 4, P)
    t["wkp"] = k_.reshape(P, 4, P)
    t["wvp"] = v_.reshape(P, 2, 32)
    t["gwb"] = gw.reshape(2, P, 16).transpose(1, 0, 2)
    t["gateb"] = rep(f("gate_b"))
    for n, k in (("lng", "ln_g"), ("lnb", "ln_b"), ("fng", "fnorm_g"), ("fnb", "fnorm_b")):
        t[n] = rep(np.tile(f(k), 4))
    t["fc1d"], t["fc2d"] = d1.reshape(65, CH), d2.reshape(65, CH)
    t["fgt"] = f("fgate_w").T
    s = np.arange(SIDE)
    causal = np.where(s[None, :] <= s[:, None], 0.0, -1e30).astype(np.float32)
    t["mask"] = np.tile(causal, (2, 8))
    for k, v in t.items():
        assert list(v.shape) == TAIL_W[k], (k, v.shape)
        out["t_" + k] = v
    return {k: np.ascontiguousarray(a) for k, a in out.items()}


def kernel(**inputs):
    import concourse.bacc as bacc
    import numpy as np
    from concourse.bass_utils import run_bass_kernel_spmd

    arrays = layout(inputs)
    nc = bacc.Bacc("TRN2", target_bir_lowering=False, num_devices=1)
    io = {n: nc.dram_tensor("in_" + n, a.shape, F32, kind="ExternalInput").ap() for n, a in arrays.items()}
    io["out"] = nc.dram_tensor("out", [BATCH * SIDE * SIDE], F32, kind="ExternalOutput").ap()
    tower_kernel(nc, io)
    r = run_bass_kernel_spmd(nc, [{"in_" + n: a for n, a in arrays.items()}], core_ids=[0])
    return np.asarray(r.results[0]["out"]).reshape(BATCH, SIDE, SIDE)
```

```python
from contextlib import ExitStack

import concourse.bass as bass
from concourse import mybir

F32 = mybir.dt.float32
ALU = mybir.AluOpType
ACT = mybir.ActivationFunctionType
AX = mybir.AxisListType

P = 128
BATCH, SIDE, CH = 32, 64, 64
PAIRS = BATCH // 2
PIX = SIDE * SIDE
LAYERS = 4
NKX, NKY = 32, 16
CHUNKS = 4
CM = NKX * NKY // CHUNKS
HM = CM // 2
BANK = 512
BN_EPS = 1e-5
HID = 128


TAIL_W = {"wkv": [65, P], "wq2": [65, P], "wproj": [65, CH], "hlp": [65, P], "wqp": [P, 4, P], "wkp": [P, 4, P], "wvp": [P, 2, 32],
          "gwb": [P, 2, 16], "gateb": [P, 16], "kvw": [P, P], "kvb": [P, P], "bd": [P, CH], "lng": [P, CH], "lnb": [P, CH],
          "fng": [P, CH], "fnb": [P, CH], "fc1d": [65, CH], "fc2d": [65, CH], "fgt": [CH, 4], "mask": [P, BANK]}


def tower_kernel(nc, io):
    ctx = ExitStack()
    with ctx:
        def sb(name, shape, dt=F32):
            return ctx.enter_context(nc.sbuf_tensor(name, shape, dt))

        def sem(name):
            return ctx.enter_context(nc.semaphore(name))

        def sems(name):
            return [sem(f"{name}{u}") for u in range(2)]

        field = nc.dram_tensor("field", [PAIRS, P, PIX], F32, kind="Internal").ap()
        colour_modes = nc.dram_tensor("colour_modes", [96, 1024], F32, kind="Internal").ap()
        xmodes = nc.dram_tensor("xmodes", [CHUNKS, 2, BATCH, CH, CM], F32, kind="Internal").ap()
        zmodes = nc.dram_tensor("zmodes", [2, NKX, NKY, BATCH, CH], F32, kind="Internal").ap()

        big = sb("big", [P, 4, PIX])
        ytile = big[:, 0:2, :]
        htile = big[:, 2:4, :]
        xin = big[:, :, :].rearrange("p (u v) (b m) -> p u v b m", u=2, b=BATCH)
        wt = sb("wt", [P, 2, CM, CH])
        work = sb("work", [P, 2 * PIX])
        ht = work[:, 0:PIX].rearrange("p (t c) -> p t c", c=P)
        atile = work[:, PIX:2 * PIX].rearrange("p (u ky rx) -> p u ky rx", u=2, ky=NKY)
        zout = work[:, :].rearrange("p (u m o) -> p u m o", u=2, o=CH)
        gtile = work[:, 0:2048].rearrange("p (x r k) -> p x r k", r=2, k=NKY)
        gt = work[:, PIX:2 * PIX].rearrange("p (u q c) -> p u q c", u=2, c=P)
        att_t = sb("att_t", [P, NKY, P])
        zin_all = sb("zin", [P, 2 * NKY * P])
        zin = zin_all[0:64, :].rearrange("p (u k c) -> p u k c", u=2, k=NKY)
        xout = sb("xout", [P, 2, CHUNKS, 2, CM])
        ident = sb("ident", [P, P])
        fy = sb("fy", [P, 64])
        fx = sb("fx", [P, 64])
        ix = sb("ix", [64, P])
        iy = sb("iy", [P, 256])
        avg = sb("avg", [P, P])
        pw = sb("pw", [P, P])
        vecs = sb("vecs", [P, 3])
        fc0 = sb("fc0", [P, P])
        fc0t = sb("fc0t", [P, 7])
        pw0 = sb("pw0", [P, P])
        fc1 = sb("fc1", [P, 2, P])
        fc1b = sb("fc1b", [P, 2])
        fc2 = sb("fc2", [P, 2, 32])
        fc2b = sb("fc2b", [P, 1])
        stats = sb("stats", [P, PAIRS * 8, 6])
        mv = sb("mv", [P, 2])
        sm = sb("sm", [P, 8])
        bn_scale = sb("bn_scale", [P, 1])
        bn_bias = sb("bn_bias", [P, 1])
        epst = sb("epst", [P, 1])
        scratch = sb("scratch", [P, 1024])
        yout = wt[:, :, :, :].rearrange("p u m o -> p (u m o)")[:, 0:2 * PIX].rearrange("p (u n) -> p u n", u=2)
        xs = work[:, 0:32 * 96].rearrange("p (t c) -> p t c", c=96)
        xq = big[:, :, :].rearrange("p a (b m) -> p (a b) m", m=1024)
        hidden = work[:, :].rearrange("p (r n) -> p r n", n=BANK)
        towr = att_t[:, :, :].rearrange("p (u q n) c -> p u q (n c)", u=2, q=2)

        free = {"big": 0, "wt": 0}
        pools = {"big": big[:, :, :].rearrange("p a b -> p (a b)"), "wt": wt[:, :, :, :].rearrange("p a b c -> p (a b c)")}

        def view(n, where="big", parts=P):
            at = free[where]
            free[where] += n
            assert free[where] <= 4 * PIX
            return pools[where][0:parts, at:at + n]

        J = PAIRS
        TD = J * CH
        h1t = nc.dram_tensor("h1_rows", [BATCH * SIDE * SIDE], F32, kind="Internal").ap()
        h1 = view(TD); xn = view(TD); xc = view(2 * TD); sq = view(2 * TD)
        kv = view(2 * TD); kn = view(TD); vn = view(TD); kvm = view(TD); ret = view(TD); ga = view(TD)
        h2 = view(TD); sx = view(TD)
        xt = view(2048, "wt", 65); qt = view(2048, "wt"); att_out = view(4 * TD, "wt"); att_T = view(4096, "wt")
        s1 = view(512, "wt"); s2 = view(512, "wt"); sd = view(512, "wt")
        prod = sq; mixed = kn; fxt = view(TD, "wt"); hx = ga; fo = view(TD, "wt")
        x2 = xn
        lg = s1[:, 0:256]; gmax = s2[:, 0:64]; gexp = sd[:, 0:256]; gsum = s2[:, 64:128]
        res = sb("res", [P, CH]); keep = scratch[:, :]
        keepT = qt[0:64, :]
        sxT = work[:, 0:256].rearrange("p (u t) -> p u t", u=2)
        qb = work[:, 256:1280].rearrange("p (u t) -> p u t", u=2)
        kb = work[:, 1280:2304].rearrange("p (u t) -> p u t", u=2)
        vb = work[:, 2304:2304 + 2 * 136].rearrange("p (u i q h o) -> p u i q h o", u=2, i=2, q=2, h=2)
        ex = work[:, 2576:2576 + 2048].rearrange("p (u i t) -> p u i t", u=2, i=2)
        exT = work[:, 4624:4624 + 1024].rearrange("p (i t) -> p i t", i=2)
        mx = work[:, 5648:5680].rearrange("p (u i g) -> p u i g", u=2, i=2)
        rden = work[:, 5680:5712].rearrange("p (u g) -> p u g", u=2)
        tw = {}
        at = 0
        for name, shape in TAIL_W.items():
            n = shape[1] * (shape[2] if len(shape) == 3 else 1)
            tw[name] = zin_all[0:shape[0], at:at + n]
            if len(shape) == 3:
                tw[name] = tw[name].rearrange("p (a b) -> p a b", a=shape[1])
            at += n
        maskb = sb("maskb", [P, BANK], mybir.dt.bfloat16)
        identb = sb("identb", [P, P], mybir.dt.bfloat16)
        eps5 = sb("eps5", [P, 1])
        eps8 = sb("eps8", [P, 1])
        zero1 = sb("zero1", [P, 1])

        fills = {}
        nth = [0] * 8
        for name, banks in (("xT", (0, 1, 2, 3)), ("q", (4, 5, 6, 7)), ("kv", (0, 1, 2, 3)), ("kvm", (4, 5)),
                            ("out", (6, 7)), ("retT", (0, 1, 2, 3)), ("proj", (4, 5)), ("x2T", (0, 1, 2, 3)),
                            ("attT", (0, 1, 2, 3, 4, 5, 6, 7)), ("gate", (0,)), ("fT", (4, 5, 6, 7)), ("fc1", (0, 1, 2, 3)),
                            ("fc2", (4, 5)), ("foT", (0, 1, 2, 3)), ("fg", (4,))):
            for i, b in enumerate(banks):
                fills[name, i] = (b, nth[b])
                nth[b] += 1

        bank = [ctx.enter_context(nc.psum_tensor(f"bank{i}", [P, BANK], F32)) for i in range(8)]

        phase = sem("phase")
        carrier = sem("carrier")
        cst = sem("cst")
        par = sem("par")
        zero_done = sem("zero_done")
        xsld = sem("xsld"); zY = sem("zY"); zYe = sem("zYe"); zR = sem("zR"); zRe = sem("zRe"); zM = sem("zM"); zMe = sem("zMe")
        lift_clear = sem("lift_clear"); cmst = sem("cmst"); xqld = sem("xqld"); zX = sem("zX"); zXe = sem("zXe"); zSt = sems("zSt"); pw0_f = sem("pw0_f"); pw0_e = sem("pw0_e")
        hclear = sem("hclear"); bXld = sems("bXld")
        yld = sems("yld"); aG = sem("aG"); aT = sem("aT"); aTe = sem("aTe")
        aY = sem("aY"); aYe = sem("aYe"); aR = sem("aR"); aRe = sem("aRe")
        aX = sem("aX"); aXe = sem("aXe"); aXst = sems("aXst")
        wld = [sems("wld0_"), sems("wld1_")]; mXld = sems("mXld"); mNeg = sem("mNeg"); mCp = sem("mCp"); mM = sem("mM")
        mE = sems("mE"); mZst = sems("mZst")
        bZld = sems("bZld"); bG = sem("bG"); bK = sem("bK"); bKe = sem("bKe")
        bT = sem("bT"); bTe = sem("bTe"); bF = sem("bF"); bFe = sem("bFe"); bS = sem("bS")
        bYst = sems("bYst")
        stv = sem("stv"); stp = sem("stp"); sta = sem("sta")
        fG = sem("fG"); fC = sem("fC"); fCe = sem("fCe"); fO = sem("fO"); fOe = sem("fOe")
        fSt = sems("fSt"); fFree = sem("fFree"); h1_st = sem("h1_st")

        full = [sem(f"full{b}") for b in range(8)]
        empty = [sem(f"empty{b}") for b in range(8)]
        twl = sem("twl"); chain = sem("chain"); h1_ld = sem("h1_ld"); out_st = sem("out_st")
        clear = sem("clear"); masks = sem("masks")
        ev = {n: sem("ev_" + n) for n in (
            "rows", "xn", "var", "rstd", "xT", "qT", "kn", "kvm", "ret", "retT", "ga", "x2", "x2T", "att", "attT", "lg", "gexp",
            "fx", "fxT", "hx", "fo", "foT", "fl", "fexp", "done")}
        lSX = sem("lSX"); lSXe = sem("lSXe"); lQ = sem("lQ"); lQe = sem("lQe"); lK = sem("lK"); lKe = sem("lKe")
        lV = sem("lV"); lVe = sem("lVe"); lS = sem("lS"); lSe = sem("lSe"); lE = sem("lE"); lT = sem("lT"); lTe = sem("lTe")
        lO = sem("lO"); lOe = sem("lOe"); lMx = sem("lMx"); lRd = sem("lRd")

        def filled(eng, name, i):
            b, n = fills[name, i]
            eng.wait_ge(full[b], n + 1)
            return bank[b]

        def to_fill(name, i):
            b, n = fills[name, i]
            if n:
                nc.tensor.wait_ge(empty[b], n)
            return bank[b]

        def skewed3(eng, step):
            step(0, 0, True, False, False)
            step(1, 1, True, True, False)
            with eng.Fori(0, J // 2 - 1) as i:
                step(i * 2 + 2, 0, True, True, True)
                step(i * 2 + 3, 1, True, True, True)
            step(J, 0, False, True, True)
            step(J + 1, 1, False, False, True)

        NCONST = 12
        NPH = 3

        def apart(eng):
            eng.sem_inc(carrier, 1)

        def barrier(eng, k):
            apart(eng)
            eng.drain().then_inc(phase, 1)
            eng.wait_ge(phase, k * 5)
            apart(eng)

        def skewed(eng, step):
            step(0, 0, True, False, True)
            with eng.Fori(0, PAIRS // 2 - 1) as i:
                step(i * 2 + 1, 1, True, True, True)
                step(i * 2 + 2, 0, True, True, True)
            step(PAIRS - 1, 1, True, True, False)
            step(PAIRS, 0, False, True, False)

        def pairs(eng, body, n=PAIRS):
            with eng.Fori(0, n // 2) as i:
                for u in range(2):
                    body(i * 2 + u, u, i)

        def later_pairs(eng, body):
            with eng.Fori(0, PAIRS // 2 - 1) as i:
                for u in range(2):
                    body(i * 2 + (2 + u), u, i)

        block = ctx.enter_context(nc.Block())

        @block.sync
        def _(sp):
            sp.dma_start(xs, io["xs"]).then_inc(xsld, 16)
            for dst, src in ((ident, "c_ident"), (fy, "c_fy"), (fx, "c_fx"), (ix, "c_ix"), (iy, "c_iy"), (avg, "c_avg"),
                             (fc1b, "fc1b"), (fc2b, "fc2b"), (fc0t, "fc0t")):
                sp.dma_start(dst[:, :], io[src]).then_inc(cst, 16)
            for dst, src in ((fc1, "fc1"), (fc2, "fc2")):
                sp.dma_start(dst[:, :, :], io[src]).then_inc(cst, 16)
            sp.wait_ge(lift_clear, 2)
            sp.dma_start(fc0[0:7, :], io["fc0"]).then_inc(cst, 16)
            sp.dma_start(xq[6:7, :, :], io["dc"]).then_inc(xqld, 16)

            barrier(sp, 1)
            sp.dma_start(xq[0:6, :, :], colour_modes.rearrange("(n q) m -> q n m", q=6)).then_inc(xqld, 16)
            barrier(sp, 2)

            def load_field(n, u):
                apart(sp)
                sp.dma_start(ytile[:, u, :], field[bass.ds(n, 1)].rearrange("a p m -> p (a m)")).then_inc(yld[u], 16)

            def forward_loads(m):
                def load_y(n, u, i):
                    sp.wait_ge(aG, (m * PAIRS + n) * 4 + 4)
                    load_field(n, u)
                later_pairs(sp, load_y)
                barrier(sp, m * NPH + 5)

            def layer(l, m):
                def load_modes(g, u, i):
                    G = l * CHUNKS + g
                    sp.wait_ge(mM, G * 8 + 8)
                    apart(sp)
                    for half, v in ((0, 1), (1, 0)):
                        src = xmodes[bass.ds(g, 1), v].rearrange("a b c m -> c (a b) m")
                        sp.dma_start(xin[CH * half:CH * half + CH, u, 1], src).then_inc(mXld[u], 16)
                pairs(sp, load_modes, CHUNKS)
                for s in range(2):
                    sp.dma_start(pw[CH * s:CH * s + CH, CH * s:CH * s + CH], io["pw"][bass.ds(l, 1)].rearrange("a i o -> (a i) o")).then_inc(par, 16)
                sp.dma_start(vecs[:, :], io["vecs"][bass.ds(l, 1)].rearrange("a p k -> (a p) k")).then_inc(par, 16)
                if m is not None:
                    sp.wait_ge(mM, (l * CHUNKS + 2) * 8 + 8 + 16)
                    for u in range(2):
                        load_field(u, u)
                barrier(sp, l * NPH + 3)
                def load_modes_back(n, u):
                    sp.wait_ge(bK, (l * PAIRS + n) * 4 + 4)
                    apart(sp)
                    for v in range(2):
                        zs = zmodes[v, :, :, bass.ds(n * 2, 2), :].rearrange("k y b o -> k y (b o)")
                        sp.dma_start(zin[NKX * v:NKX * v + NKX, u], zs).then_inc(bZld[u], 16)

                def load_x(n, u):
                    sp.wait_ge(bF, (l * PAIRS + n) * 8 + 8)
                    apart(sp)
                    sp.dma_start(htile[0:7, u, :], io["x"][bass.ds(n, 1)].rearrange("a p m -> p (a m)")).then_inc(bXld[u], 16)

                for u in range(2):
                    load_modes_back(u, u)
                if m is None:
                    sp.wait_ge(hclear, 1)
                    for u in range(2):
                        load_x(u, u)

                def load_back(n, u, i):
                    load_modes_back(n, u)
                    if m is None:
                        load_x(n, u)
                    else:
                        sp.wait_ge(bG, m * PAIRS + n + 1)
                        load_field(n, u)
                later_pairs(sp, load_back)
                if m is not None:
                    sp.wait_ge(bG, m * PAIRS + PAIRS + 2)
                for u in range(2):
                    sp.wait_ge(bYst[u], l * 8 * PAIRS + 32)
                    load_field(u, u)
                barrier(sp, l * NPH + 4)

            layer(0, None)
            with sp.Fori(0, LAYERS - 1) as m:
                forward_loads(m)
                layer(m + 1, m)

            def load_last(n, u, i):
                sp.wait_ge(fG, n + 1)
                load_field(n, u)
            later_pairs(sp, load_last)
            barrier(sp, LAYERS * NPH + 2)
            for name in TAIL_W:
                sp.dma_start(tw[name], io["t_" + name]).then_inc(twl, 16)
            sp.wait_ge(h1_st, 1)
            sp.dma_start(h1.rearrange("p (j c) -> p j c", j=J), h1t.rearrange("(j p c) -> p j c", j=J, p=P)).then_inc(h1_ld, 16)
            sp.wait_ge(ev["done"], 1)
            sp.dma_start(io["out"].rearrange("(j p c) -> p j c", j=J, p=P), h2.rearrange("p (j c) -> p j c", j=J)).then_inc(out_st, 16)
            sp.wait_ge(out_st, 16)

        @block.gpsimd
        def _(pool):
            nc.gpsimd.memset(fc0[:, :], 0.0).then_inc(lift_clear, 1)
            nc.gpsimd.memset(pw0[:, :], 0.0).then_inc(zero_done, 1)
            nc.gpsimd.memset(pw[:, :], 0.0)
            nc.gpsimd.memset(epst[:, :], BN_EPS)
            def load_w(l, g, u, h, ahead):
                G = l * CHUNKS + g
                if not ahead:
                    pool.wait_ge(mM, G * 8 + 4 + 4 * h)
                    apart(pool)
                dst = wt[:, u, HM * h:HM * h + HM]
                pool.dma_start(dst, io["w"][bass.ds(G, 1), :, HM * h:HM * h + HM].rearrange("a p m o -> (a p) m o")).then_inc(wld[u][h], 16)

            def layer(l):
                for u in range(2):
                    for h in range(2):
                        load_w(l, 2 + u, u, h, False)
                barrier(pool, l * NPH + 3)
                barrier(pool, l * NPH + 4)
            barrier(pool, 1)
            for u in range(2):
                for h in range(2):
                    load_w(0, u, u, h, True)
            barrier(pool, 2)
            layer(0)
            with pool.Fori(0, LAYERS - 1) as m:
                for u in range(2):
                    for h in range(2):
                        pool.wait_ge(aG, (m * PAIRS + 2 * u + h + 1) * 4 + 8)
                        apart(pool)
                        load_w(m + 1, u, u, h, True)
                barrier(pool, m * NPH + 5)
                layer(m + 1)

            def store_tower(n, u, i):
                pool.wait_ge(fOe, n * 2 + 2 + 4)
                apart(pool)
                for s in range(2):
                    dst = h1t[bass.ds(n * 8192 + s * PIX, PIX)].rearrange("(q i m) -> i q m", q=2, i=4)
                    pool.dma_start(dst, towr[s:s + 97:32, u]).then_inc(fSt[u], 16)
                pool.wait_ge(fSt[u], i * 32 + 32)
                pool.sem_inc(fFree, 1)
            pool.sem_inc(fFree, 2)
            pairs(pool, store_tower)
            pool.sem_inc(h1_st, 1)
            barrier(pool, LAYERS * NPH + 2)
            n_clear = 0
            for dst, value in [(vb.rearrange("p u i q h o -> p (u i q h o)"), 0.0), (xt[64:65, :], 1.0), (eps5[:, :], 1e-5), (eps8[:, :], 1e-8)] + [
                    (vb[64 * h:64 * h + 64, u, :, :, h, 16:17].rearrange("p i q o -> p (i q) o"), 1.0) for h in range(2) for u in range(2)]:
                nc.gpsimd.memset(dst, value).then_inc(clear, 1)
                n_clear += 1
                pool.wait_ge(clear, n_clear)

        @block.tensor
        def _(pe):
            pe.sem_inc(aT, 16)
            pe.sem_inc(mM, 16)
            pe.sem_inc(bK, 8)
            pe.sem_inc(bF, 16)
            pe.sem_inc(fO, 2)
            pe.wait_ge(cst, 16 * NCONST)

            pe.wait_ge(xsld, 16)
            for g in range(4):
                for t in range(8):
                    mm = pe.matmul(bank[g][0:96, t * 64:(t + 1) * 64], xs[:, 8 * g + t, :], fy[:, :], start=True, stop=True)
                mm.then_inc(zY, 1)
            pe.wait_ge(zYe, 4)
            for j in range(4):
                for t in range(4):
                    mm = pe.transpose(bank[4 + j][:, t * P:t * P + 96], atile[0:96, 0, 4 * j + t, :], ident[0:96, 0:96])
                mm.then_inc(zR, 1)
            for g in range(2):
                pe.wait_ge(zRe, 2 * g + 2)
                for t in range(8):
                    mm = pe.matmul(bank[g][0:96, t * 64:(t + 1) * 64], att_t[:, 8 * g + t, 0:96], fx[:, :], start=True, stop=True)
                mm.then_inc(zM, 1)
            barrier(pe, 1)

            pe.wait_ge(xqld, 32)

            def lift(n, u, i):
                for g in range(2):
                    pe.wait_ge(zXe, n * 2 + g + 1)
                    pe.matmul(bank[2 * u + g][:, :], fc0[:, :], xq[:, bass.ds(n, 1), g * BANK:(g + 1) * BANK].rearrange("p a m -> p (a m)"),
                              start=True, stop=True).then_inc(zX, 1)
            pairs(pe, lift)
            barrier(pe, 2)

            def forward(m):
                def fwd(k, u, front, back, ahead):
                    N = m * PAIRS + k
                    B = N + (-1)
                    ub = 1 - u

                    def T(j):
                        pe.wait_ge(aTe, N * 8 + j + 1)
                        if j % 2 == 0:
                            pe.wait_ge(aG, N * 4 + j // 2 + 1 + 8)
                        for t in range(4):
                            s = 4 * j + t
                            mm = pe.transpose(bank[j % 2][:, t * P:(t + 1) * P], htile[:, u, s * P:(s + 1) * P], ident[:, :])
                        mm.then_inc(aT, 1)

                    def Y(g):
                        pe.wait_ge(aTe, N * 8 + 2 * g + 4)
                        pe.wait_ge(aYe, N * 4 + g + 1)
                        for t in range(8):
                            mm = pe.matmul(bank[2 + g % 2][:, t * 64:(t + 1) * 64], ht[:, 8 * g + t, :], fy[:, :], start=True, stop=True)
                        mm.then_inc(aY, 1)

                    def R(j):
                        if j == 0:
                            pe.wait_ge(aYe, B * 4 + 6)
                        pe.wait_ge(aRe, B * 4 + j + 1)
                        for t in range(4):
                            mm = pe.transpose(bank[4 + j % 2][:, t * P:(t + 1) * P], atile[:, ub, 4 * j + t, :], ident[:, :])
                        mm.then_inc(aR, 1)

                    def X(g):
                        pe.wait_ge(aRe, B * 4 + 2 * g + 4)
                        pe.wait_ge(aXe, B * 2 + g + 1)
                        for t in range(8):
                            mm = pe.matmul(bank[6 + g][:, t * 64:(t + 1) * 64], att_t[:, 8 * g + t, :], fx[:, :], start=True, stop=True)
                        mm.then_inc(aX, 1)

                    if front:
                        T(0); T(1); T(2); T(3)
                    if back:
                        R(0); R(1)
                    if front:
                        Y(0); T(4); T(5)
                    if back:
                        R(2); R(3)
                    if front:
                        Y(1); T(6); T(7)
                    if back:
                        X(0)
                    if front:
                        Y(2)
                    if back:
                        X(1)
                    if front:
                        Y(3)
                skewed(pe, fwd)
                barrier(pe, m * NPH + 5)

            def layer(l, m):
                def mix(g, u, i):
                    G = l * CHUNKS + g
                    M = l * (CHUNKS // 2) + i
                    pe.wait_ge(wld[u][0], M * 16 + 16)
                    pe.wait_ge(mNeg, G + 1)
                    pe.wait_ge(mCp, G + 1)
                    for k in range(8):
                        if k == 4:
                            pe.wait_ge(wld[u][1], M * 16 + 16)
                        pe.wait_ge(mE[k % 2], G * 4 + k // 2 + 1)
                        for t in range(8):
                            for par_ in range(2):
                                y0 = 2 * (8 * k + t) % 16 + par_
                                x0 = (8 * k + t) // 8
                                mm = pe.matmul(bank[k][64 * par_:64 * par_ + 64, t * 64:(t + 1) * 64],
                                               xin[:, u, :, :, y0 * 8 + x0], wt[:, u, x0 * 16 + y0, :], start=True, stop=True)
                        mm.then_inc(mM, 1)
                pairs(pe, mix, CHUNKS)
                barrier(pe, l * NPH + 3)
                pe.wait_ge(par, l * 48 + 48)
                apart(pe)
                if m is None:
                    pe.wait_ge(zero_done, 1)
                    pe.matmul(bank[0][0:7, 0:P], fc0t[:, :], pw[:, :], start=True, stop=True).then_inc(pw0_f, 1)
                    pe.wait_ge(pw0_e, 1)

                def inv(k, u, front, back, ahead):
                    N = l * PAIRS + k
                    B = N + (-1)
                    ub = 1 - u

                    def K(j):
                        if j == 0:
                            pe.wait_ge(bZld[u], zcount(l, k, u))
                        pe.wait_ge(bKe, N * 4 + j + 1)
                        for t in range(4):
                            mm = pe.matmul(bank[j % 2][:, t * P:(t + 1) * P], zin[:, u, 4 * j + t, :], ix[:, :], start=True, stop=True)
                        mm.then_inc(bK, 1)

                    def T(j):
                        if j == 0:
                            pe.wait_ge(bKe, N * 4 + 6)
                        pe.wait_ge(bTe, N * 4 + j + 1)
                        for t in range(4):
                            q = 4 * j + t
                            mm = pe.transpose(bank[2 + j % 2][:, t * P:(t + 1) * P],
                                              gtile[:, 4 * q:4 * q + 4].rearrange("p x r k -> p (x r k)"), ident[:, :])
                        mm.then_inc(bT, 1)

                    def F(f):
                        if f == 0:
                            if m is None:
                                pe.wait_ge(bXld[ub], (k + (-1) - ub) * 8 + 16)
                            else:
                                pe.wait_ge(bG, m * PAIRS + k + 2)
                            pe.wait_ge(bTe, B * 4 + 6)
                        pe.wait_ge(bFe, B * 8 + f + 1)
                        o = bank[4 + f % 4]
                        pe.matmul(o[:, :], (pw0 if m is None else pw)[:, :], htile[:, ub, f * BANK:(f + 1) * BANK], start=True, stop=True)
                        for t in range(2):
                            mm = pe.matmul(o[:, t * 256:(t + 1) * 256], gt[:, ub, 2 * f + t, :], iy[:, :], start=False, stop=True,
                                           skip_group_check=True)
                        mm.then_inc(bF, 1)

                    if back:
                        F(0)
                    if front:
                        K(0); K(1)
                    if back:
                        F(1)
                    if front:
                        K(2); K(3)
                    if back:
                        F(2)
                    if front:
                        T(0); T(1)
                    if back:
                        F(3); F(4)
                    if front:
                        T(2); T(3)
                    if back:
                        F(5); F(6); F(7)
                skewed(pe, inv)
                pe.wait_ge(stv, l * 8 + 2)
                pe.matmul(bank[0][:, 0:1], avg[:, :], mv[:, 0:1], start=True, stop=True).then_inc(stp, 1)
                pe.wait_ge(stv, l * 8 + 5)
                pe.matmul(bank[0][:, 1:2], avg[:, :], sm[:, 3:4], start=True, stop=True).then_inc(stp, 1)
                barrier(pe, l * NPH + 4)

            def zcount(l, k, u):
                return (l * PAIRS + k - u) * 16 + 32
            layer(0, None)
            with pe.Fori(0, LAYERS - 1) as m:
                forward(m)
                layer(m + 1, m)

            def last(k, u, front, back, ahead):
                def C(r):
                    pe.wait_ge(fCe, k * 16 + r + 1)
                    c, half = r // 2, r % 2
                    pe.matmul(bank[r % 4][:, :], fc1[:, half, :], htile[:, u, c * BANK:(c + 1) * BANK], start=True, stop=True).then_inc(fC, 1)

                def O(n, un, q):
                    pe.wait_ge(fCe, n * 16 + 8 * q + 8 + 4)
                    pe.wait_ge(fOe, n * 2 + q + 1)
                    for half in range(2):
                        for i in range(4):
                            mm = pe.matmul(bank[4 + 2 * un + q][32 * i:32 * i + 32, :], fc2[:, half, :], hidden[:, (4 * q + i) * 2 + half, :],
                                           start=(half == 0), stop=(half == 1), skip_group_check=True)
                    mm.then_inc(fO, 1)
                if front:
                    pe.wait_ge(fG, k + 3)
                    for r in range(4):
                        C(r)
                if back:
                    O(k + (-1), 1 - u, 1)
                if front:
                    for r in range(4, 12):
                        C(r)
                    O(k, u, 0)
                    for r in range(12, 16):
                        C(r)
            skewed(pe, last)
            barrier(pe, LAYERS * NPH + 2)

            def stage_T(name, src, cols=CH):
                for j in range(src.shape[1] // cols):
                    b = j // 4
                    o = to_fill(name, b) if j % 4 == 0 else bank[fills[name, b][0]]
                    mm = pe.transpose(o[0:cols, (j % 4) * P:(j % 4 + 1) * P], src[:, j * cols:(j + 1) * cols], ident[:, :])
                    if j % 4 == 3:
                        mm.then_inc(full[fills[name, b][0]], 1)

            def stage_W(name, w, src, n, k):
                per = min(BANK // n, J)
                for j in range(J):
                    b = j // per
                    o = to_fill(name, b) if j % per == 0 else bank[fills[name, b][0]]
                    mm = pe.matmul(o[:, (j % per) * n:(j % per + 1) * n], src[0:k, j * P:(j + 1) * P], w, start=True, stop=True)
                    if j % per == per - 1:
                        mm.then_inc(full[fills[name, b][0]], 1)

            def stage_F(name, w, src, m):
                for b in range(4):
                    o = to_fill(name, b)
                    pe.matmul(o[0:m, :], w, src[:, b * BANK:(b + 1) * BANK], start=True, stop=True).then_inc(full[fills[name, b][0]], 1)

            pe.wait_ge(twl, 16 * len(TAIL_W))
            pe.wait_ge(ev["xn"], 1)
            stage_T("xT", xn)
            pe.wait_ge(clear, 8)
            pe.wait_ge(ev["xT"], 4)
            stage_F("q", tw["wq2"][:, :], xt[:, :], P)
            stage_W("kv", tw["wkv"][:, :], xt, P, 65)
            pe.wait_ge(ev["kn"], 1)
            for j in range(J):
                o = to_fill("kvm", j // 8) if j % 8 == 0 else bank[fills["kvm", j // 8][0]]
                for i in range(2):
                    half = slice(64 * i, 64 * i + 64)
                    mm = pe.matmul(o[half, (j % 8) * CH:(j % 8 + 1) * CH], kn[half, j * CH:(j + 1) * CH], vn[half, j * CH:(j + 1) * CH],
                                   start=True, stop=True)
                if j % 8 == 7:
                    mm.then_inc(full[fills["kvm", j // 8][0]], 1)
            pe.wait_ge(ev["qT"], 4)
            pe.wait_ge(ev["kvm"], 2)
            for j in range(J):
                o = to_fill("out", j // 8) if j % 8 == 0 else bank[fills["out", j // 8][0]]
                for i in range(2):
                    half = slice(64 * i, 64 * i + 64)
                    mm = pe.matmul(o[half, (j % 8) * CH:(j % 8 + 1) * CH], qt[half, j * P + 64 * i:j * P + 64 * i + 64],
                                   kvm[half, j * CH:(j + 1) * CH], start=True, stop=True)
                if j % 8 == 7:
                    mm.then_inc(full[fills["out", j // 8][0]], 1)
            pe.wait_ge(ev["ret"], 1)
            stage_T("retT", ret)
            pe.wait_ge(ev["retT"], 4)
            stage_W("proj", tw["wproj"][:, :], xt, CH, 65)
            pe.wait_ge(ev["x2"], 1)
            stage_T("x2T", x2)
            pe.wait_ge(ev["x2T"], 4)
            pe.wait_ge(ev["ga"], 2)
            pe.wait_ge(masks, 2)

            def pair_step(k, u, proj, score, comb):
                u1 = 1 - u

                def project():
                    pe.wait_ge(lSXe, k + 1)
                    pe.matmul(bank[0][:, 0:P], tw["hlp"][:, :], xt[:, bass.ds(k * P, P)], start=True, stop=True).then_inc(lSX, 1)

                def project2():
                    pe.wait_ge(lSXe, k + 2)
                    pe.wait_ge(lQe, k + 1)
                    for e in range(4):
                        mm = pe.matmul(bank[1][:, e * P:(e + 1) * P], tw["wqp"][:, e, :], sxT[:, u, :], start=True, stop=True)
                    mm.then_inc(lQ, 1)
                    pe.wait_ge(lKe, k + 1)
                    for n in range(4):
                        mm = pe.matmul(bank[2][:, n * P:(n + 1) * P], tw["wkp"][:, n, :], sxT[:, u, :], start=True, stop=True)
                    mm.then_inc(lK, 1)
                    pe.wait_ge(lVe, k + 1)
                    for i in range(2):
                        for h in range(2):
                            pe.matmul(bank[3][64 * h:64 * h + 64, i * 32:(i + 1) * 32], sxT[:, u, 64 * i:64 * i + 64], tw["wvp"][:, h, :],
                                      start=True, stop=True)
                    pe.transpose(bank[3][:, P:2 * P], sxT[:, u, :], ident[:, :]).then_inc(lV, 1)

                def scores(i):
                    B = k + (-1)
                    if i == 0:
                        pe.wait_ge(lQe, B + 2)
                        pe.wait_ge(lKe, B + 2)
                    pe.wait_ge(lSe, B * 2 + i + 1)
                    o = bank[4 + i]
                    pe.matmul(o[:, :], identb[:, :], maskb[:, :], start=True, stop=True)
                    for q in range(2):
                        mm = pe.matmul(o[:, q * 256:(q + 1) * 256], qb[:, u1, i * 256 + q * P:i * 256 + (q + 1) * P],
                                       kb[:, u1, i * 256:(i + 1) * 256], start=False, stop=True, skip_group_check=True)
                    mm.then_inc(lS, 1)

                def turn(i):
                    C = k + (-2)
                    pe.wait_ge(lE, C * 2 + i + 1)
                    pe.wait_ge(lTe, C * 2 + i + 1)
                    for q in range(4):
                        mm = pe.transpose(bank[6][:, q * P:(q + 1) * P], ex[:, u, i, q * P:(q + 1) * P], ident[:, :])
                    mm.then_inc(lT, 1)

                def combine(i):
                    C = k + (-2)
                    pe.wait_ge(lTe, C * 2 + i + 2)
                    if i == 0:
                        pe.wait_ge(lVe, C + 2)
                        pe.wait_ge(lOe, C + 1)
                    for e2 in range(2):
                        for q in range(2):
                            for h in range(2):
                                at = ((e2 * 2 + q) * 2 + h) * 34
                                mm = pe.matmul(bank[7][64 * i:64 * i + 64, at:at + 34],
                                               exT[:, i, (q * 2 + h) * P + 64 * e2:(q * 2 + h) * P + 64 * e2 + 64],
                                               vb[:, u, i, h].rearrange("p h o -> p (h o)"), start=True, stop=True)
                    if i == 1:
                        mm.then_inc(lO, 1)
                if proj: project()
                if comb: turn(0)
                if score: scores(0)
                if proj: project2()
                if comb: combine(0); turn(1)
                if score: scores(1)
                if comb: combine(1)
            skewed3(pe, pair_step)

            pe.wait_ge(ev["att"], 1)
            stage_T("attT", att_out, P)
            pe.wait_ge(ev["attT"], 8)
            o = to_fill("gate", 0)
            for j in range(J):
                for h in range(2):
                    mm = pe.matmul(o[:, j * 16:(j + 1) * 16], att_T[:, (2 * j + h) * P:(2 * j + h + 1) * P], tw["gwb"][:, h, :],
                                   start=(h == 0), stop=(h == 1))
            mm.then_inc(full[fills["gate", 0][0]], 1)
            pe.wait_ge(ev["fx"], 1)
            stage_T("fT", fxt)
            pe.wait_ge(ev["fxT"], 4)
            stage_F("fc1", tw["fc1d"][:, :], xt[:, :], CH)
            pe.wait_ge(ev["hx"], 4)
            stage_W("fc2", tw["fc2d"][:, :], xt, CH, 65)
            pe.wait_ge(ev["fo"], 1)
            stage_T("foT", fo)
            pe.wait_ge(ev["foT"], 4)
            o = to_fill("fg", 0)
            for j in range(J):
                mm = pe.matmul(o[:, j * 4:(j + 1) * 4], xt[0:64, j * P:(j + 1) * P], tw["fgt"][:, :], start=True, stop=True)
            mm.then_inc(full[fills["fg", 0][0]], 1)

        @block.vector
        def _(dve):
            dve.sem_inc(aTe, 2)
            dve.sem_inc(aRe, 2)
            dve.sem_inc(mE[1], 4)
            dve.sem_inc(bKe, 2)
            dve.sem_inc(bTe, 2)
            dve.sem_inc(bS, 2)
            dve.sem_inc(fOe, 4)
            dve.memset(xq.rearrange("p n m -> p (n m)"), 0.0).then_inc(lift_clear, 1)
            for j in range(4):
                dve.wait_ge(zR, j + 1)
                src = bank[4 + j][:, :].rearrange("p (t c) -> p t c", c=P)[:, :, 0:96]
                dve.tensor_copy(att_t[:, 4 * j:4 * j + 4, 0:96], src).then_inc(zRe, 1)
            barrier(dve, 1)
            barrier(dve, 2)

            def forward(m):
                def fwd(k, u, front, back, ahead):
                    N = m * PAIRS + k
                    B = N + (-1)

                    def T(j):
                        dve.wait_ge(aT, N * 8 + j + 1 + 16)
                        dve.tensor_copy(ht[:, 4 * j:4 * j + 4, :].rearrange("p t c -> p (t c)"), bank[j % 2][:, :]).then_inc(aTe, 1)

                    def R(j):
                        dve.wait_ge(aR, B * 4 + j + 1)
                        dve.tensor_copy(att_t[:, 4 * j:4 * j + 4, :].rearrange("p t c -> p (t c)"), bank[4 + j % 2][:, :]).then_inc(aRe, 1)
                    if front:
                        T(0); T(1); T(2); T(3)
                    if back:
                        R(0); R(1)
                    if front:
                        T(4); T(5)
                    if back:
                        R(2); R(3)
                    if front:
                        T(6); T(7)
                skewed(dve, fwd)
                barrier(dve, m * NPH + 5)

            def layer(l, m):
                def turn(g):
                    u = g % 2
                    dve.wait_ge(mXld[u], (l * (CHUNKS // 2) + g // 2) * 32 + 32)
                    dve.tensor_copy(xin[0:CH, u, 0].rearrange("p b m -> p (b m)"), xin[CH:P, u, 1].rearrange("p b m -> p (b m)")).then_inc(mCp, 1)
                turn(0)
                for g in range(CHUNKS):
                    u = g % 2
                    dve.wait_ge(mZst[u], (l * (CHUNKS // 2) + g // 2) * 64 + 64)
                    for k in range(1, 8, 2):
                        if k == 3 and g + 1 < CHUNKS:
                            turn(g + 1)
                        dve.wait_ge(mM, (l * CHUNKS + g) * 8 + k + 1 + 16)
                        dve.tensor_copy(zout[:, u, 8 * k:8 * k + 8, :].rearrange("p m o -> p (m o)"), bank[k][:, :]).then_inc(mE[1], 1)
                barrier(dve, l * NPH + 3)
                if m is None:
                    dve.memset(htile.rearrange("p u n -> p (u n)"), 0.0).then_inc(hclear, 1)

                def inv(k, u, front, back, ahead):
                    N = l * PAIRS + k
                    B = N + (-1)
                    ub = 1 - u

                    def K(j):
                        dve.wait_ge(bK, N * 4 + j + 1 + 8)
                        dst = gtile[:, :, :, 4 * j:4 * j + 4].rearrange("p x r k -> p k r x")
                        dve.tensor_copy(dst, bank[j % 2][:, :].rearrange("p (k r x) -> p k r x", k=4, r=2)).then_inc(bKe, 1)

                    def T(j):
                        dve.wait_ge(bT, N * 4 + j + 1)
                        dve.tensor_copy(gt[:, u, 4 * j:4 * j + 4, :].rearrange("p t c -> p (t c)"), bank[2 + j % 2][:, :]).then_inc(bTe, 1)

                    def S(f):
                        dve.wait_ge(bFe, B * 8 + f + 1 + 4)
                        at = (k + (-1)) * 8 + f
                        st = dve.bn_stats(stats[:, bass.ds(at, 1), :].rearrange("p a s -> p (a s)"), yout[:, ub, f * BANK:(f + 1) * BANK])
                        if f == 7:
                            st.then_inc(bS, 1)
                    if front:
                        K(0); K(1)
                    if back:
                        S(0)
                    if front:
                        K(2); K(3)
                    if back:
                        S(1)
                    if front:
                        T(0); T(1)
                    if back:
                        S(2); S(3)
                    if front:
                        T(2); T(3)
                    if back:
                        S(4); S(5); S(6); S(7)
                skewed(dve, inv)
                dve.wait_ge(bS, l * PAIRS + PAIRS + 2)
                dve.bn_aggr(mv[:, :], stats[:, :, :].rearrange("p a s -> p (a s)")).then_inc(stv, 2)
                dve.wait_ge(stp, l * 2 + 1)
                dve.tensor_copy(sm[:, 0:1], bank[0][:, 0:1]).then_inc(stv, 1)
                dve.wait_ge(stv, l * 8 + 3)
                dve.tensor_tensor(sm[:, 1:2], mv[:, 0:1], sm[:, 0:1], ALU.subtract).then_inc(stv, 1)
                dve.wait_ge(stv, l * 8 + 4)
                dve.scalar_tensor_tensor(out=sm[:, 3:4], in0=sm[:, 1:2], scalar=sm[:, 1:2], in1=mv[:, 1:2], op0=ALU.mult, op1=ALU.add).then_inc(stv, 1)
                dve.wait_ge(sta, l + 1)
                dve.reciprocal(sm[:, 5:6], sm[:, 4:5]).then_inc(stv, 1)
                dve.wait_ge(stv, l * 8 + 6)
                dve.tensor_tensor(bn_scale[:, :], sm[:, 5:6], vecs[:, 1:2], ALU.mult).then_inc(stv, 1)
                dve.wait_ge(stv, l * 8 + 7)
                dve.tensor_tensor(sm[:, 6:7], sm[:, 0:1], bn_scale[:, :], ALU.mult).then_inc(stv, 1)
                dve.wait_ge(stv, l * 8 + 8)
                dve.tensor_tensor(bn_bias[:, :], vecs[:, 2:3], sm[:, 6:7], ALU.subtract)
                barrier(dve, l * NPH + 4)
            layer(0, None)
            with dve.Fori(0, LAYERS - 1) as m:
                forward(m)
                layer(m + 1, m)

            def last(n, u, i):
                dve.wait_ge(fFree, n + 1)
                for q in range(2):
                    dve.wait_ge(fO, n * 2 + q + 1 + 2)
                    dve.tensor_scalar(towr[:, u, q, :], bank[4 + 2 * u + q][:, :], fc2b[:, 0:1], None, ALU.add).then_inc(fOe, 1)
            pairs(dve, last)
            dve.sem_inc(lKe, 1)
            dve.sem_inc(lSe, 2)
            dve.sem_inc(lTe, 1)
            dve.sem_inc(lOe, 1)
            dve.sem_inc(lVe, 1)
            barrier(dve, LAYERS * NPH + 2)
            n_chain = [0]

            def link(ins):
                n_chain[0] += 1
                ins.then_inc(chain, 1)
                dve.wait_ge(chain, n_chain[0])

            n_var = [0]

            def g3(x, g):
                return x.rearrange("p (g d) -> p g d", g=g)

            def wide(x, d):
                return x.rearrange("p (g o) -> p g o", o=1).to_broadcast([P, x.shape[1], d])

            def center_norm(x, out, g, d, eps_after=None):
                link(dve.tensor_reduce(s1[:, 0:g], g3(x, g), AX.X, ALU.add))
                link(dve.scalar_tensor_tensor(out=g3(xc[:, 0:g * d], g), in0=wide(s1[:, 0:g], d), scalar=-1.0 / d, in1=g3(x, g),
                                              op0=ALU.mult, op1=ALU.add))
                link(dve.tensor_tensor(sq[:, 0:g * d], xc[:, 0:g * d], xc[:, 0:g * d], ALU.mult))
                dve.tensor_reduce(s2[:, 0:g], g3(sq[:, 0:g * d], g), AX.X, ALU.add).then_inc(ev["var"], 1)
                n_var[0] += 1
                dve.wait_ge(ev["rstd"], n_var[0])
                if eps_after is not None:
                    link(dve.tensor_scalar(sd[:, 0:g], sd[:, 0:g], eps_after, None, ALU.add))
                link(dve.reciprocal(s2[:, 0:g], sd[:, 0:g]))
                return dve.tensor_tensor(g3(out, g), g3(xc[:, 0:g * d], g), wide(s2[:, 0:g], d), ALU.mult)

            def per_tile(w, n):
                return w.rearrange("p (o n) -> p o n", o=1).to_broadcast([P, J, n])

            dve.wait_ge(h1_ld, 16)
            center_norm(h1, xn, J, CH).then_inc(ev["xn"], 1)
            for b in range(4):
                o = filled(dve, "kv", b)
                ins = dve.tensor_copy(kv[:, b * BANK:(b + 1) * BANK], o[:, :])
                ins.then_inc(empty[fills["kv", b][0]], 1)
            for b in range(4):
                dve.wait_ge(empty[fills["kv", b][0]], fills["kv", b][1] + 1)
            link(center_norm(kv, kv, 512, 4, 1e-5))
            link(dve.tensor_tensor(g3(kv, J), g3(kv, J), per_tile(tw["kvw"], P), ALU.mult))
            for t, dst in ((0, kn), (1, vn)):
                src = kv.rearrange("p (j h t d) -> p t (j h) d", j=J, t=2, d=4)[:, t]
                link(dve.tensor_copy(dst.rearrange("p (g d) -> p g d", d=4), src))
            link(dve.tensor_tensor(g3(kn, J), g3(kn, J), per_tile(tw["kvb"][:, 0:CH], CH), ALU.add))
            dve.tensor_tensor(g3(vn, J), g3(vn, J), per_tile(tw["kvb"][:, CH:2 * CH], CH), ALU.add).then_inc(ev["kn"], 1)
            for b in range(2):
                o = filled(dve, "kvm", b)
                bd = tw["bd"].rearrange("p (o n) -> p o n", o=1).to_broadcast([P, 8, CH])
                dve.tensor_tensor(g3(kvm[:, b * BANK:(b + 1) * BANK], 8), g3(o[:, :], 8), bd, ALU.mult).then_inc(ev["kvm"], 1)
            dve.wait_ge(ev["kvm"], 2)
            for b in range(2):
                dve.sem_inc(empty[fills["kvm", b][0]], 1)
            for b in range(2):
                o = filled(dve, "out", b)
                link(dve.tensor_tensor(ret[:, b * BANK:(b + 1) * BANK], o[:, :], xn[:, b * BANK:(b + 1) * BANK], ALU.add))
                dve.sem_inc(empty[fills["out", b][0]], 1)
            dve.sem_inc(ev["ret"], 1)
            link(dve.tensor_tensor(h2, h1, xn, ALU.add))
            dve.wait_ge(ev["ga"], 2)
            link(dve.tensor_tensor(h2, h2, ga, ALU.add))
            center_norm(h2, x2, J, CH).then_inc(ev["x2"], 1)

            def pair_step(k, u, proj, score, comb):
                u1 = 1 - u

                def keys():
                    dve.wait_ge(lK, k + 1)
                    dst = kb[:, u].rearrange("p (i n t) -> p n i t", i=2, n=4)
                    dve.tensor_copy(dst, bank[2][:, :].rearrange("p (n i t) -> p n i t", n=4, i=2)).then_inc(lKe, 1)

                def values():
                    dve.wait_ge(lV, k + 1)
                    for h in range(2):
                        src = bank[3][64 * h:64 * h + 64, 0:64].rearrange("p (iq o) -> p iq o", o=16)
                        dve.tensor_copy(vb[64 * h:64 * h + 64, u, :, :, h, 0:16].rearrange("p i q o -> p (i q) o"), src)
                    dve.tensor_copy(sx[:, bass.ds(k * CH, CH)].rearrange("p (n d) -> p n d", d=16),
                                    bank[3][:, P:2 * P].rearrange("p (n d) -> p n d", d=32)[:, :, 0:16]).then_inc(lVe, 1)

                def soft(i):
                    B = k + (-1)
                    dve.wait_ge(lS, B * 2 + i + 1)
                    v = bank[4 + i][:, :].rearrange("p (g t) -> p g t", t=64)
                    dve.tensor_reduce(mx[:, u1, i, :], v, AX.X, ALU.max).then_inc(lMx, 1)
                    dve.wait_ge(lMx, B * 2 + i + 1)
                    m = mx[:, u1, i, :].rearrange("p (g o) -> p g o", o=1).to_broadcast([P, 8, 64])
                    dve.tensor_tensor(ex[:, u1, i, :].rearrange("p (g t) -> p g t", t=64), v, m, ALU.subtract).then_inc(lSe, 1)

                def turned(i):
                    C = k + (-2)
                    dve.wait_ge(lT, C * 2 + i + 1)
                    dve.tensor_copy(exT[:, i, :], bank[6][:, :]).then_inc(lTe, 1)

                def divide():
                    C = k + (-2)
                    dve.wait_ge(lO, C + 1)
                    v = bank[7][:, 0:272].rearrange("p (g o) -> p g o", o=17)
                    dve.reciprocal(rden[:, u, :].rearrange("p (g o) -> p g o", o=1), v[:, :, 16:17]).then_inc(lRd, 1)
                    dve.wait_ge(lRd, C + 1)
                    for e2 in range(2):
                        r = rden[:, u, 8 * e2:8 * e2 + 8].rearrange("p (g o) -> p g o", o=1).to_broadcast([P, 8, 16])
                        for ep in range(2):
                            d = att_out[:, bass.ds(C * 256 + ep * 128 + e2 * 64, 64)].rearrange("p (n d) -> p n d", d=16)
                            g = e2 * 8 + ep * 4
                            rr = rden[:, u, g:g + 4].rearrange("p (g o) -> p g o", o=1).to_broadcast([P, 4, 16])
                            ins = dve.tensor_tensor(d, v[:, g:g + 4, 0:16], rr, ALU.mult)
                    ins.then_inc(lOe, 1)
                if comb: turned(0)
                if score: soft(0)
                if proj: keys()
                if comb: turned(1)
                if score: soft(1)
                if comb: divide()
                if proj: values()
            dve.wait_ge(clear, 8)
            skewed3(dve, pair_step)
            dve.wait_ge(lOe, J + 1)
            apart(dve)
            link(dve.tensor_scalar(keep, sx, 0.0, None, ALU.not_equal))
            a4 = att_out.rearrange("p (j e c) -> p e j c", j=J, e=4)
            for e in range(4):
                ins = dve.tensor_tensor(a4[:, e], a4[:, e], g3(keep, J), ALU.mult)
            link(ins)
            dve.sem_inc(ev["att"], 1)
            for n in range(4):
                src = sx[64 * (n % 2):64 * (n % 2) + 64, (n // 2) * CH + 16 * n:(n // 2) * CH + 16 * n + 16]
                for i in range(2):
                    ins = dve.tensor_copy(res[64 * i:64 * i + 64, 16 * n:16 * n + 16], src)
            link(ins)
            for b in range(0, 8, 2):
                o = filled(dve, "attT", b)
                link(dve.tensor_copy(att_T[:, b * BANK:(b + 1) * BANK], o[:, :]))
                dve.sem_inc(empty[fills["attT", b][0]], 1)
                dve.sem_inc(ev["attT"], 1)
            o = filled(dve, "gate", 0)
            link(dve.tensor_tensor(g3(lg, J), g3(o[:, 0:256], J), per_tile(tw["gateb"], 16), ALU.add))
            dve.sem_inc(empty[fills["gate", 0][0]], 1)
            link(dve.tensor_reduce(gmax, g3(lg, 64), AX.X, ALU.max))
            link(dve.tensor_tensor(g3(lg, 64), g3(lg, 64), wide(gmax, 4), ALU.subtract))
            dve.sem_inc(ev["lg"], 1)
            dve.wait_ge(ev["gexp"], 1)
            link(dve.tensor_reduce(gsum, g3(gexp, 64), AX.X, ALU.add))
            link(dve.reciprocal(gmax, gsum))
            link(dve.tensor_tensor(g3(gexp, 64), g3(gexp, 64), wide(gmax, 4), ALU.mult))
            ge = gexp.rearrange("p (jn e) -> p e jn", e=4)
            for e in range(4):
                gw = ge[:, e].rearrange("p (g o) -> p g o", o=1).to_broadcast([P, 64, 16])
                dst = mixed if e == 0 else prod[:, 0:TD]
                gwj = gw.rearrange("p (j n) d -> p j n d", j=J)
                link(dve.tensor_tensor(dst.rearrange("p (j n d) -> p j n d", j=J, d=16),
                                       a4[:, e].rearrange("p j (n d) -> p j n d", d=16), gwj, ALU.mult))
                if e:
                    link(dve.tensor_tensor(mixed, mixed, prod[:, 0:TD], ALU.add))
            link(dve.tensor_tensor(g3(mixed, J), g3(mixed, J), per_tile(res[:, :], CH), ALU.add))
            link(center_norm(mixed, fxt, 64, 16))
            link(dve.tensor_tensor(g3(fxt, J), g3(fxt, J), per_tile(tw["lng"], CH), ALU.mult))
            link(dve.tensor_tensor(g3(fxt, J), g3(fxt, J), per_tile(tw["lnb"], CH), ALU.add))
            dve.sem_inc(ev["fx"], 1)
            link(dve.tensor_scalar(keep, fxt, 0.0, None, ALU.not_equal))
            dve.wait_ge(ev["fxT"], 4)
            link(dve.tensor_scalar(keepT, xt[0:64, :], 0.0, None, ALU.not_equal))
            for b in range(4):
                o = filled(dve, "fc1", b)
                if b == 0:
                    filled(dve, "fc1", 3)
                link(dve.scalar_tensor_tensor(out=xt[0:64, b * BANK:(b + 1) * BANK], in0=o[0:64, :], scalar=0.0,
                                              in1=keepT[:, b * BANK:(b + 1) * BANK], op0=ALU.max, op1=ALU.mult))
                dve.sem_inc(empty[fills["fc1", b][0]], 1)
                dve.sem_inc(ev["hx"], 1)
            for b in range(2):
                o = filled(dve, "fc2", b)
                link(dve.tensor_tensor(hx[:, b * BANK:(b + 1) * BANK], o[:, :], keep[:, b * BANK:(b + 1) * BANK], ALU.mult))
                dve.sem_inc(empty[fills["fc2", b][0]], 1)
            link(dve.tensor_tensor(hx, hx, fxt, ALU.add))
            link(center_norm(hx, fo, 64, 16))
            link(dve.tensor_tensor(g3(fo, J), g3(fo, J), per_tile(tw["fng"], CH), ALU.mult))
            link(dve.tensor_tensor(g3(fo, J), g3(fo, J), per_tile(tw["fnb"], CH), ALU.add))
            dve.sem_inc(ev["fo"], 1)
            o = filled(dve, "fg", 0)
            v = g3(o[:, 0:64], J)
            link(dve.tensor_reduce(gmax[:, 0:J], v, AX.X, ALU.max))
            link(dve.tensor_tensor(g3(lg[:, 0:64], J), v, wide(gmax[:, 0:J], 4), ALU.subtract))
            dve.sem_inc(ev["fl"], 1)
            dve.wait_ge(ev["fexp"], 1)
            link(dve.tensor_reduce(gsum[:, 0:J], g3(gexp[:, 0:64], J), AX.X, ALU.add))
            link(dve.reciprocal(gmax[:, 0:J], gsum[:, 0:J]))
            link(dve.tensor_tensor(g3(gexp[:, 0:64], J), g3(gexp[:, 0:64], J), wide(gmax[:, 0:J], 4), ALU.mult))
            link(dve.tensor_tensor(g3(fo, 64), g3(fo, 64), wide(gexp[:, 0:64], 16), ALU.mult))
            dve.tensor_tensor(h2, h2, fo, ALU.add).then_inc(ev["done"], 1)

        @block.scalar
        def _(act):
            act.sem_inc(zXe, 4)
            act.sem_inc(zSt[0], 16)
            act.sem_inc(zSt[1], 16)
            act.sem_inc(bG, 2)
            act.sem_inc(aG, 8)
            act.sem_inc(aYe, 2)
            act.sem_inc(aXe, 2)
            act.sem_inc(aXst[0], 16)
            act.sem_inc(aXst[1], 16)
            act.sem_inc(mE[0], 4)
            act.sem_inc(mZst[0], 64)
            act.sem_inc(mZst[1], 64)
            act.sem_inc(bFe, 4)
            act.sem_inc(bYst[0], 16)
            act.sem_inc(bYst[1], 16)
            act.sem_inc(fG, 2)
            act.sem_inc(fCe, 4)
            act.wait_ge(cst, 16 * NCONST)

            def evac_y(dst, src, g):
                d = dst.rearrange("p k (r x) -> p x r k", r=2)[:, 16 * g:16 * g + 16]
                return act.copy(d, src.rearrange("p (x r k) -> p x r k", x=16, r=2))

            def evac_x(dst, src, g):
                v = src.rearrange("p (k r c x) -> p r c k x", k=8, r=2, c=CHUNKS)
                for r in range(2):
                    d = dst[:, :, r, 64 * g:64 * g + 64].rearrange("p c (k x) -> p c k x", x=8)
                    cp = act.copy(d, v[:, r])
                return cp

            for g in range(4):
                act.wait_ge(zY, g + 1)
                evac_y(atile[0:96, 0], bank[g][0:96, :], g).then_inc(zYe, 1)
            for g in range(2):
                act.wait_ge(zM, g + 1)
                evac_x(xout[0:96, 0], bank[g][0:96, :], g).then_inc(zMe, 1)
            act.wait_ge(zMe, 2)
            act.dma_start(colour_modes, xout[0:96, 0].rearrange("p g r m -> p (g r m)")).then_inc(cmst, 16)
            act.wait_ge(cmst, 16)
            barrier(act, 1)

            def lift(n, u, i):
                act.wait_ge(zSt[u], i * 16 + 16)
                for g in range(2):
                    act.wait_ge(zX, n * 2 + g + 1)
                    act.copy(xout[:, u].rearrange("p g r m -> p (g r m)")[:, g * BANK:(g + 1) * BANK], bank[2 * u + g][:, :]).then_inc(zXe, 1)
                act.wait_ge(zXe, n * 2 + 2 + 4)
                dst = xmodes.rearrange("g r b c m -> (b c) (g r) m")[bass.ds(n * P, P)]
                act.dma_start(dst, xout[:, u].rearrange("p g r m -> p (g r) m")).then_inc(zSt[u], 16)
            pairs(act, lift)
            for u in range(2):
                act.wait_ge(zSt[u], 16 * (PAIRS // 2 + 1))
            barrier(act, 2)

            def gelu(q, u):
                src = ytile[:, u, q * 1024:(q + 1) * 1024]
                dst = htile[:, u, q * 1024:(q + 1) * 1024]
                return act.activation(dst, src, ACT.Gelu, bias=bn_bias[:, 0:1], scale=bn_scale[:, 0:1])

            def forward(m):
                def fwd(k, u, front, back, ahead):
                    N = m * PAIRS + k
                    B = N + (-1)
                    ub = 1 - u

                    def A(q):
                        if q == 0:
                            act.wait_ge(yld[ub], (m * 2 * PAIRS + k + 1 - ub) * 8 + 16)
                            act.wait_ge(aT, (N + 1) * 8 + 8)
                        gelu(q, ub).then_inc(aG, 1)

                    def Y(g):
                        act.wait_ge(aY, N * 4 + g + 1)
                        evac_y(atile[:, u], bank[2 + g % 2][:, :], g).then_inc(aYe, 1)

                    def X(g):
                        if g == 0:
                            act.wait_ge(aXst[ub], (B - ub) * 8 + 16)
                        act.wait_ge(aX, B * 2 + g + 1)
                        evac_x(xout[:, ub], bank[6 + g][:, :], g).then_inc(aXe, 1)

                    if ahead: A(0)
                    if front: Y(0)
                    if ahead: A(1)
                    if front: Y(1)
                    if back: X(0)
                    if ahead: A(2)
                    if front: Y(2)
                    if ahead: A(3)
                    if back: X(1)
                    if front: Y(3)
                    if back:
                        act.wait_ge(aXe, B * 2 + 4)
                        dst = xmodes.rearrange("g r b c m -> (b c) (g r) m")[bass.ds((k + (-1)) * P, P)]
                        act.dma_start(dst, xout[:, ub].rearrange("p g r m -> p (g r) m")).then_inc(aXst[ub], 16)
                act.wait_ge(yld[0], m * 2 * PAIRS * 8 + 16)
                for q in range(4):
                    gelu(q, 0).then_inc(aG, 1)
                skewed(act, fwd)
                for u in range(2):
                    act.wait_ge(aXst[u], (m + 1) * 8 * PAIRS + 16)
                barrier(act, m * NPH + 5)

            def layer(l, m):
                def turn(g):
                    u = g % 2
                    act.wait_ge(mXld[u], (l * (CHUNKS // 2) + g // 2) * 32 + 32)
                    act.mul(xin[CH:P, u, 0], xin[0:CH, u, 1], -1.0).then_inc(mNeg, 1)
                turn(0)
                for g in range(CHUNKS):
                    u = g % 2
                    G = l * CHUNKS + g
                    act.wait_ge(mZst[u], (l * (CHUNKS // 2) + g // 2) * 64 + 64)
                    for k in range(0, 8, 2):
                        if k == 4 and g + 1 < CHUNKS:
                            turn(g + 1)
                        act.wait_ge(mM, G * 8 + k + 1 + 16)
                        act.copy(zout[:, u, 8 * k:8 * k + 8, :].rearrange("p m o -> p (m o)"), bank[k][:, :]).then_inc(mE[0], 1)
                    act.wait_ge(mE[0], G * 4 + 4 + 4)
                    act.wait_ge(mE[1], G * 4 + 4 + 4)
                    for parity in range(2):
                        for v in range(2):
                            p0 = 64 * parity + 32 * v
                            dst = zmodes[v].rearrange("k (y q) b o -> q b (k y) o", q=2)[parity][:, g * 64:g * 64 + 64, :]
                            act.dma_start(dst, zout[p0:p0 + 32, u]).then_inc(mZst[u], 16)
                for u in range(2):
                    act.wait_ge(mZst[u], (l + 1) * 128 + 64)
                barrier(act, l * NPH + 3)
                act.wait_ge(par, l * 48 + 48)
                apart(act)
                if m is None:
                    act.wait_ge(pw0_f, 1)
                    act.copy(pw0[0:7, :], bank[0][0:7, 0:P]).then_inc(pw0_e, 1)

                def inv(k, u, front, back, ahead):
                    N = l * PAIRS + k
                    B = N + (-1)
                    ub = 1 - u

                    def A(q):
                        if q == 0:
                            act.wait_ge(yld[u], (m * 2 * PAIRS + PAIRS + k - u) * 8 + 16)
                            act.wait_ge(bF, N * 8 + 8)
                        h = gelu(q, u)
                        if q == 3:
                            h.then_inc(bG, 1)

                    def F(f):
                        if f == 0:
                            act.wait_ge(bYst[ub], (B - ub) * 8 + 16)
                            act.wait_ge(bS, B + 1)
                        act.wait_ge(bF, B * 8 + f + 1 + 16)
                        act.activation(yout[:, ub, f * BANK:(f + 1) * BANK], bank[4 + f % 4][:, :], ACT.Identity, bias=vecs[:, 0:1]).then_inc(bFe, 1)
                    front = front and m is not None
                    if front: A(0)
                    if back: F(0)
                    if front: A(1)
                    if back: F(1)
                    if back: F(2)
                    if front: A(2)
                    if back: F(3)
                    if back: F(4)
                    if front: A(3)
                    if back:
                        F(5); F(6); F(7)
                        act.wait_ge(bFe, B * 8 + 8 + 4)
                        act.dma_start(field[bass.ds(k + (-1), 1)].rearrange("a p m -> p (a m)"), yout[:, ub, :]).then_inc(bYst[ub], 16)
                skewed(act, inv)
                for u in range(2):
                    act.wait_ge(bYst[u], (l + 1) * 8 * PAIRS + 16)
                act.wait_ge(stp, l * 2 + 2)
                act.activation(sm[:, 4:5], bank[0][:, 1:2], ACT.Sqrt, bias=epst[:, 0:1]).then_inc(sta, 1)
                barrier(act, l * NPH + 4)
            layer(0, None)
            with act.Fori(0, LAYERS - 1) as m:
                forward(m)
                layer(m + 1, m)

            def last(k, u, front, back, ahead):
                def A(q):
                    if q == 0:
                        act.wait_ge(yld[1 - u], ((LAYERS - 1) * 2 * PAIRS + k + 1 - (1 - u)) * 8 + 16)
                    h = gelu(q, 1 - u)
                    if q == 3:
                        h.then_inc(fG, 1)
                if not front:
                    return
                for r in range(16):
                    if r % 8 == 0:
                        act.wait_ge(fO, k * 2 + r // 8 + 1)
                    act.wait_ge(fC, k * 16 + r + 1)
                    act.activation(hidden[:, r, :], bank[r % 4][:, :], ACT.Gelu, bias=fc1b[:, r % 2:r % 2 + 1]).then_inc(fCe, 1)
                    if ahead and r % 4 == 1:
                        A(r // 4)
            act.wait_ge(yld[0], (LAYERS - 1) * 2 * PAIRS * 8 + 16)
            for q in range(4):
                h = gelu(q, 0)
            h.then_inc(fG, 1)
            skewed(act, last)
            act.sem_inc(lSXe, 1)
            act.sem_inc(lQe, 1)
            barrier(act, LAYERS * NPH + 2)

            def move(name, b, dst, event, parts=P):
                o = filled(act, name, b)
                act.copy(dst, o[0:parts, :]).then_inc(ev[event], 1)

            def emptied(name, n, event):
                act.wait_ge(ev[event], n)
                for b in range(n):
                    act.sem_inc(empty[fills[name, b][0]], 1)

            def root(n, g, scale, eps):
                act.wait_ge(ev["var"], n)
                bias = {} if eps is None else {"bias": eps[:, 0:1]}
                act.activation(sd[:, 0:g], s2[:, 0:g], ACT.Sqrt, scale=scale, **bias).then_inc(ev["rstd"], 1)

            act.wait_ge(clear, 8)
            root(1, J, 1.0 / CH, eps5)
            for b in range(4):
                move("xT", b, xt[0:64, b * BANK:(b + 1) * BANK], "xT", 64)
            emptied("xT", 4, "xT")
            for b in range(4):
                move("q", b, qt[:, b * BANK:(b + 1) * BANK], "qT")
            emptied("q", 4, "qT")
            act.copy(maskb[:, :], tw["mask"][:, :]).then_inc(masks, 1)
            act.copy(identb[:, :], ident[:, :]).then_inc(masks, 1)
            root(2, 512, 1.0 / 3.0, None)
            filled(act, "kv", 3)
            for b in range(4):
                move("retT", b, xt[0:64, b * BANK:(b + 1) * BANK], "retT", 64)
            emptied("retT", 4, "retT")
            for b in range(2):
                o = filled(act, "proj", b)
                act.activation(ga[:, b * BANK:(b + 1) * BANK], o[:, :], ACT.Gelu).then_inc(ev["ga"], 1)
            emptied("proj", 2, "ga")
            root(3, J, 1.0 / CH, eps5)
            for b in range(4):
                move("x2T", b, xt[0:64, b * BANK:(b + 1) * BANK], "x2T", 64)
            emptied("x2T", 4, "x2T")

            def pair_step(k, u, proj, score, comb):
                u1 = 1 - u

                def inputs():
                    act.wait_ge(lSX, k + 1)
                    act.copy(sxT[:, u, :], bank[0][:, 0:P]).then_inc(lSXe, 1)

                def queries():
                    act.wait_ge(lQ, k + 1)
                    dst = qb[:, u].rearrange("p (i e s) -> p e i s", i=2, e=4)
                    act.copy(dst, bank[1][:, :].rearrange("p (e i s) -> p e i s", e=4, i=2)).then_inc(lQe, 1)

                def exps(i):
                    B = k + (-1)
                    act.wait_ge(lSe, B * 2 + i + 1 + 2)
                    act.activation(ex[:, u1, i, :], ex[:, u1, i, :], ACT.Exp, scale=4.0).then_inc(lE, 1)
                if proj: inputs()
                if score: exps(0)
                if proj: queries()
                if score: exps(1)
            skewed3(act, pair_step)
            for b in range(1, 8, 2):
                o = filled(act, "attT", b)
                act.copy(att_T[:, b * BANK:(b + 1) * BANK], o[:, :]).then_inc(ev["attT"], 1)
            act.wait_ge(ev["attT"], 8)
            for b in range(1, 8, 2):
                act.sem_inc(empty[fills["attT", b][0]], 1)
            act.wait_ge(ev["lg"], 1)
            act.activation(gexp, lg, ACT.Exp).then_inc(ev["gexp"], 1)
            root(4, 64, 1.0 / 16, eps8)
            for b in range(4):
                move("fT", b, xt[0:64, b * BANK:(b + 1) * BANK], "fxT", 64)
            emptied("fT", 4, "fxT")
            root(5, 64, 1.0 / 16, eps8)
            for b in range(4):
                move("foT", b, xt[0:64, b * BANK:(b + 1) * BANK], "foT", 64)
            emptied("foT", 4, "foT")
            act.wait_ge(ev["fl"], 1)
            act.activation(gexp[:, 0:64], lg[:, 0:64], ACT.Exp).then_inc(ev["fexp"], 1)


def constants():
    import numpy as np
    f = np.float64
    y = np.arange(SIDE)
    ky = np.arange(NKY)
    kx = np.concatenate([np.arange(16), np.arange(SIDE - 16, SIDE)])
    ay = 2 * np.pi * np.outer(y, ky) / SIDE
    ax = 2 * np.pi * np.outer(y, kx) / SIDE
    one = np.stack([np.cos(ay), -np.sin(ay)], 1).reshape(SIDE, 2 * NKY)
    fy = np.kron(np.eye(2), one)
    c, s = np.cos(ax), np.sin(ax)
    fx = np.block([[c, -s], [s, c]])
    ix = np.block([[c.T, s.T], [-s.T, c.T]]) / SIDE
    wk = np.where(ky == 0, 1.0, 2.0)[:, None]
    inv = np.concatenate([wk * np.cos(ay.T), -wk * np.sin(ay.T)], 0) / SIDE
    iy = np.kron(np.eye(4), inv)
    avg = np.kron(np.full((2, 2), 0.5), np.eye(CH))
    return {"c_ident": np.eye(P), "c_fy": fy, "c_fx": fx, "c_ix": ix, "c_iy": iy, "c_avg": avg}


def layout(d):
    import numpy as np
    g = lambda k: np.asarray(d[k])
    out = {k: v.astype(np.float32) for k, v in constants().items()}
    x = g("x")
    pair = x.reshape(PAIRS, 2, PIX, 3).transpose(0, 1, 3, 2).reshape(PAIRS, 6, PIX)
    out["x"] = np.concatenate([pair, np.ones((PAIRS, 1, PIX), np.float32)], 1)
    out["xs"] = x.reshape(BATCH, 32, 2, SIDE, 3).transpose(2, 3, 1, 0, 4).reshape(P, 32, 96)
    dc = np.zeros((1, PAIRS, 1024), np.float32)
    dc[:, :, 0] = PIX
    out["dc"] = dc
    two = lambda a: np.concatenate([a, a], 0)
    w0, b0 = g("L0_tok_fc0_w"), g("L0_tok_fc0_b")
    fc0 = np.zeros((7, 2, CH), np.float32)
    fc0[0:3, 0], fc0[3:6, 1], fc0[6] = w0, w0, b0
    out["fc0"] = fc0.reshape(7, P)
    out["fc0t"] = fc0.reshape(7, P).T
    w = np.stack([np.stack([g("L0_tok_w1r"), g("L0_tok_w1i")], 1), np.stack([g("L0_tok_w2r"), g("L0_tok_w2i")], 1)], 1)
    w = w.reshape(LAYERS, 2, 2, CH, CH, 2, CM).transpose(0, 1, 5, 2, 3, 6, 4)
    out["w"] = np.ascontiguousarray(w).reshape(LAYERS * CHUNKS, P, CM, CH)
    out["pw"] = np.ascontiguousarray(g("L0_tok_pw_w").transpose(0, 2, 1))
    v = np.stack([g("L0_tok_pw_b"), g("L0_tok_gamma"), g("L0_tok_beta")], -1)
    out["vecs"] = np.concatenate([v, v], 1)
    w1 = g("L0_tok_fc1_w").reshape(CH, 2, 64)
    w2 = g("L0_tok_fc2_w").reshape(2, 64)
    fc1 = np.zeros((2, CH, 2, 2, 64), np.float32)
    fc2 = np.zeros((2, 64, 2, 32), np.float32)
    for s in range(2):
        fc1[s, :, :, s] = w1
        fc2[s, :, :, s] = w2.T
    out["fc1"], out["fc2"] = fc1.reshape(P, 2, P), fc2.reshape(P, 2, 32)
    out["fc1b"] = two(g("L0_tok_fc1_b").reshape(2, 64).T)
    out["fc2b"] = np.broadcast_to(g("L0_tok_fc2_b")[:, None], (P, 1))
    a = lambda k: g("L0_attn_" + k)
    wq = a("W_qkv").reshape(16, 3, 4, CH)
    bq = a("b_qkv").reshape(16, 3, 4)
    t = {}
    t["wkv"] = np.concatenate([wq[:, 1:].reshape(P, CH).T, bq[:, 1:].reshape(1, P)], 0)
    q = np.concatenate([wq[:, 0].reshape(CH, CH).T, bq[:, 0].reshape(1, CH)], 0)
    t["wq2"] = np.concatenate([q, q], 1)
    t["wproj"] = np.concatenate([a("W_proj").T, a("b_proj")[None]], 0)
    rep = lambda v: np.broadcast_to(v.reshape(1, -1), (P, v.size))
    t["kvw"] = rep(np.stack([a("kln_w")[:, 0], a("vln_w")[:, 0]], 1))
    t["kvb"] = rep(np.stack([a("kln_b")[:, 0], a("vln_b")[:, 0]], 0))
    hd = np.arange(CH) // 4
    t["bd"] = np.tile((hd[:, None] == hd[None, :]) / CH, (2, 1)).astype(np.float32)
    f = lambda k: g("L0_ffn_" + k)
    z = lambda *s: np.zeros(s, np.float32)
    hl = z(65, 4, 32)
    hl[0:64, :, 0:16] = f("hl_w").transpose(2, 0, 1)
    hl[64, :, 0:16] = f("hl_b")
    t["hlp"] = hl.reshape(65, P)
    w = z(4, 32, 4, 4, 32)
    k_ = z(4, 32, 4, 4, 32)
    v_ = z(4, 32, 2, 2, 16)
    gw = z(2, 2, 4, 16, 4, 4)
    d1, d2 = z(65, 4, 16), z(65, 4, 16)
    for n in range(4):
        w[n, 0:16, :, n, 0:16] = f("wq")[n].transpose(2, 0, 1)
        k_[n, 0:16, n, n, 0:16] = f("wk")[n].T
        v_[n, 0:16, n % 2, n // 2] = f("wv")[n].T
        gw[:, :, n, :, n, :] = f("gate_w")[n].reshape(4, 2, 2, 16).transpose(1, 2, 3, 0)
        d1[16 * n:16 * n + 16, n] = f("fc1_w").T
        d2[16 * n:16 * n + 16, n] = f("fc2_w").T
        d1[64, n], d2[64, n] = f("fc1_b"), f("fc2_b")
    t["wqp"] = w.reshape(P, 4, P)
    t["wkp"] = k_.reshape(P, 4, P)
    t["wvp"] = v_.reshape(P, 2, 32)
    t["gwb"] = gw.reshape(2, P, 16).transpose(1, 0, 2)
    t["gateb"] = rep(f("gate_b"))
    for n, k in (("lng", "ln_g"), ("lnb", "ln_b"), ("fng", "fnorm_g"), ("fnb", "fnorm_b")):
        t[n] = rep(np.tile(f(k), 4))
    t["fc1d"], t["fc2d"] = d1.reshape(65, CH), d2.reshape(65, CH)
    t["fgt"] = f("fgate_w").T
    s = np.arange(SIDE)
    causal = np.where(s[None, :] <= s[:, None], 0.0, -1e30).astype(np.float32)
    t["mask"] = np.tile(causal, (2, 8))
    for k, v in t.items():
        assert list(v.shape) == TAIL_W[k], (k, v.shape)
        out["t_" + k] = v
    return {k: np.ascontiguousarray(a) for k, a in out.items()}


def kernel(**inputs):
    import concourse.bacc as bacc
    import numpy as np
    from concourse.bass_utils import run_bass_kernel_spmd

    arrays = layout(inputs)
    nc = bacc.Bacc("TRN2", target_bir_lowering=False, num_devices=1)
    io = {n: nc.dram_tensor("in_" + n, a.shape, F32, kind="ExternalInput").ap() for n, a in arrays.items()}
    io["out"] = nc.dram_tensor("out", [BATCH * SIDE * SIDE], F32, kind="ExternalOutput").ap()
    tower_kernel(nc, io)
    r = run_bass_kernel_spmd(nc, [{"in_" + n: a for n, a in arrays.items()}], core_ids=[0])
    return np.asarray(r.results[0]["out"]).reshape(BATCH, SIDE, SIDE)
```

```python
from contextlib import ExitStack

import concourse.bass as bass
from concourse import mybir

F32 = mybir.dt.float32
ALU = mybir.AluOpType
ACT = mybir.ActivationFunctionType
AX = mybir.AxisListType

P = 128
BATCH, SIDE, CH = 32, 64, 64
PAIRS = BATCH // 2
PIX = SIDE * SIDE
LAYERS = 4
NKX, NKY = 32, 16
CHUNKS = 4
CM = NKX * NKY // CHUNKS
HM = CM // 2
BANK = 512
BN_EPS = 1e-5
HID = 128


TAIL_W = {"wkv": [65, P], "wq2": [65, P], "wproj": [65, CH], "hlp": [65, P], "wqp": [P, 4, P], "wkp": [P, P], "wvp": [P, 2, 32],
          "gwb": [P, 2, 16], "gateb": [P, 16], "kvw": [P, P], "kvb": [P, P], "bd": [P, CH], "lng": [P, CH], "lnb": [P, CH],
          "fng": [P, CH], "fnb": [P, CH], "fc1d": [65, CH], "fc2d": [65, CH], "fgt": [CH, 4], "mask": [P, BANK]}


def tower_kernel(nc, io):
    ctx = ExitStack()
    with ctx:
        def sb(name, shape, dt=F32):
            return ctx.enter_context(nc.sbuf_tensor(name, shape, dt))

        def sem(name):
            return ctx.enter_context(nc.semaphore(name))

        def sems(name):
            return [sem(f"{name}{u}") for u in range(2)]

        field = nc.dram_tensor("field", [PAIRS, P, PIX], F32, kind="Internal").ap()
        colour_modes = nc.dram_tensor("colour_modes", [96, 1024], F32, kind="Internal").ap()
        xmodes = nc.dram_tensor("xmodes", [CHUNKS, 2, BATCH, CH, CM], F32, kind="Internal").ap()
        zmodes = nc.dram_tensor("zmodes", [2, BATCH, NKX, 2, NKY // 2, CH], F32, kind="Internal").ap()

        big = sb("big", [P, 4, PIX])
        ytile = big[:, 0:2, :]
        htile = big[:, 2:4, :]
        xin = big[:, :, :].rearrange("p (u v) (b m) -> p u v b m", u=2, b=BATCH)
        wt = sb("wt", [P, 2, CM, CH])
        work = sb("work", [P, 2 * PIX])
        ht = work[:, 0:PIX].rearrange("p (t c) -> p t c", c=P)
        atile = work[:, PIX:2 * PIX].rearrange("p (u ky rx) -> p u ky rx", u=2, ky=NKY)
        zout = work[:, :].rearrange("p (u m o) -> p u m o", u=2, o=CH)
        gtile = work[:, 0:2048].rearrange("p (x r k) -> p x r k", r=2, k=NKY)
        gflat = work[:, 0:2048]
        att_t = sb("att_t", [P, NKY, P])
        zin_all = sb("zin", [P, 2 * NKY * P])
        zin = zin_all[0:64, :].rearrange("p (u k c) -> p u k c", u=2, k=NKY)
        yt = zin_all[:, 0:16 * P].rearrange("p (s c) -> p s c", c=P)
        xout = sb("xout", [P, 2, CHUNKS, 2, CM])
        ident = sb("ident", [P, P])
        fy = sb("fy", [P, 64])
        fx = sb("fx", [P, 64])
        ix = sb("ix", [64, P])
        iy = sb("iy", [P, P])
        avg = sb("avg", [P, P])
        pw = sb("pw", [P, P])
        vecs = sb("vecs", [P, 3])
        fc0 = sb("fc0", [P, P])
        fc0t = sb("fc0t", [P, 7])
        pw0 = sb("pw0", [P, P])
        fc1 = sb("fc1", [P, 2, P])
        fc1b = sb("fc1b", [P, 2])
        fc2 = sb("fc2", [P, 2, 32])
        fc2b = sb("fc2b", [P, 1])
        stats = sb("stats", [P, PAIRS * 8, 6])
        mv = sb("mv", [P, 2])
        sm = sb("sm", [P, 8])
        bn_scale = sb("bn_scale", [P, 1])
        bn_bias = sb("bn_bias", [P, 1])
        epst = sb("epst", [P, 1])
        scratch = sb("scratch", [P, 1024])
        yout = wt[:, :, :, :].rearrange("p u m o -> p (u m o)")[:, 0:2 * PIX].rearrange("p (u n) -> p u n", u=2)
        moving = (htile, wt[:, :, :, :].rearrange("p u m o -> p (u m o)")[:, 2 * PIX:4 * PIX].rearrange("p (u n) -> p u n", u=2))
        half_work = [work[:, PIX + 2048 * s:PIX + 2048 * s + 2048].rearrange("p (x o) -> p x o", o=CH) for s in range(2)]
        still = (half_work, (att_t[:, :, :].rearrange("p k (a o) -> p (k a) o", o=CH),
                             xout[:, :, :, :, :].rearrange("p u c r (a o) -> p (u c r a) o", o=CH)))
        xs = work[:, 0:32 * 96].rearrange("p (t c) -> p t c", c=96)
        lifted = work[:, PIX:2 * PIX].rearrange("p (u n) -> p u n", u=4)
        xq = big[:, :, :].rearrange("p a (b m) -> p (a b) m", m=1024)
        hidden = work[:, :].rearrange("p (r n) -> p r n", n=BANK)
        towr = att_t[:, :, :].rearrange("p (u q n) c -> p u q (n c)", u=2, q=2)

        free = {"big": 0, "wt": 0}
        pools = {"big": big[:, :, :].rearrange("p a b -> p (a b)"), "wt": wt[:, :, :, :].rearrange("p a b c -> p (a b c)")}

        def view(n, where="big", parts=P):
            at = free[where]
            free[where] += n
            assert free[where] <= 4 * PIX
            return pools[where][0:parts, at:at + n]

        J = PAIRS
        TD = J * CH
        h1t = nc.dram_tensor("h1_rows", [BATCH * SIDE * SIDE], F32, kind="Internal").ap()
        h1 = view(TD); xn = view(TD); xc = view(2 * TD); sq = view(2 * TD)
        kv = view(2 * TD); kn = view(TD); vn = view(TD); kvm = view(TD); ret = view(TD); ga = view(TD)
        h2 = view(TD); sx = view(TD)
        xt = view(2048, "wt", 65); qt = view(2048, "wt"); att_out = view(4 * TD, "wt"); att_T = view(4096, "wt")
        s1 = view(512, "wt"); s2 = view(512, "wt"); sd = view(512, "wt")
        prod = sq; mixed = kn; fxt = view(TD, "wt"); hx = ga; fo = view(TD, "wt")
        x2 = xn
        lg = s1[:, 0:256]; gmax = s2[:, 0:64]; gexp = sd[:, 0:256]; gsum = s2[:, 64:128]
        res = sb("res", [P, CH]); keep = scratch[:, :]
        keepT = qt[0:64, :]
        sxT = work[:, 0:256].rearrange("p (u t) -> p u t", u=2)
        qb = work[:, 256:1280].rearrange("p (u t) -> p u t", u=2)
        kb = work[:, 1280:2304].rearrange("p (u t) -> p u t", u=2)
        vb = work[:, 2304:2304 + 2 * 136].rearrange("p (u i q h o) -> p u i q h o", u=2, i=2, q=2, h=2)
        ex = work[:, 2576:2576 + 2048].rearrange("p (u i t) -> p u i t", u=2, i=2)
        exT = work[:, 4624:4624 + 1024].rearrange("p (i t) -> p i t", i=2)
        mx = work[:, 5648:5680].rearrange("p (u i g) -> p u i g", u=2, i=2)
        rden = work[:, 5680:5712].rearrange("p (u g) -> p u g", u=2)
        tw = {}
        at = 0
        for name, shape in TAIL_W.items():
            n = shape[1] * (shape[2] if len(shape) == 3 else 1)
            tw[name] = zin_all[0:shape[0], at:at + n]
            if len(shape) == 3:
                tw[name] = tw[name].rearrange("p (a b) -> p a b", a=shape[1])
            at += n
        maskb = sb("maskb", [P, BANK], mybir.dt.bfloat16)
        identb = sb("identb", [P, P], mybir.dt.bfloat16)
        unused = sb("unused", [P, 2])
        eps5 = sb("eps5", [P, 1])
        eps8 = sb("eps8", [P, 1])

        fills = {}
        nth = [0] * 8
        for name, banks in (("xT", (0, 1, 2, 3)), ("q", (4, 5, 6, 7)), ("kv", (0, 1, 2, 3)), ("kvm", (4, 5)),
                            ("out", (6, 7)), ("retT", (0, 1, 2, 3)), ("proj", (4, 5)), ("x2T", (0, 1, 2, 3)),
                            ("attT", (0, 1, 2, 3, 4, 5, 6, 7)), ("gate", (0,)), ("fT", (4, 5, 6, 7)), ("fc1", (0, 1, 2, 3)),
                            ("fc2", (4, 5)), ("foT", (0, 1, 2, 3)), ("fg", (4,))):
            for i, b in enumerate(banks):
                fills[name, i] = (b, nth[b])
                nth[b] += 1

        bank = [ctx.enter_context(nc.psum_tensor(f"bank{i}", [P, BANK], F32)) for i in range(8)]

        phase = sem("phase")
        carrier = sem("carrier")
        consts_loaded = sem("consts_loaded"); params_loaded = sem("params_loaded")
        colours_loaded = sem("colours_loaded"); colour_y_done = sem("colour_y_done"); colour_y_read = sem("colour_y_read")
        colour_turned = sem("colour_turned"); colour_turned_read = sem("colour_turned_read")
        colour_x_done = sem("colour_x_done"); colour_x_read = sem("colour_x_read"); colour_modes_stored = sem("colour_modes_stored")
        lift_clear = sem("lift_clear"); lift_loaded = sem("lift_loaded"); lift_done = sem("lift_done"); lift_read = sem("lift_read")
        lift_stored = [sem(f"lift_stored{u}") for u in range(4)]
        pw0_clear = sem("pw0_clear"); pw0_folded = sem("pw0_folded"); pw0_ready = sem("pw0_ready")
        colour_rows_clear = sem("colour_rows_clear"); colour_field_loaded = sems("colour_field_loaded")
        field_loaded = sems("field_loaded"); fw_activated = sem("fw_activated")
        fw_turned = sem("fw_turned"); fw_turned_read = sem("fw_turned_read"); fw_y_done = sem("fw_y_done"); fw_y_read = sem("fw_y_read")
        fw_back = sem("fw_back"); fw_back_read = sem("fw_back_read"); fw_x_turned = sem("fw_x_turned"); fw_x_turned_read = sem("fw_x_turned_read")
        fw_x_done = sem("fw_x_done"); fw_x_read = sem("fw_x_read"); fw_modes_stored = sems("fw_modes_stored")
        mix_weights_loaded = [sems("mix_weights0_loaded"), sems("mix_weights1_loaded")]
        mix_modes_loaded = sems("mix_modes_loaded"); mix_negated = sem("mix_negated"); mix_copied = sem("mix_copied")
        mix_done = sem("mix_done"); mix_read = sems("mix_read")
        mix_stored = sems("mix_stored")
        transform_laid = sems("transform_laid"); weights_laid = sem("weights_laid"); inv_modes_loaded = sems("inv_modes_loaded")
        inv_activated = sem("inv_activated"); inv_x_done = sem("inv_x_done"); inv_x_read = sem("inv_x_read")
        inv_turned = sem("inv_turned"); inv_turned_read = sem("inv_turned_read"); inv_done = sem("inv_done"); inv_read = sem("inv_read")
        inv_measured = sem("inv_measured"); field_stored = sems("field_stored")
        norm_step = sem("norm_step"); norm_shared = sem("norm_shared"); norm_root = sem("norm_root")
        last_activated = sem("last_activated"); hidden_done = sem("hidden_done"); hidden_read = sem("hidden_read")
        tower_done = sem("tower_done"); tower_read = sem("tower_read"); tower_stored = sems("tower_stored")
        tower_free = sem("tower_free"); tower_in_dram = sem("tower_in_dram")
        full = [sem(f"full{b}") for b in range(8)]
        empty = [sem(f"empty{b}") for b in range(8)]
        tail_loaded = sem("tail_loaded"); h1_loaded = sem("h1_loaded"); out_stored = sem("out_stored")
        chain = sem("chain")
        clear = sem("clear"); masks = sem("masks")
        ev = {n: sem("ev_" + n) for n in (
            "xn", "var", "rstd", "xT", "qT", "kn", "kvm", "ret", "retT", "ga", "x2", "x2T", "att", "attT", "lg", "gexp",
            "fx", "fxT", "hx", "fo", "foT", "fl", "fexp", "done")}
        ffn_in_done = sem("ffn_in_done"); ffn_in_read = sem("ffn_in_read"); ffn_q_done = sem("ffn_q_done"); ffn_q_read = sem("ffn_q_read")
        ffn_k_done = sem("ffn_k_done"); ffn_k_read = sem("ffn_k_read"); ffn_v_done = sem("ffn_v_done"); ffn_v_read = sem("ffn_v_read")
        ffn_scores_done = sem("ffn_scores_done"); ffn_scores_read = sem("ffn_scores_read"); ffn_max_done = sem("ffn_max_done")
        ffn_exp_done = sem("ffn_exp_done"); ffn_turned = sem("ffn_turned"); ffn_turned_read = sem("ffn_turned_read")
        ffn_out_done = sem("ffn_out_done"); ffn_out_read = sem("ffn_out_read"); ffn_recip_done = sem("ffn_recip_done")

        def filled(eng, name, i):
            b, n = fills[name, i]
            eng.wait_ge(full[b], n + 1)
            return bank[b]

        def to_fill(name, i):
            b, n = fills[name, i]
            if n:
                nc.tensor.wait_ge(empty[b], n)
            return bank[b]

        def skewed3(eng, step):
            step(0, 0, True, False, False)
            step(1, 1, True, True, False)
            with eng.Fori(0, J // 2 - 1) as i:
                step(i * 2 + 2, 0, True, True, True)
                step(i * 2 + 3, 1, True, True, True)
            step(J, 0, False, True, True)
            step(J + 1, 1, False, False, True)

        CONSTS = 11
        PHASES = 3

        def apart(eng):
            eng.sem_inc(carrier, 1)

        def barrier(eng, k):
            apart(eng)
            eng.drain().then_inc(phase, 1)
            eng.wait_ge(phase, k * 5)
            apart(eng)

        def skewed(eng, step):
            step(0, 0, True, False, True)
            with eng.Fori(0, PAIRS // 2 - 1) as i:
                step(i * 2 + 1, 1, True, True, True)
                step(i * 2 + 2, 0, True, True, True)
            step(PAIRS - 1, 1, True, True, False)
            step(PAIRS, 0, False, True, False)

        def pairs(eng, body, n=PAIRS):
            with eng.Fori(0, n // 2) as i:
                for u in range(2):
                    body(i * 2 + u, u, i)

        def later_pairs(eng, body):
            with eng.Fori(0, PAIRS // 2 - 1) as i:
                for u in range(2):
                    body(i * 2 + (2 + u), u, i)

        def wait_stored(eng, l):
            for u in range(2):
                eng.wait_ge(field_stored[u], (l + 1) * 8 * PAIRS + 16)
            apart(eng)

        block = ctx.enter_context(nc.Block())

        @block.sync
        def _(sp):
            sp.dma_start(xs, io["xs"]).then_inc(colours_loaded, 16)
            for dst, src in ((ident, "c_ident"), (fy, "c_fy"), (fx, "c_fx"), (ix, "c_ix"), (iy, "c_iy"), (avg, "c_avg"),
                             (fc1b, "fc1b"), (fc2b, "fc2b"), (fc0t, "fc0t")):
                sp.dma_start(dst[:, :], io[src]).then_inc(consts_loaded, 16)
            for dst, src in ((fc1, "fc1"), (fc2, "fc2")):
                sp.dma_start(dst[:, :, :], io[src]).then_inc(consts_loaded, 16)
            sp.wait_ge(lift_clear, 3)
            sp.dma_start(fc0[0:7, :], io["fc0"]).then_inc(lift_loaded, 16)
            sp.dma_start(xq[6:7, :, :], io["dc"]).then_inc(lift_loaded, 16)

            barrier(sp, 1)
            sp.dma_start(xq[0:6, :, :], colour_modes.rearrange("(n q) m -> q n m", q=6)).then_inc(lift_loaded, 16)
            barrier(sp, 2)

            def load_field(n, u):
                apart(sp)
                sp.dma_start(ytile[:, u, :], field[bass.ds(n, 1)].rearrange("a p m -> p (a m)")).then_inc(field_loaded[u], 16)

            def forward_loads(m):
                wait_stored(sp, m)

                def load_y(n, u, i):
                    sp.wait_ge(fw_activated, (m * PAIRS + n) * 4 + 4)
                    load_field(n, u)
                later_pairs(sp, load_y)
                barrier(sp, m * PHASES + 5)

            def layer(l, m):
                def load_modes(g, u, i):
                    G = l * CHUNKS + g
                    sp.wait_ge(mix_done, G * 8 + 8)
                    apart(sp)
                    for half, v in ((0, 1), (1, 0)):
                        src = xmodes[bass.ds(g, 1), v].rearrange("a b c m -> c (a b) m")
                        sp.dma_start(xin[CH * half:CH * half + CH, u, 1], src).then_inc(mix_modes_loaded[u], 16)
                pairs(sp, load_modes, CHUNKS)
                for s in range(2):
                    sp.dma_start(pw[CH * s:CH * s + CH, CH * s:CH * s + CH], io["pw"][bass.ds(l, 1)].rearrange("a i o -> (a i) o")).then_inc(
                        params_loaded, 16)
                sp.dma_start(vecs[:, :], io["vecs"][bass.ds(l, 1)].rearrange("a p k -> (a p) k")).then_inc(params_loaded, 16)
                if m is not None:
                    sp.wait_ge(mix_done, (l * CHUNKS + 2) * 8 + 8 + 16)
                    load_field(0, 0)
                barrier(sp, l * PHASES + 3)
                def load_modes_back(n, u):
                    sp.wait_ge(inv_x_done, (l * PAIRS + n) * 4 + 4)
                    apart(sp)
                    for v in range(2):
                        for b in range(2):
                            zs = zmodes[v, bass.ds(n * 2 + b, 1)].rearrange("a k q y o -> (a k) (q y) o")
                            sp.dma_start(zin[NKX * v:NKX * v + NKX, u, :, CH * b:CH * b + CH], zs).then_inc(
                                inv_modes_loaded[u], 16)

                def load_x(n, u):
                    sp.wait_ge(inv_done, (l * PAIRS + n) * 8 + 8)
                    apart(sp)
                    for s in range(2):
                        sp.dma_start(moving[s][64 * s:64 * s + 7, u, :], io["x"][bass.ds(n, 1)].rearrange("a p m -> p (a m)")).then_inc(
                            colour_field_loaded[u], 16)

                def load_transform(u):
                    for s in range(2):
                        src = io["c_iy"][0:64].rearrange("p (a n) -> p a n", a=1).to_broadcast([64, SIDE // 2, P])
                        dst = moving[s][64 - 64 * s:128 - 64 * s, u, :].rearrange("p (x n) -> p x n", n=P)
                        sp.dma_start(dst, src).then_inc(transform_laid[u], 16)

                for u in range(2):
                    load_modes_back(u, u)
                load_transform(0)
                if m is not None:
                    load_field(1, 1)
                load_transform(1)
                if m is None:
                    for u in range(2):
                        sp.wait_ge(colour_rows_clear, 2 * u + 2)
                        load_x(u, u)

                def load_back(n, u, i):
                    load_modes_back(n, u)
                    if m is None:
                        load_x(n, u)
                    else:
                        sp.wait_ge(inv_activated, m * PAIRS + n + 1)
                        load_field(n, u)
                later_pairs(sp, load_back)
                if m is not None:
                    sp.wait_ge(inv_activated, m * PAIRS + PAIRS + 2)
                    apart(sp)
                for u in range(2):
                    sp.wait_ge(field_stored[u], l * 8 * PAIRS + 32)
                    load_field(u, u)
                barrier(sp, l * PHASES + 4)

            layer(0, None)
            with sp.Fori(0, LAYERS - 1) as m:
                forward_loads(m)
                layer(m + 1, m)

            wait_stored(sp, LAYERS - 1)

            def load_last(n, u, i):
                sp.wait_ge(last_activated, n + 1)
                load_field(n, u)
            later_pairs(sp, load_last)
            for name in TAIL_W:
                sp.dma_start(tw[name], io["t_" + name]).then_inc(tail_loaded, 16)
            barrier(sp, LAYERS * PHASES + 2)
            sp.wait_ge(tower_in_dram, 1)
            sp.dma_start(h1.rearrange("p (j c) -> p j c", j=J), h1t.rearrange("(j p c) -> p j c", j=J, p=P)).then_inc(
                h1_loaded, 16)
            sp.wait_ge(ev["done"], 1)
            sp.dma_start(io["out"].rearrange("(j p c) -> p j c", j=J, p=P), h2.rearrange("p (j c) -> p j c", j=J)).then_inc(
                out_stored, 16)
            sp.wait_ge(out_stored, 16)

        @block.gpsimd
        def _(pool):
            nc.gpsimd.memset(fc0[:, :], 0.0).then_inc(lift_clear, 1)
            nc.gpsimd.memset(xq[:, 8:16].rearrange("p n m -> p (n m)"), 0.0).then_inc(lift_clear, 1)
            nc.gpsimd.memset(pw0[:, :], 0.0).then_inc(pw0_clear, 1)
            nc.gpsimd.memset(pw[:, :], 0.0)
            nc.gpsimd.memset(epst[:, :], BN_EPS)

            def load_w(l, g, u, h, ahead):
                G = l * CHUNKS + g
                if not ahead:
                    pool.wait_ge(mix_done, G * 8 + 4 + 4 * h)
                    apart(pool)
                dst = wt[:, u, HM * h:HM * h + HM]
                pool.dma_start(dst, io["w"][bass.ds(G, 1), :, HM * h:HM * h + HM].rearrange("a p m o -> (a p) m o")).then_inc(
                    mix_weights_loaded[u][h], 16)

            def layer(l, first):
                for u in range(2):
                    for h in range(2):
                        load_w(l, 2 + u, u, h, False)
                barrier(pool, l * PHASES + 3)
                if first:
                    for u in range(2):
                        for s in range(2):
                            pool.memset(moving[s][64 * s:64 * s + 64, u, :], 0.0).then_inc(colour_rows_clear, 1)
                barrier(pool, l * PHASES + 4)
            pool.wait_ge(consts_loaded, 16 * CONSTS)
            for u in range(2):
                for h in range(2):
                    load_w(0, u, u, h, True)
            barrier(pool, 1)
            barrier(pool, 2)
            layer(0, True)
            with pool.Fori(0, LAYERS - 1) as m:
                wait_stored(pool, m)
                for u in range(2):
                    for h in range(2):
                        pool.wait_ge(fw_activated, (m * PAIRS + 2 * u + h + 1) * 4 + 8)
                        apart(pool)
                        load_w(m + 1, u, u, h, True)
                barrier(pool, m * PHASES + 5)
                layer(m + 1, False)

            def store_tower(n, u, i):
                pool.wait_ge(tower_read, n * 2 + 2 + 4)
                apart(pool)
                for s in range(2):
                    dst = h1t[bass.ds(n * 8192 + s * PIX, PIX)].rearrange("(q i m) -> i q m", q=2, i=4)
                    pool.dma_start(dst, towr[s:s + 97:32, u]).then_inc(tower_stored[u], 16)
                pool.wait_ge(tower_stored[u], i * 32 + 32)
                pool.sem_inc(tower_free, 1)
            pool.sem_inc(tower_free, 2)
            pairs(pool, store_tower)
            pool.sem_inc(tower_in_dram, 1)
            barrier(pool, LAYERS * PHASES + 2)
            n_clear = 0
            for dst, value in [(vb.rearrange("p u i q h o -> p (u i q h o)"), 0.0), (kb.rearrange("p u t -> p (u t)"), 0.0), (xt[64:65, :], 1.0), (eps5[:, :], 1e-5), (eps8[:, :], 1e-8)] + [
                    (vb[64 * h:64 * h + 64, u, :, :, h, 16:17].rearrange("p i q o -> p (i q) o"), 1.0) for h in range(2) for u in range(2)]:
                nc.gpsimd.memset(dst, value).then_inc(clear, 1)
                n_clear += 1
                pool.wait_ge(clear, n_clear)

        @block.tensor
        def _(pe):
            pe.sem_inc(fw_turned, 16)
            pe.sem_inc(mix_done, 16)
            pe.sem_inc(fw_back, 4)
            pe.sem_inc(inv_x_done, 8)
            pe.sem_inc(inv_done, 16)
            pe.sem_inc(tower_done, 2)
            pe.wait_ge(consts_loaded, 16 * CONSTS)

            def warm_up(n):
                for _ in range(n):
                    pe.matmul(bank[0][:, 0:P], avg[:, :], iy[:, :], start=True, stop=True)

            pe.wait_ge(colours_loaded, 16)
            for g in range(4):
                for t in range(8):
                    mm = pe.matmul(bank[g][0:96, t * 64:(t + 1) * 64], xs[:, 8 * g + t, :], fy[:, :], start=True, stop=True)
                mm.then_inc(colour_y_done, 1)
            pe.wait_ge(colour_y_read, 4)
            for j in range(4):
                for t in range(4):
                    mm = pe.transpose(bank[4 + j][:, t * P:t * P + 96], atile[0:96, 0, 4 * j + t, :], ident[0:96, 0:96])
                mm.then_inc(colour_turned, 1)
            for g in range(2):
                pe.wait_ge(colour_turned_read, 2 * g + 2)
                for t in range(8):
                    mm = pe.matmul(bank[g][0:96, t * 64:(t + 1) * 64], att_t[:, 8 * g + t, 0:96], fx[:, :], start=True, stop=True)
                mm.then_inc(colour_x_done, 1)
            barrier(pe, 1)

            pe.wait_ge(lift_loaded, 48)

            def lift(n, u, i):
                for g in range(2):
                    pe.wait_ge(lift_read, n * 2 + g + 1)
                    pe.matmul(bank[2 * u + g][:, :], fc0[:, :], xq[:, bass.ds(n, 1), g * BANK:(g + 1) * BANK].rearrange("p a m -> p (a m)"),
                              start=True, stop=True).then_inc(lift_done, 1)
            pairs(pe, lift)
            barrier(pe, 2)

            def forward(m):
                def fwd(k, u, front, back, ahead):
                    N = m * PAIRS + k
                    B = N + (-1)
                    ub = 1 - u

                    def T(j, later=0):
                        pe.wait_ge(fw_turned_read, (N + later) * 8 + j + 1)
                        if j % 2 == 0:
                            pe.wait_ge(fw_activated, (N + later) * 4 + j // 2 + 1 + 8)
                        for t in range(4):
                            s = 4 * j + t
                            mm = pe.transpose(bank[j % 2][:, t * P:(t + 1) * P], htile[:, ub if later else u, s * P:(s + 1) * P],
                                    ident[:, :])
                        mm.then_inc(fw_turned, 1)

                    def Y(j):
                        pe.wait_ge(fw_turned_read, N * 8 + 2 * j + 4)
                        pe.wait_ge(fw_y_read, N * 4 + j + 1)
                        for odd in range(2):
                            src = ht[:, 8 * j:8 * j + 8, :].rearrange("p (t o) c -> p o t c", o=2)[:, odd]
                            mm = pe.matmul(bank[2 + j % 2][64 * odd:64 * odd + 64, :], fy[:, :], src, start=True, stop=True)
                        mm.then_inc(fw_y_done, 1)

                    def U(j):
                        pe.wait_ge(fw_y_read, N * 4 + j + 1 + 2)
                        pe.wait_ge(fw_back_read, N * 4 + j + 1)
                        for t in range(4):
                            mm = pe.transpose(bank[4 + j % 2][:, t * P:(t + 1) * P], yt[:, 4 * j + t, :], ident[:, :])
                        mm.then_inc(fw_back, 1)

                    def R(j):
                        if j == 0:
                            pe.wait_ge(fw_back_read, B * 4 + 6)
                        pe.wait_ge(fw_x_turned_read, B * 4 + j + 1)
                        for t in range(4):
                            mm = pe.transpose(bank[6][:, t * P:(t + 1) * P], atile[:, ub, 4 * j + t, :], ident[:, :])
                        mm.then_inc(fw_x_turned, 1)

                    def X(g):
                        pe.wait_ge(fw_x_turned_read, B * 4 + 2 * g + 3)
                        pe.wait_ge(fw_x_read, B * 2 + g + 1)
                        for t in range(8):
                            mm = pe.matmul(bank[7][:, t * 64:(t + 1) * 64], att_t[:, 8 * g + t, :], fx[:, :],
                                    start=True, stop=True)
                        mm.then_inc(fw_x_done, 1)

                    if isinstance(k, int) and k == 0:
                        T(0); T(1)
                    if back: R(0)
                    if front: T(2); T(3); Y(0)
                    if back: R(1)
                    if front: T(4); T(5); Y(1); U(0)
                    if back: R(2)
                    if front: T(6); T(7); Y(2); U(1)
                    if back: R(3); X(0)
                    if front: Y(3); U(2)
                    if ahead: T(0, 1)
                    if front: U(3)
                    if ahead: T(1, 1)
                    if back: X(1)
                skewed(pe, fwd)
                barrier(pe, m * PHASES + 5)

            def layer(l, m):
                def mix(g, u, i):
                    G = l * CHUNKS + g
                    M = l * (CHUNKS // 2) + i
                    pe.wait_ge(mix_modes_loaded[u], M * 32 + 32)
                    pe.wait_ge(mix_read[0], G * 4 + 1)
                    apart(pe)
                    warm_up(12)
                    pe.wait_ge(mix_weights_loaded[u][0], M * 16 + 16)
                    pe.wait_ge(mix_negated, G + 1)
                    pe.wait_ge(mix_copied, G + 1)
                    for k in range(8):
                        if k == 4:
                            pe.wait_ge(mix_weights_loaded[u][1], M * 16 + 16)
                        pe.wait_ge(mix_read[k % 2], G * 4 + k // 2 + 1)
                        for t in range(8):
                            for par_ in range(2):
                                y0 = 2 * (8 * k + t) % 16 + par_
                                x0 = (8 * k + t) // 8
                                mm = pe.matmul(bank[k][64 * par_:64 * par_ + 64, t * 64:(t + 1) * 64],
                                               xin[:, u, :, :, y0 * 8 + x0], wt[:, u, x0 * 16 + y0, :], start=True, stop=True)
                        mm.then_inc(mix_done, 1)
                pairs(pe, mix, CHUNKS)
                barrier(pe, l * PHASES + 3)
                pe.wait_ge(params_loaded, l * 48 + 48)
                apart(pe)
                if m is not None:
                    warm_up(10)
                if m is None:
                    pe.wait_ge(pw0_clear, 1)
                    for s in range(2):
                        mm = pe.matmul(bank[0][64 * s:64 * s + 7, 0:P], fc0t[:, :], pw[:, :], start=True, stop=True)
                    mm.then_inc(pw0_folded, 1)
                    pe.wait_ge(pw0_ready, 2)

                def inv(k, u, front, back, ahead):
                    N = l * PAIRS + k
                    B = N + (-1)
                    ub = 1 - u

                    def K(j):
                        if j == 0:
                            pe.wait_ge(inv_modes_loaded[u], zcount(l, k, u))
                        pe.wait_ge(inv_x_read, N * 4 + j + 1)
                        for t in range(4):
                            mm = pe.matmul(bank[j % 2][:, t * P:(t + 1) * P], zin[:, u, t % 2 * 8 + 2 * j + t // 2, :], ix[:, :],
                                    start=True, stop=True)
                        mm.then_inc(inv_x_done, 1)

                    def T(j):
                        if j == 0:
                            pe.wait_ge(inv_x_read, N * 4 + 6)
                        pe.wait_ge(inv_turned_read, N * 8 + j + 1)
                        o = bank[2 + j % 2]
                        for t in range(4):
                            x = 4 * j + t
                            cols = slice(t * P, t * P + P)
                            if x < SIDE // 2 - 1:
                                mm = pe.transpose(o[:, cols], gflat[:, 64 * x:64 * x + 128], ident[:, :])
                            else:
                                pe.matmul(o[0:64, cols], gflat[:, 64 * x:64 * x + 64], ident[:, :], start=True, stop=True)
                                mm = pe.matmul(o[64:128, cols], gflat[:, 0:64], ident[:, :], start=True, stop=True)
                        mm.then_inc(inv_turned, 1)

                    def F(f):
                        if f == 0:
                            pe.wait_ge(transform_laid[ub], l * 32 + 32)
                            pe.wait_ge(weights_laid, l * 4 + 4)
                            if m is None:
                                pe.wait_ge(colour_field_loaded[ub], (k + (-1) - ub) * 16 + 32)
                            else:
                                pe.wait_ge(inv_activated, m * PAIRS + k + 2)
                            pe.wait_ge(inv_turned_read, B * 8 + 10)
                        pe.wait_ge(inv_read, B * 8 + f + 1)
                        o = bank[4 + f % 4]
                        for t in range(4):
                            x = 4 * f + t
                            for s in range(2):
                                slot = x if s else (x - 1) % (SIDE // 2)
                                mm = pe.matmul(o[64 * s:64 * s + 64, t * P:(t + 1) * P], still[ub][s][:, slot, :],
                                               moving[s][:, ub, x * P:(x + 1) * P], start=True, stop=True)
                        mm.then_inc(inv_done, 1)

                    if back: F(0)
                    if front: K(0); K(1)
                    if back: F(1)
                    if front: K(2); K(3)
                    if back: F(2)
                    if front: T(0); T(1)
                    if back: F(3)
                    if front: T(2)
                    if back: F(4)
                    if front: T(3); T(4)
                    if back: F(5)
                    if front: T(5)
                    if back: F(6)
                    if front: T(6); T(7)
                    if back: F(7)
                skewed(pe, inv)
                pe.wait_ge(norm_step, l * 8 + 2)
                pe.matmul(bank[0][:, 0:1], avg[:, :], mv[:, 0:1], start=True, stop=True).then_inc(norm_shared, 1)
                pe.wait_ge(norm_step, l * 8 + 5)
                pe.matmul(bank[0][:, 1:2], avg[:, :], sm[:, 3:4], start=True, stop=True).then_inc(norm_shared, 1)
                barrier(pe, l * PHASES + 4)

            def zcount(l, k, u):
                return (l * PAIRS + k - u) * 32 + 64
            layer(0, None)
            with pe.Fori(0, LAYERS - 1) as m:
                forward(m)
                layer(m + 1, m)

            def last(k, u, front, back, ahead):
                def C(r):
                    pe.wait_ge(hidden_read, k * 16 + r + 1)
                    c, half = r // 2, r % 2
                    pe.matmul(bank[r % 4][:, :], fc1[:, half, :], htile[:, u, c * BANK:(c + 1) * BANK], start=True, stop=True).then_inc(
                        hidden_done, 1)

                def O(n, un, q):
                    pe.wait_ge(hidden_read, n * 16 + 8 * q + 8 + 4)
                    pe.wait_ge(tower_read, n * 2 + q + 1)
                    for half in range(2):
                        for i in range(4):
                            mm = pe.matmul(bank[4 + 2 * un + q][32 * i:32 * i + 32, :], fc2[:, half, :], hidden[:, (4 * q + i) * 2 + half, :],
                                           start=(half == 0), stop=(half == 1), skip_group_check=True)
                    mm.then_inc(tower_done, 1)
                if front:
                    pe.wait_ge(last_activated, k + 3)
                    for r in range(4):
                        C(r)
                if back:
                    O(k + (-1), 1 - u, 1)
                if front:
                    for r in range(4, 12):
                        C(r)
                    O(k, u, 0)
                    for r in range(12, 16):
                        C(r)
            skewed(pe, last)
            barrier(pe, LAYERS * PHASES + 2)

            def stage_T(name, src, cols=CH):
                for j in range(src.shape[1] // cols):
                    b = j // 4
                    o = to_fill(name, b) if j % 4 == 0 else bank[fills[name, b][0]]
                    mm = pe.transpose(o[0:cols, (j % 4) * P:(j % 4 + 1) * P], src[:, j * cols:(j + 1) * cols], ident[:, :])
                    if j % 4 == 3:
                        mm.then_inc(full[fills[name, b][0]], 1)

            def stage_W(name, w, src, n, k):
                per = min(BANK // n, J)
                for j in range(J):
                    b = j // per
                    o = to_fill(name, b) if j % per == 0 else bank[fills[name, b][0]]
                    mm = pe.matmul(o[:, (j % per) * n:(j % per + 1) * n], src[0:k, j * P:(j + 1) * P], w, start=True, stop=True)
                    if j % per == per - 1:
                        mm.then_inc(full[fills[name, b][0]], 1)

            def stage_F(name, w, src, m):
                for b in range(4):
                    o = to_fill(name, b)
                    pe.matmul(o[0:m, :], w, src[:, b * BANK:(b + 1) * BANK], start=True, stop=True).then_inc(
                        full[fills[name, b][0]], 1)

            pe.wait_ge(tail_loaded, 16 * len(TAIL_W))
            pe.wait_ge(ev["xn"], 1)
            stage_T("xT", xn)
            pe.wait_ge(clear, 9)
            pe.wait_ge(ev["xT"], 4)
            stage_W("kv", tw["wkv"][:, :], xt, P, 65)
            stage_F("q", tw["wq2"][:, :], xt[:, :], P)
            pe.wait_ge(ev["kn"], 1)
            for j in range(J):
                o = to_fill("kvm", j // 8) if j % 8 == 0 else bank[fills["kvm", j // 8][0]]
                for i in range(2):
                    half = slice(64 * i, 64 * i + 64)
                    mm = pe.matmul(o[half, (j % 8) * CH:(j % 8 + 1) * CH], kn[half, j * CH:(j + 1) * CH], vn[half, j * CH:(j + 1) * CH],
                                   start=True, stop=True)
                if j % 8 == 7:
                    mm.then_inc(full[fills["kvm", j // 8][0]], 1)
            pe.wait_ge(ev["qT"], 4)
            pe.wait_ge(ev["kvm"], 2)
            for j in range(J):
                o = to_fill("out", j // 8) if j % 8 == 0 else bank[fills["out", j // 8][0]]
                for i in range(2):
                    half = slice(64 * i, 64 * i + 64)
                    mm = pe.matmul(o[half, (j % 8) * CH:(j % 8 + 1) * CH], qt[half, j * P + 64 * i:j * P + 64 * i + 64],
                                   kvm[half, j * CH:(j + 1) * CH], start=True, stop=True)
                if j % 8 == 7:
                    mm.then_inc(full[fills["out", j // 8][0]], 1)
            pe.wait_ge(ev["ret"], 1)
            stage_T("retT", ret)
            pe.wait_ge(ev["retT"], 4)
            stage_W("proj", tw["wproj"][:, :], xt, CH, 65)
            pe.wait_ge(ev["x2"], 1)
            stage_T("x2T", x2)
            pe.wait_ge(ev["x2T"], 4)
            pe.wait_ge(ev["ga"], 2)
            pe.wait_ge(masks, 2)

            def pair_step(k, u, proj, score, comb):
                u1 = 1 - u

                def project():
                    pe.wait_ge(ffn_in_read, k + 1)
                    pe.matmul(bank[0][:, 0:P], tw["hlp"][:, :], xt[:, bass.ds(k * P, P)], start=True, stop=True).then_inc(
                        ffn_in_done, 1)

                def project2():
                    pe.wait_ge(ffn_in_read, k + 2)
                    pe.wait_ge(ffn_q_read, k + 1)
                    for e in range(4):
                        mm = pe.matmul(bank[1][:, e * P:(e + 1) * P], tw["wqp"][:, e, :], sxT[:, u, :], start=True, stop=True)
                    mm.then_inc(ffn_q_done, 1)
                    pe.wait_ge(ffn_k_read, k + 1)
                    pe.matmul(bank[2][:, 0:P], tw["wkp"][:, :], sxT[:, u, :], start=True, stop=True).then_inc(ffn_k_done, 1)
                    pe.wait_ge(ffn_v_read, k + 1)
                    for i in range(2):
                        for h in range(2):
                            pe.matmul(bank[3][64 * h:64 * h + 64, i * 32:(i + 1) * 32], sxT[:, u, 64 * i:64 * i + 64], tw["wvp"][:, h, :],
                                      start=True, stop=True)
                    pe.transpose(bank[3][:, P:2 * P], sxT[:, u, :], ident[:, :]).then_inc(ffn_v_done, 1)

                def scores(i):
                    B = k + (-1)
                    if i == 0:
                        pe.wait_ge(ffn_q_read, B + 2)
                        pe.wait_ge(ffn_k_read, B + 2)
                    pe.wait_ge(ffn_scores_read, B * 2 + i + 1)
                    o = bank[4 + i]
                    pe.matmul(o[:, :], identb[:, :], maskb[:, :], start=True, stop=True)
                    for q in range(2):
                        mm = pe.matmul(o[:, q * 256:(q + 1) * 256], qb[:, u1, i * 256 + q * P:i * 256 + (q + 1) * P],
                                       kb[:, u1, i * 256:(i + 1) * 256], start=False, stop=True, skip_group_check=True)
                    mm.then_inc(ffn_scores_done, 1)

                def turn(i):
                    C = k + (-2)
                    pe.wait_ge(ffn_exp_done, C * 2 + i + 1)
                    pe.wait_ge(ffn_turned_read, C * 2 + i + 1)
                    for q in range(4):
                        mm = pe.transpose(bank[6][:, q * P:(q + 1) * P], ex[:, u, i, q * P:(q + 1) * P], ident[:, :])
                    mm.then_inc(ffn_turned, 1)

                def combine(i):
                    C = k + (-2)
                    pe.wait_ge(ffn_turned_read, C * 2 + i + 2)
                    if i == 0:
                        pe.wait_ge(ffn_v_read, C + 2)
                        pe.wait_ge(ffn_out_read, C + 1)
                    for q in range(2):
                        for h in range(2):
                            at = ((i * 2 + q) * 2 + h) * 34
                            mm = pe.matmul(bank[7][:, at:at + 34], exT[:, i, (q * 2 + h) * P:(q * 2 + h + 1) * P],
                                           vb[:, u, i, h].rearrange("p h o -> p (h o)"), start=True, stop=True)
                    if i == 1:
                        mm.then_inc(ffn_out_done, 1)
                if proj: project()
                if comb: turn(0)
                if score: scores(0)
                if proj: project2()
                if comb: combine(0); turn(1)
                if score: scores(1)
                if comb: combine(1)
            skewed3(pe, pair_step)

            pe.wait_ge(ev["att"], 1)
            stage_T("attT", att_out, P)
            pe.wait_ge(ev["attT"], 8)
            o = to_fill("gate", 0)
            for j in range(J):
                for h in range(2):
                    mm = pe.matmul(o[:, j * 16:(j + 1) * 16], att_T[:, (2 * j + h) * P:(2 * j + h + 1) * P], tw["gwb"][:, h, :],
                                   start=(h == 0), stop=(h == 1))
            mm.then_inc(full[fills["gate", 0][0]], 1)
            pe.wait_ge(ev["fx"], 1)
            stage_T("fT", fxt)
            pe.wait_ge(ev["fxT"], 4)
            stage_F("fc1", tw["fc1d"][:, :], xt[:, :], CH)
            pe.wait_ge(ev["hx"], 4)
            stage_W("fc2", tw["fc2d"][:, :], xt, CH, 65)
            pe.wait_ge(ev["fo"], 1)
            stage_T("foT", fo)
            pe.wait_ge(ev["foT"], 4)
            o = to_fill("fg", 0)
            for j in range(J):
                mm = pe.matmul(o[:, j * 4:(j + 1) * 4], xt[0:64, j * P:(j + 1) * P], tw["fgt"][:, :], start=True, stop=True)
            mm.then_inc(full[fills["fg", 0][0]], 1)

        @block.vector
        def _(dve):
            dve.sem_inc(fw_turned_read, 2)
            dve.sem_inc(fw_x_turned_read, 1)
            dve.sem_inc(fw_y_read, 2)
            dve.sem_inc(mix_read[1], 4)
            dve.sem_inc(inv_x_read, 2)
            dve.sem_inc(inv_turned_read, 2)
            dve.sem_inc(inv_measured, 2)
            dve.sem_inc(tower_read, 4)
            dve.memset(xq[:, 0:8].rearrange("p n m -> p (n m)"), 0.0).then_inc(lift_clear, 1)
            for j in range(4):
                dve.wait_ge(colour_turned, j + 1)
                src = bank[4 + j][:, :].rearrange("p (t c) -> p t c", c=P)[:, :, 0:96]
                dve.tensor_copy(att_t[:, 4 * j:4 * j + 4, 0:96], src).then_inc(colour_turned_read, 1)
            barrier(dve, 1)
            barrier(dve, 2)

            def forward(m):
                def fwd(k, u, front, back, ahead):
                    N = m * PAIRS + k
                    B = N + (-1)

                    def T(j, later=0):
                        dve.wait_ge(fw_turned, (N + later) * 8 + j + 1 + 16)
                        dve.tensor_copy(ht[:, 4 * j:4 * j + 4, :].rearrange("p t c -> p (t c)"), bank[j % 2][:, :]).then_inc(
                            fw_turned_read, 1)

                    def C(j):
                        dve.wait_ge(fw_y_done, N * 4 + j + 1)
                        dve.wait_ge(fw_back, N * 4 + j + 1)
                        dve.tensor_copy(yt[:, 4 * j:4 * j + 4, :].rearrange("p s c -> p (s c)"), bank[2 + j % 2][:, :]).then_inc(
                            fw_y_read, 1)

                    def R(j):
                        dve.wait_ge(fw_x_turned, B * 4 + j + 1)
                        dve.tensor_copy(att_t[:, 4 * j:4 * j + 4, :].rearrange("p t c -> p (t c)"), bank[6][:, :]).then_inc(
                            fw_x_turned_read, 1)
                    if isinstance(k, int) and k == 0:
                        T(0); T(1)
                    if back: R(0)
                    if front: T(2); T(3); C(0)
                    if back: R(1)
                    if front: T(4); T(5); C(1)
                    if back: R(2)
                    if front: T(6); T(7); C(2)
                    if back: R(3)
                    if front: C(3)
                    if ahead: T(0, 1); T(1, 1)
                skewed(dve, fwd)
                barrier(dve, m * PHASES + 5)

            def layer(l, m):
                def turn(g):
                    u = g % 2
                    dve.wait_ge(mix_modes_loaded[u], (l * (CHUNKS // 2) + g // 2) * 32 + 32)
                    dve.tensor_copy(xin[0:CH, u, 0].rearrange("p b m -> p (b m)"), xin[CH:P, u, 1].rearrange("p b m -> p (b m)")).then_inc(
                        mix_copied, 1)
                turn(0)
                for g in range(CHUNKS):
                    u = g % 2
                    dve.wait_ge(mix_stored[u], (l * (CHUNKS // 2) + g // 2) * 64 + 64)
                    for k in range(1, 8, 2):
                        if k == 3 and g + 1 < CHUNKS:
                            turn(g + 1)
                        dve.wait_ge(mix_done, (l * CHUNKS + g) * 8 + k + 1 + 16)
                        dve.tensor_copy(zout[:, u, 8 * k:8 * k + 8, :].rearrange("p m o -> p (m o)"), bank[k][:, :]).then_inc(
                            mix_read[1], 1)
                weights = pw0 if m is None else pw

                def lay_weights(u):
                    for s in range(2):
                        own = slice(64 * s, 64 * s + 64)
                        dve.tensor_copy(still[u][s][own, :, :], weights[own, own].rearrange("p (a o) -> p a o", a=1).to_broadcast(
                            [64, SIDE // 2, CH])).then_inc(weights_laid, 1)
                if m is not None:
                    dve.wait_ge(params_loaded, l * 48 + 48)
                    apart(dve)
                    lay_weights(1)
                barrier(dve, l * PHASES + 3)
                if m is None:
                    dve.wait_ge(pw0_ready, 2)
                    lay_weights(1)
                lay_weights(0)

                def inv(k, u, front, back, ahead):
                    N = l * PAIRS + k
                    B = N + (-1)
                    ub = 1 - u

                    def K(j):
                        dve.wait_ge(inv_x_done, N * 4 + j + 1 + 8)
                        dst = gtile[:, :, :, 4 * j:4 * j + 4].rearrange("p x r k -> p k r x")
                        dve.tensor_copy(dst, bank[j % 2][:, :].rearrange("p (k r x) -> p k r x", k=4, r=2)).then_inc(
                            inv_x_read, 1)

                    def T(j):
                        dve.wait_ge(inv_turned, N * 8 + j + 1)
                        o = bank[2 + j % 2][:, :].rearrange("p (t c) -> p t c", c=P)
                        dve.tensor_copy(still[u][1][0:64, 4 * j:4 * j + 4, :], o[0:64, :, CH:P])
                        dve.tensor_copy(still[u][0][64:128, 4 * j:4 * j + 4, :], o[64:128, :, 0:CH]).then_inc(inv_turned_read, 1)

                    def S(f):
                        dve.wait_ge(inv_read, B * 8 + f + 1 + 4)
                        at = (k + (-1)) * 8 + f
                        st = dve.bn_stats(stats[:, bass.ds(at, 1), :].rearrange("p a s -> p (a s)"), yout[:, ub, f * BANK:(f + 1) * BANK])
                        if f == 7:
                            st.then_inc(inv_measured, 1)
                    if front: K(0); K(1)
                    if back: S(0)
                    if front: K(2); K(3)
                    if back: S(1)
                    if front: T(0); T(1)
                    if back: S(2)
                    if front: T(2)
                    if back: S(3)
                    if front: T(3); T(4)
                    if back: S(4)
                    if front: T(5)
                    if back: S(5)
                    if front: T(6); T(7)
                    if back: S(6); S(7)
                skewed(dve, inv)
                dve.wait_ge(inv_measured, l * PAIRS + PAIRS + 2)
                dve.bn_aggr(mv[:, :], stats[:, :, :].rearrange("p a s -> p (a s)")).then_inc(norm_step, 2)
                dve.wait_ge(norm_shared, l * 2 + 1)
                dve.tensor_copy(sm[:, 0:1], bank[0][:, 0:1]).then_inc(norm_step, 1)
                dve.wait_ge(norm_step, l * 8 + 3)
                dve.tensor_tensor(sm[:, 1:2], mv[:, 0:1], sm[:, 0:1], ALU.subtract).then_inc(norm_step, 1)
                dve.wait_ge(norm_step, l * 8 + 4)
                dve.scalar_tensor_tensor(out=sm[:, 3:4], in0=sm[:, 1:2], scalar=sm[:, 1:2], in1=mv[:, 1:2], op0=ALU.mult, op1=ALU.add).then_inc(
                    norm_step, 1)
                dve.wait_ge(norm_root, l + 1)
                dve.reciprocal(sm[:, 5:6], sm[:, 4:5]).then_inc(norm_step, 1)
                dve.wait_ge(norm_step, l * 8 + 6)
                dve.tensor_tensor(bn_scale[:, :], sm[:, 5:6], vecs[:, 1:2], ALU.mult).then_inc(norm_step, 1)
                dve.wait_ge(norm_step, l * 8 + 7)
                dve.tensor_tensor(sm[:, 6:7], sm[:, 0:1], bn_scale[:, :], ALU.mult).then_inc(norm_step, 1)
                dve.wait_ge(norm_step, l * 8 + 8)
                dve.tensor_tensor(bn_bias[:, :], vecs[:, 2:3], sm[:, 6:7], ALU.subtract)
                barrier(dve, l * PHASES + 4)
            layer(0, None)
            with dve.Fori(0, LAYERS - 1) as m:
                forward(m)
                layer(m + 1, m)

            def last(n, u, i):
                dve.wait_ge(tower_free, n + 1)
                for q in range(2):
                    dve.wait_ge(tower_done, n * 2 + q + 1 + 2)
                    dve.tensor_scalar(towr[:, u, q, :], bank[4 + 2 * u + q][:, :], fc2b[:, 0:1], None, ALU.add).then_inc(
                        tower_read, 1)
            pairs(dve, last)
            dve.sem_inc(ffn_scores_read, 2)
            dve.sem_inc(ffn_out_read, 1)
            dve.sem_inc(ffn_v_read, 1)
            barrier(dve, LAYERS * PHASES + 2)
            n_chain = [0]

            def link(ins):
                n_chain[0] += 1
                ins.then_inc(chain, 1)
                dve.wait_ge(chain, n_chain[0])

            n_var = [0]

            def g3(x, g):
                return x.rearrange("p (g d) -> p g d", g=g)

            def wide(x, d):
                return x.rearrange("p (g o) -> p g o", o=1).to_broadcast([P, x.shape[1], d])

            def center_norm(x, out, g, d, eps_after=None):
                n = g if not isinstance(x, str) else BANK // d
                for b in range(g // n):
                    v = g3(x, g) if n == g else g3(filled(dve, x, b)[:, :], n)
                    ins = dve.tensor_reduce(s1[:, b * n:(b + 1) * n], v, AX.X, ALU.add)
                link(ins)
                for b in range(g // n):
                    v = g3(x, g) if n == g else g3(bank[fills[x, b][0]][:, :], n)
                    ins = dve.scalar_tensor_tensor(out=g3(xc[:, b * n * d:(b + 1) * n * d], n), in0=wide(s1[:, b * n:(b + 1) * n], d),
                                                   scalar=-1.0 / d, in1=v, op0=ALU.mult, op1=ALU.add)
                link(ins)
                if n != g:
                    for b in range(g // n):
                        dve.sem_inc(empty[fills[x, b][0]], 1)
                link(dve.tensor_tensor(sq[:, 0:g * d], xc[:, 0:g * d], xc[:, 0:g * d], ALU.mult))
                dve.tensor_reduce(s2[:, 0:g], g3(sq[:, 0:g * d], g), AX.X, ALU.add).then_inc(ev["var"], 1)
                n_var[0] += 1
                dve.wait_ge(ev["rstd"], n_var[0])
                if eps_after is not None:
                    link(dve.tensor_scalar(sd[:, 0:g], sd[:, 0:g], eps_after, None, ALU.add))
                link(dve.reciprocal(s2[:, 0:g], sd[:, 0:g]))
                return dve.tensor_tensor(g3(out, g), g3(xc[:, 0:g * d], g), wide(s2[:, 0:g], d), ALU.mult)

            def per_tile(w, n):
                return w.rearrange("p (o n) -> p o n", o=1).to_broadcast([P, J, n])

            dve.wait_ge(h1_loaded, 16)
            center_norm(h1, xn, J, CH).then_inc(ev["xn"], 1)
            link(center_norm("kv", kv, 512, 4, 1e-5))
            for t, dst in ((0, kn), (1, vn)):
                src = kv.rearrange("p (j h t d) -> p t j h d", j=J, t=2, d=4)[:, t]
                w = tw["kvw"].rearrange("p (o h t d) -> p t o h d", o=1, t=2, d=4)[:, t].to_broadcast([P, J, 16, 4])
                ins = dve.tensor_tensor(dst.rearrange("p (j h d) -> p j h d", j=J, d=4), src, w, ALU.mult)
            link(ins)
            link(dve.tensor_tensor(g3(kn, J), g3(kn, J), per_tile(tw["kvb"][:, 0:CH], CH), ALU.add))
            dve.tensor_tensor(g3(vn, J), g3(vn, J), per_tile(tw["kvb"][:, CH:2 * CH], CH), ALU.add).then_inc(ev["kn"], 1)
            for b in range(2):
                o = filled(dve, "kvm", b)
                bd = tw["bd"].rearrange("p (o n) -> p o n", o=1).to_broadcast([P, 8, CH])
                dve.tensor_tensor(g3(kvm[:, b * BANK:(b + 1) * BANK], 8), g3(o[:, :], 8), bd, ALU.mult).then_inc(ev["kvm"], 1)
            dve.wait_ge(ev["kvm"], 2)
            for b in range(2):
                dve.sem_inc(empty[fills["kvm", b][0]], 1)
            for b in range(2):
                o = filled(dve, "out", b)
                link(dve.tensor_tensor(ret[:, b * BANK:(b + 1) * BANK], o[:, :], xn[:, b * BANK:(b + 1) * BANK], ALU.add))
                dve.sem_inc(empty[fills["out", b][0]], 1)
            dve.sem_inc(ev["ret"], 1)
            link(dve.tensor_tensor(h2, h1, xn, ALU.add))
            dve.wait_ge(ev["ga"], 2)
            link(dve.tensor_tensor(h2, h2, ga, ALU.add))
            center_norm(h2, x2, J, CH).then_inc(ev["x2"], 1)

            def pair_step(k, u, proj, score, comb):
                u1 = 1 - u

                def values():
                    dve.wait_ge(ffn_v_done, k + 1)
                    for h in range(2):
                        src = bank[3][64 * h:64 * h + 64, 0:64].rearrange("p (iq o) -> p iq o", o=16)
                        dve.tensor_copy(vb[64 * h:64 * h + 64, u, :, :, h, 0:16].rearrange("p i q o -> p (i q) o"), src)
                    dve.tensor_copy(sx[:, bass.ds(k * CH, CH)].rearrange("p (n d) -> p n d", d=16),
                                    bank[3][:, P:2 * P].rearrange("p (n d) -> p n d", d=32)[:, :, 0:16]).then_inc(ffn_v_read, 1)

                def soft(i):
                    B = k + (-1)
                    dve.wait_ge(ffn_scores_done, B * 2 + i + 1)
                    v = bank[4 + i][:, :].rearrange("p (g t) -> p g t", t=64)
                    dve.tensor_reduce(mx[:, u1, i, :], v, AX.X, ALU.max).then_inc(ffn_max_done, 1)
                    dve.wait_ge(ffn_max_done, B * 2 + i + 1)
                    m = mx[:, u1, i, :].rearrange("p (g o) -> p g o", o=1).to_broadcast([P, 8, 64])
                    dve.tensor_tensor(ex[:, u1, i, :].rearrange("p (g t) -> p g t", t=64), v, m, ALU.subtract).then_inc(
                        ffn_scores_read, 1)

                def divide():
                    C = k + (-2)
                    dve.wait_ge(ffn_out_done, C + 1)
                    v = bank[7][:, 0:272].rearrange("p (g o) -> p g o", o=17)
                    dve.reciprocal(rden[:, u, :].rearrange("p (g o) -> p g o", o=1), v[:, :, 16:17]).then_inc(ffn_recip_done, 1)
                    dve.wait_ge(ffn_recip_done, C + 1)
                    for e2 in range(2):
                        for i in range(2):
                            src, dst = slice(64 * e2, 64 * e2 + 64), slice(64 * i, 64 * i + 64)
                            d = att_out[dst, bass.ds(C * 256, 256)].rearrange("p (q e n d) -> p q e n d", q=2, e=2, n=4)[:, :, e2]
                            rr = rden[src, u, 8 * i:8 * i + 8].rearrange("p (q n o) -> p q n o", q=2, o=1).to_broadcast([64, 2, 4, 16])
                            ins = dve.tensor_tensor(d, v[src, 8 * i:8 * i + 8, 0:16].rearrange("p (q n) d -> p q n d", q=2), rr, ALU.mult)
                    ins.then_inc(ffn_out_read, 1)
                if score: soft(0)
                if score: soft(1)
                if comb: divide()
                if proj: values()
            dve.wait_ge(clear, 9)
            skewed3(dve, pair_step)
            dve.wait_ge(ffn_out_read, J + 1)
            apart(dve)
            link(dve.tensor_scalar(keep, sx, 0.0, None, ALU.not_equal))
            a4 = att_out.rearrange("p (j e c) -> p e j c", j=J, e=4)
            for e in range(4):
                ins = dve.tensor_tensor(a4[:, e], a4[:, e], g3(keep, J), ALU.mult)
            link(ins)
            dve.sem_inc(ev["att"], 1)
            for n in range(4):
                src = sx[64 * (n % 2):64 * (n % 2) + 64, (n // 2) * CH + 16 * n:(n // 2) * CH + 16 * n + 16]
                for i in range(2):
                    ins = dve.tensor_copy(res[64 * i:64 * i + 64, 16 * n:16 * n + 16], src)
            link(ins)
            for b in range(0, 8, 2):
                o = filled(dve, "attT", b)
                link(dve.tensor_copy(att_T[:, b * BANK:(b + 1) * BANK], o[:, :]))
                dve.sem_inc(empty[fills["attT", b][0]], 1)
                dve.sem_inc(ev["attT"], 1)
            o = filled(dve, "gate", 0)
            link(dve.tensor_tensor(g3(lg, J), g3(o[:, 0:256], J), per_tile(tw["gateb"], 16), ALU.add))
            dve.sem_inc(empty[fills["gate", 0][0]], 1)
            link(dve.tensor_reduce(gmax, g3(lg, 64), AX.X, ALU.max))
            link(dve.tensor_tensor(g3(lg, 64), g3(lg, 64), wide(gmax, 4), ALU.subtract))
            dve.sem_inc(ev["lg"], 1)
            dve.wait_ge(ev["gexp"], 1)
            link(dve.tensor_reduce(gsum, g3(gexp, 64), AX.X, ALU.add))
            link(dve.reciprocal(gmax, gsum))
            link(dve.tensor_tensor(g3(gexp, 64), g3(gexp, 64), wide(gmax, 4), ALU.mult))
            ge = gexp.rearrange("p (jn e) -> p e jn", e=4)
            for e in range(4):
                gw = ge[:, e].rearrange("p (g o) -> p g o", o=1).to_broadcast([P, 64, 16])
                dst = mixed if e == 0 else prod[:, 0:TD]
                gwj = gw.rearrange("p (j n) d -> p j n d", j=J)
                link(dve.tensor_tensor(dst.rearrange("p (j n d) -> p j n d", j=J, d=16),
                                       a4[:, e].rearrange("p j (n d) -> p j n d", d=16), gwj, ALU.mult))
                if e:
                    link(dve.tensor_tensor(mixed, mixed, prod[:, 0:TD], ALU.add))
            link(dve.tensor_tensor(g3(mixed, J), g3(mixed, J), per_tile(res[:, :], CH), ALU.add))
            link(center_norm(mixed, fxt, 64, 16))
            link(dve.tensor_tensor(g3(fxt, J), g3(fxt, J), per_tile(tw["lng"], CH), ALU.mult))
            link(dve.tensor_tensor(g3(fxt, J), g3(fxt, J), per_tile(tw["lnb"], CH), ALU.add))
            dve.sem_inc(ev["fx"], 1)
            link(dve.tensor_scalar(keep, fxt, 0.0, None, ALU.not_equal))
            dve.wait_ge(ev["fxT"], 4)
            link(dve.tensor_scalar(keepT, xt[0:64, :], 0.0, None, ALU.not_equal))
            for b in range(4):
                o = filled(dve, "fc1", b)
                if b == 0:
                    filled(dve, "fc1", 3)
                link(dve.scalar_tensor_tensor(out=xt[0:64, b * BANK:(b + 1) * BANK], in0=o[0:64, :], scalar=0.0,
                                              in1=keepT[:, b * BANK:(b + 1) * BANK], op0=ALU.max, op1=ALU.mult))
                dve.sem_inc(empty[fills["fc1", b][0]], 1)
                dve.sem_inc(ev["hx"], 1)
            for b in range(2):
                o = filled(dve, "fc2", b)
                link(dve.tensor_tensor(hx[:, b * BANK:(b + 1) * BANK], o[:, :], keep[:, b * BANK:(b + 1) * BANK], ALU.mult))
                dve.sem_inc(empty[fills["fc2", b][0]], 1)
            link(dve.tensor_tensor(hx, hx, fxt, ALU.add))
            link(center_norm(hx, fo, 64, 16))
            link(dve.tensor_tensor(g3(fo, J), g3(fo, J), per_tile(tw["fng"], CH), ALU.mult))
            link(dve.tensor_tensor(g3(fo, J), g3(fo, J), per_tile(tw["fnb"], CH), ALU.add))
            dve.sem_inc(ev["fo"], 1)
            o = filled(dve, "fg", 0)
            v = g3(o[:, 0:64], J)
            link(dve.tensor_reduce(gmax[:, 0:J], v, AX.X, ALU.max))
            link(dve.tensor_tensor(g3(lg[:, 0:64], J), v, wide(gmax[:, 0:J], 4), ALU.subtract))
            dve.sem_inc(ev["fl"], 1)
            dve.wait_ge(ev["fexp"], 1)
            link(dve.tensor_reduce(gsum[:, 0:J], g3(gexp[:, 0:64], J), AX.X, ALU.add))
            link(dve.reciprocal(gmax[:, 0:J], gsum[:, 0:J]))
            link(dve.tensor_tensor(g3(gexp[:, 0:64], J), g3(gexp[:, 0:64], J), wide(gmax[:, 0:J], 4), ALU.mult))
            link(dve.tensor_tensor(g3(fo, 64), g3(fo, 64), wide(gexp[:, 0:64], 16), ALU.mult))
            dve.tensor_tensor(h2, h2, fo, ALU.add).then_inc(ev["done"], 1)

        @block.scalar
        def _(act):
            act.sem_inc(lift_read, 4)
            for u in range(4):
                act.sem_inc(lift_stored[u], 16)
            act.sem_inc(inv_activated, 2)
            act.sem_inc(fw_activated, 8)
            act.sem_inc(fw_back_read, 2)
            act.sem_inc(fw_x_read, 1)
            act.sem_inc(fw_modes_stored[0], 16)
            act.sem_inc(fw_modes_stored[1], 16)
            act.sem_inc(mix_read[0], 4)
            act.sem_inc(mix_stored[0], 64)
            act.sem_inc(mix_stored[1], 64)
            act.sem_inc(inv_read, 4)
            act.sem_inc(field_stored[0], 16)
            act.sem_inc(field_stored[1], 16)
            act.sem_inc(last_activated, 2)
            act.sem_inc(hidden_read, 4)
            act.wait_ge(consts_loaded, 16 * CONSTS)

            def evac_y(dst, src, g):
                d = dst.rearrange("p k (r x) -> p x r k", r=2)[:, 16 * g:16 * g + 16]
                return act.copy(d, src.rearrange("p (x r k) -> p x r k", x=16, r=2))

            def evac_x(dst, src, g):
                v = src.rearrange("p (k r c x) -> p r c k x", k=8, r=2, c=CHUNKS)
                for r in range(2):
                    d = dst[:, :, r, 64 * g:64 * g + 64].rearrange("p c (k x) -> p c k x", x=8)
                    cp = act.copy(d, v[:, r])
                return cp

            for g in range(4):
                act.wait_ge(colour_y_done, g + 1)
                evac_y(atile[0:96, 0], bank[g][0:96, :], g).then_inc(colour_y_read, 1)
            for g in range(2):
                act.wait_ge(colour_x_done, g + 1)
                evac_x(xout[0:96, 0], bank[g][0:96, :], g).then_inc(colour_x_read, 1)
            act.wait_ge(colour_x_read, 2)
            act.dma_start(colour_modes, xout[0:96, 0].rearrange("p g r m -> p (g r m)")).then_inc(colour_modes_stored, 16)
            act.wait_ge(colour_modes_stored, 16)
            barrier(act, 1)

            def lift(n, u, i):
                act.wait_ge(lift_stored[u], i * 16 + 16)
                for g in range(2):
                    act.wait_ge(lift_done, n * 2 + g + 1)
                    act.copy(lifted[:, u, g * BANK:(g + 1) * BANK], bank[2 * (u % 2) + g][:, :]).then_inc(lift_read, 1)
                act.wait_ge(lift_read, n * 2 + 2 + 4)
                dst = xmodes.rearrange("g r b c m -> (b c) (g r) m")[bass.ds(n * P, P)]
                act.dma_start(dst, lifted[:, u].rearrange("p (q m) -> p q m", m=CM)).then_inc(lift_stored[u], 16)
            with act.Fori(0, PAIRS // 4) as i:
                for u in range(4):
                    lift(i * 4 + u, u, i)
            for u in range(4):
                act.wait_ge(lift_stored[u], 16 * (PAIRS // 4 + 1))
            barrier(act, 2)

            def gelu(q, u, s=None):
                rows = slice(0, P) if s is None else slice(64 * s, 64 * s + 64)
                src = ytile[rows, u, q * 1024:(q + 1) * 1024]
                dst = (htile if s is None else moving[s])[rows, u, q * 1024:(q + 1) * 1024]
                return act.activation(dst, src, ACT.Gelu, bias=bn_bias[rows, 0:1], scale=bn_scale[rows, 0:1])

            def forward(m):
                def fwd(k, u, front, back, ahead):
                    N = m * PAIRS + k
                    B = N + (-1)
                    ub = 1 - u

                    def A(q):
                        if q == 0:
                            act.wait_ge(field_loaded[ub], (m * 2 * PAIRS + k + 1 - ub) * 8 + 16)
                            act.wait_ge(fw_turned, (N + 1) * 8 + 8)
                        gelu(q, ub).then_inc(fw_activated, 1)

                    def Y(g):
                        act.wait_ge(fw_back, N * 4 + g + 1 + 4)
                        evac_y(atile[:, u], bank[4 + g % 2][:, :], g).then_inc(fw_back_read, 1)

                    def X(g):
                        if g == 0:
                            act.wait_ge(fw_modes_stored[ub], (B - ub) * 8 + 16)
                        act.wait_ge(fw_x_done, B * 2 + g + 1)
                        evac_x(xout[:, ub], bank[7][:, :], g).then_inc(fw_x_read, 1)

                    if ahead: A(0)
                    if front: Y(0)
                    if ahead: A(1)
                    if front: Y(1)
                    if back: X(0)
                    if ahead: A(2)
                    if front: Y(2)
                    if ahead: A(3)
                    if front: Y(3)
                    if back: X(1)
                    if back:
                        act.wait_ge(fw_x_read, B * 2 + 3)
                        dst = xmodes.rearrange("g r b c m -> (b c) (g r) m")[bass.ds((k + (-1)) * P, P)]
                        act.dma_start(dst, xout[:, ub].rearrange("p g r m -> p (g r) m")).then_inc(fw_modes_stored[ub], 16)
                act.wait_ge(field_loaded[0], m * 2 * PAIRS * 8 + 16)
                for q in range(4):
                    gelu(q, 0).then_inc(fw_activated, 1)
                skewed(act, fwd)
                for u in range(2):
                    act.wait_ge(fw_modes_stored[u], (m + 1) * 8 * PAIRS + 16)
                barrier(act, m * PHASES + 5)

            def layer(l, m):
                def turn(g):
                    u = g % 2
                    act.wait_ge(mix_modes_loaded[u], (l * (CHUNKS // 2) + g // 2) * 32 + 32)
                    act.mul(xin[CH:P, u, 0], xin[0:CH, u, 1], -1.0).then_inc(mix_negated, 1)
                turn(0)
                for g in range(CHUNKS):
                    u = g % 2
                    G = l * CHUNKS + g
                    act.wait_ge(mix_stored[u], (l * (CHUNKS // 2) + g // 2) * 64 + 64)
                    for k in range(0, 8, 2):
                        if k == 4 and g + 1 < CHUNKS:
                            turn(g + 1)
                        act.wait_ge(mix_done, G * 8 + k + 1 + 16)
                        act.copy(zout[:, u, 8 * k:8 * k + 8, :].rearrange("p m o -> p (m o)"), bank[k][:, :]).then_inc(
                            mix_read[0], 1)
                    act.wait_ge(mix_read[0], G * 4 + 4 + 4)
                    act.wait_ge(mix_read[1], G * 4 + 4 + 4)
                    for parity in range(2):
                        for v in range(2):
                            p0 = 64 * parity + 32 * v
                            dst = zmodes[v, :, 8 * g:8 * g + 8, parity].rearrange("b k y o -> b k (y o)")
                            act.dma_start(dst, zout[p0:p0 + 32, u].rearrange("b (k y) o -> b k (y o)", k=8)).then_inc(
                                mix_stored[u], 16)
                for u in range(2):
                    act.wait_ge(mix_stored[u], (l + 1) * 128 + 64)
                barrier(act, l * PHASES + 3)
                act.wait_ge(params_loaded, l * 48 + 48)
                apart(act)
                if m is None:
                    act.wait_ge(pw0_folded, 1)
                    for s in range(2):
                        act.copy(pw0[64 * s:64 * s + 7, :], bank[0][64 * s:64 * s + 7, 0:P]).then_inc(pw0_ready, 1)

                def inv(k, u, front, back, ahead):
                    N = l * PAIRS + k
                    B = N + (-1)
                    ub = 1 - u

                    def A(i):
                        if i == 0:
                            act.wait_ge(field_loaded[u], (m * 2 * PAIRS + PAIRS + k - u) * 8 + 16)
                            act.wait_ge(inv_done, N * 8 + 8)
                        h = gelu(i // 2, u, i % 2)
                        if i == 7:
                            h.then_inc(inv_activated, 1)

                    def F(f):
                        if f == 0:
                            act.wait_ge(field_stored[ub], (B - ub) * 8 + 16)
                            act.wait_ge(inv_measured, B + 1)
                        act.wait_ge(inv_done, B * 8 + f + 1 + 16)
                        act.activation(yout[:, ub, f * BANK:(f + 1) * BANK], bank[4 + f % 4][:, :], ACT.Identity, bias=vecs[:, 0:1]).then_inc(
                            inv_read, 1)
                    front = front and m is not None
                    if back: F(0)
                    if front: A(0); A(1)
                    if back: F(1)
                    if front: A(2); A(3)
                    if back: F(2)
                    if front: A(4)
                    if back: F(3)
                    if front: A(5)
                    if back: F(4)
                    if front: A(6)
                    if back: F(5)
                    if front: A(7)
                    if back:
                        F(6); F(7)
                        act.wait_ge(inv_read, B * 8 + 8 + 4)
                        act.dma_start(field[bass.ds(k + (-1), 1)].rearrange("a p m -> p (a m)"), yout[:, ub, :]).then_inc(
                            field_stored[ub], 16)
                skewed(act, inv)
                act.activation(unused[:, 0:1], epst[:, 0:1], ACT.Sqrt)
                act.wait_ge(norm_shared, l * 2 + 2)
                act.activation(sm[:, 4:5], bank[0][:, 1:2], ACT.Sqrt, bias=epst[:, 0:1]).then_inc(norm_root, 1)
                act.activation(unused[:, 1:2], epst[:, 0:1], ACT.Gelu)
                barrier(act, l * PHASES + 4)
            layer(0, None)
            with act.Fori(0, LAYERS - 1) as m:
                forward(m)
                layer(m + 1, m)

            def last(k, u, front, back, ahead):
                def A(q):
                    if q == 0:
                        act.wait_ge(field_loaded[1 - u], ((LAYERS - 1) * 2 * PAIRS + k + 1 - (1 - u)) * 8 + 16)
                    h = gelu(q, 1 - u)
                    if q == 3:
                        h.then_inc(last_activated, 1)
                if not front:
                    return
                for r in range(16):
                    if r % 8 == 0:
                        act.wait_ge(tower_done, k * 2 + r // 8 + 1)
                    act.wait_ge(hidden_done, k * 16 + r + 1)
                    act.activation(hidden[:, r, :], bank[r % 4][:, :], ACT.Gelu, bias=fc1b[:, r % 2:r % 2 + 1]).then_inc(
                        hidden_read, 1)
                    if ahead and r % 4 == 1:
                        A(r // 4)
            act.wait_ge(field_loaded[0], (LAYERS - 1) * 2 * PAIRS * 8 + 16)
            for q in range(4):
                h = gelu(q, 0)
            h.then_inc(last_activated, 1)
            skewed(act, last)
            act.sem_inc(ffn_in_read, 1)
            act.sem_inc(ffn_q_read, 1)
            act.sem_inc(ffn_k_read, 1)
            act.sem_inc(ffn_turned_read, 1)
            barrier(act, LAYERS * PHASES + 2)

            def move(name, b, dst, event, parts=P):
                o = filled(act, name, b)
                act.copy(dst, o[0:parts, :]).then_inc(ev[event], 1)

            def emptied(name, n, event):
                act.wait_ge(ev[event], n)
                for b in range(n):
                    act.sem_inc(empty[fills[name, b][0]], 1)

            def root(n, g, scale, eps):
                act.wait_ge(ev["var"], n)
                bias = {} if eps is None else {"bias": eps[:, 0:1]}
                act.activation(sd[:, 0:g], s2[:, 0:g], ACT.Sqrt, scale=scale, **bias).then_inc(ev["rstd"], 1)

            act.wait_ge(clear, 9)
            root(1, J, 1.0 / CH, eps5)
            for b in range(4):
                move("xT", b, xt[0:64, b * BANK:(b + 1) * BANK], "xT", 64)
            emptied("xT", 4, "xT")
            for b in range(4):
                move("q", b, qt[:, b * BANK:(b + 1) * BANK], "qT")
            emptied("q", 4, "qT")
            act.copy(maskb[:, :], tw["mask"][:, :]).then_inc(masks, 1)
            act.copy(identb[:, :], ident[:, :]).then_inc(masks, 1)
            root(2, 512, 1.0 / 3.0, None)
            filled(act, "kv", 3)
            for b in range(4):
                move("retT", b, xt[0:64, b * BANK:(b + 1) * BANK], "retT", 64)
            emptied("retT", 4, "retT")
            for b in range(2):
                o = filled(act, "proj", b)
                act.activation(ga[:, b * BANK:(b + 1) * BANK], o[:, :], ACT.Gelu).then_inc(ev["ga"], 1)
            emptied("proj", 2, "ga")
            root(3, J, 1.0 / CH, eps5)
            for b in range(4):
                move("x2T", b, xt[0:64, b * BANK:(b + 1) * BANK], "x2T", 64)
            emptied("x2T", 4, "x2T")

            def pair_step(k, u, proj, score, comb):
                u1 = 1 - u

                def inputs():
                    act.wait_ge(ffn_in_done, k + 1)
                    act.copy(sxT[:, u, :], bank[0][:, 0:P]).then_inc(ffn_in_read, 1)

                def queries():
                    act.wait_ge(ffn_q_done, k + 1)
                    dst = qb[:, u].rearrange("p (i e s) -> p e i s", i=2, e=4)
                    act.copy(dst, bank[1][:, :].rearrange("p (e i s) -> p e i s", e=4, i=2)).then_inc(ffn_q_read, 1)

                def keys():
                    act.wait_ge(ffn_k_done, k + 1)
                    for n in range(4):
                        rows = slice(32 * n, 32 * n + 32)
                        dst = kb[rows, u].rearrange("p (i n t) -> p n i t", i=2, n=4)[:, n]
                        cp = act.copy(dst, bank[2][rows, 0:P].rearrange("p (i t) -> p i t", i=2))
                    cp.then_inc(ffn_k_read, 1)

                def turned(i):
                    C = k + (-2)
                    act.wait_ge(ffn_turned, C * 2 + i + 1)
                    act.copy(exT[:, i, :], bank[6][:, :]).then_inc(ffn_turned_read, 1)

                def exps(i):
                    B = k + (-1)
                    act.wait_ge(ffn_scores_read, B * 2 + i + 1 + 2)
                    act.activation(ex[:, u1, i, :], ex[:, u1, i, :], ACT.Exp, scale=4.0).then_inc(ffn_exp_done, 1)
                if proj: inputs()
                if comb: turned(0)
                if score: exps(0)
                if proj: queries(); keys()
                if comb: turned(1)
                if score: exps(1)
            skewed3(act, pair_step)
            for b in range(1, 8, 2):
                o = filled(act, "attT", b)
                act.copy(att_T[:, b * BANK:(b + 1) * BANK], o[:, :]).then_inc(ev["attT"], 1)
            act.wait_ge(ev["attT"], 8)
            for b in range(1, 8, 2):
                act.sem_inc(empty[fills["attT", b][0]], 1)
            act.wait_ge(ev["lg"], 1)
            act.activation(gexp, lg, ACT.Exp).then_inc(ev["gexp"], 1)
            root(4, 64, 1.0 / 16, eps8)
            for b in range(4):
                move("fT", b, xt[0:64, b * BANK:(b + 1) * BANK], "fxT", 64)
            emptied("fT", 4, "fxT")
            root(5, 64, 1.0 / 16, eps8)
            for b in range(4):
                move("foT", b, xt[0:64, b * BANK:(b + 1) * BANK], "foT", 64)
            emptied("foT", 4, "foT")
            act.wait_ge(ev["fl"], 1)
            act.activation(gexp[:, 0:64], lg[:, 0:64], ACT.Exp).then_inc(ev["fexp"], 1)


def constants():
    import numpy as np
    f = np.float64
    y = np.arange(SIDE)
    ky = np.arange(NKY)
    kx = np.concatenate([np.arange(16), np.arange(SIDE - 16, SIDE)])
    ay = 2 * np.pi * np.outer(y, ky) / SIDE
    ax = 2 * np.pi * np.outer(y, kx) / SIDE
    one = np.stack([np.cos(ay), -np.sin(ay)], 1).reshape(SIDE, 2 * NKY)
    fy = np.kron(np.eye(2), one)
    c, s = np.cos(ax), np.sin(ax)
    fx = np.block([[c, -s], [s, c]])
    ix = np.block([[c.T, s.T], [-s.T, c.T]]) / SIDE
    wk = np.where(ky == 0, 1.0, 2.0)[:, None]
    inv = np.concatenate([wk * np.cos(ay.T), -wk * np.sin(ay.T)], 0) / SIDE
    iy = np.tile(np.kron(np.eye(2), inv), (2, 1))
    avg = np.kron(np.full((2, 2), 0.5), np.eye(CH))
    return {"c_ident": np.eye(P), "c_fy": fy, "c_fx": fx, "c_ix": ix, "c_iy": iy, "c_avg": avg}


def layout(d):
    import numpy as np
    g = lambda k: np.asarray(d[k])
    out = {k: v.astype(np.float32) for k, v in constants().items()}
    x = g("x")
    pair = x.reshape(PAIRS, 2, PIX, 3).transpose(0, 1, 3, 2).reshape(PAIRS, 6, PIX)
    out["x"] = np.concatenate([pair, np.ones((PAIRS, 1, PIX), np.float32)], 1)
    out["xs"] = x.reshape(BATCH, 32, 2, SIDE, 3).transpose(2, 3, 1, 0, 4).reshape(P, 32, 96)
    dc = np.zeros((1, PAIRS, 1024), np.float32)
    dc[:, :, 0] = PIX
    out["dc"] = dc
    two = lambda a: np.concatenate([a, a], 0)
    w0, b0 = g("L0_tok_fc0_w"), g("L0_tok_fc0_b")
    fc0 = np.zeros((7, 2, CH), np.float32)
    fc0[0:3, 0], fc0[3:6, 1], fc0[6] = w0, w0, b0
    out["fc0"] = fc0.reshape(7, P)
    out["fc0t"] = fc0.reshape(7, P).T
    w = np.stack([np.stack([g("L0_tok_w1r"), g("L0_tok_w1i")], 1), np.stack([g("L0_tok_w2r"), g("L0_tok_w2i")], 1)], 1)
    w = w.reshape(LAYERS, 2, 2, CH, CH, 2, CM).transpose(0, 1, 5, 2, 3, 6, 4)
    out["w"] = np.ascontiguousarray(w).reshape(LAYERS * CHUNKS, P, CM, CH)
    out["pw"] = np.ascontiguousarray(g("L0_tok_pw_w").transpose(0, 2, 1))
    v = np.stack([g("L0_tok_pw_b"), g("L0_tok_gamma"), g("L0_tok_beta")], -1)
    out["vecs"] = np.concatenate([v, v], 1)
    w1 = g("L0_tok_fc1_w").reshape(CH, 2, 64)
    w2 = g("L0_tok_fc2_w").reshape(2, 64)
    fc1 = np.zeros((2, CH, 2, 2, 64), np.float32)
    fc2 = np.zeros((2, 64, 2, 32), np.float32)
    for s in range(2):
        fc1[s, :, :, s] = w1
        fc2[s, :, :, s] = w2.T
    out["fc1"], out["fc2"] = fc1.reshape(P, 2, P), fc2.reshape(P, 2, 32)
    out["fc1b"] = two(g("L0_tok_fc1_b").reshape(2, 64).T)
    out["fc2b"] = np.broadcast_to(g("L0_tok_fc2_b")[:, None], (P, 1))
    a = lambda k: g("L0_attn_" + k)
    wq = a("W_qkv").reshape(16, 3, 4, CH)
    bq = a("b_qkv").reshape(16, 3, 4)
    t = {}
    t["wkv"] = np.concatenate([wq[:, 1:].reshape(P, CH).T, bq[:, 1:].reshape(1, P)], 0)
    q = np.concatenate([wq[:, 0].reshape(CH, CH).T, bq[:, 0].reshape(1, CH)], 0)
    t["wq2"] = np.concatenate([q, q], 1)
    t["wproj"] = np.concatenate([a("W_proj").T, a("b_proj")[None]], 0)
    rep = lambda v: np.broadcast_to(v.reshape(1, -1), (P, v.size))
    t["kvw"] = rep(np.stack([a("kln_w")[:, 0], a("vln_w")[:, 0]], 1))
    t["kvb"] = rep(np.stack([a("kln_b")[:, 0], a("vln_b")[:, 0]], 0))
    hd = np.arange(CH) // 4
    t["bd"] = np.tile((hd[:, None] == hd[None, :]) / CH, (2, 1)).astype(np.float32)
    f = lambda k: g("L0_ffn_" + k)
    z = lambda *s: np.zeros(s, np.float32)
    hl = z(65, 4, 32)
    hl[0:64, :, 0:16] = f("hl_w").transpose(2, 0, 1)
    hl[64, :, 0:16] = f("hl_b")
    t["hlp"] = hl.reshape(65, P)
    w = z(4, 32, 4, 4, 32)
    k_ = z(4, 32, 4, 32)
    v_ = z(4, 32, 2, 2, 16)
    gw = z(2, 2, 4, 16, 4, 4)
    d1, d2 = z(65, 4, 16), z(65, 4, 16)
    for n in range(4):
        w[n, 0:16, :, n, 0:16] = f("wq")[n].transpose(2, 0, 1)
        k_[n, 0:16, n, 0:16] = f("wk")[n].T
        v_[n, 0:16, n % 2, n // 2] = f("wv")[n].T
        gw[:, :, n, :, n, :] = f("gate_w")[n].reshape(4, 2, 2, 16).transpose(1, 2, 3, 0)
        d1[16 * n:16 * n + 16, n] = f("fc1_w").T
        d2[16 * n:16 * n + 16, n] = f("fc2_w").T
        d1[64, n], d2[64, n] = f("fc1_b"), f("fc2_b")
    t["wqp"] = w.reshape(P, 4, P)
    t["wkp"] = k_.reshape(P, P)
    t["wvp"] = v_.reshape(P, 2, 32)
    t["gwb"] = gw.reshape(2, P, 16).transpose(1, 0, 2)
    t["gateb"] = rep(f("gate_b"))
    for n, k in (("lng", "ln_g"), ("lnb", "ln_b"), ("fng", "fnorm_g"), ("fnb", "fnorm_b")):
        t[n] = rep(np.tile(f(k), 4))
    t["fc1d"], t["fc2d"] = d1.reshape(65, CH), d2.reshape(65, CH)
    t["fgt"] = f("fgate_w").T
    s = np.arange(SIDE)
    causal = np.where(s[None, :] <= s[:, None], 0.0, -1e30).astype(np.float32)
    t["mask"] = np.tile(causal, (2, 8))
    for k, v in t.items():
        assert list(v.shape) == TAIL_W[k], (k, v.shape)
        out["t_" + k] = v
    return {k: np.ascontiguousarray(a) for k, a in out.items()}


def kernel(**inputs):
    import concourse.bacc as bacc
    import numpy as np
    from concourse.bass_utils import run_bass_kernel_spmd

    arrays = layout(inputs)
    nc = bacc.Bacc("TRN2", target_bir_lowering=False, num_devices=1)
    io = {n: nc.dram_tensor("in_" + n, a.shape, F32, kind="ExternalInput").ap() for n, a in arrays.items()}
    io["out"] = nc.dram_tensor("out", [BATCH * SIDE * SIDE], F32, kind="ExternalOutput").ap()
    tower_kernel(nc, io)
    r = run_bass_kernel_spmd(nc, [{"in_" + n: a for n, a in arrays.items()}], core_ids=[0])
    return np.asarray(r.results[0]["out"]).reshape(BATCH, SIDE, SIDE)
```
